# Optimizing a Trainium2 kernel written in Bass

```python
import numpy as np
import jax
import jax.numpy as jnp

def _softmax(x, axis=-1):
    return jax.nn.softmax(x, axis=axis)

def _gelu(x):
    return jax.nn.gelu(x, approximate=True)

def _silu(x):
    return jax.nn.silu(x)

def _sigmoid(x):
    return jax.nn.sigmoid(x)

def _layernorm(x, axis=-1, eps=1e-05):
    m = jnp.mean(x, axis=axis, keepdims=True)
    v = jnp.var(x, axis=axis, keepdims=True)
    return (x - m) / jnp.sqrt(v + eps)

def _scatter_add(tgt, idx, src, axis=0):
    return tgt.at[idx].add(src)

def _segment_sum(src, seg, n):
    return jax.ops.segment_sum(src, seg, n)
kernel_name = 'mk_vit_tower_d1_tok_img1024_r4_2910c6'

def setup_inputs(seed: int=0):
    np.random.seed(seed)
    _w = jnp.asarray

    def _rec_inputs():
        import jax
        import jax.numpy as jnp
        _rk = jax.random.key(seed)
        x = -0.000125008 + 0.999885 * jax.random.normal(jax.random.fold_in(_rk, 1), (32, 512, 256, 4), jnp.float32)
        return x
    x = _rec_inputs()

    def _L0_tok_setup():
        import jax, jax.numpy as jnp
        import numpy as np
        key = jax.random.key(seed)
        k1, k2, k3 = jax.random.split(key, 3)
        B, H, I, O, Dp1 = (4, 512, 256, 256, 4)
        x = jax.random.normal(k1, (B, H, I, Dp1), dtype=jnp.float32)
        weight = 0.1 * jax.random.normal(k2, (O, Dp1), dtype=jnp.float32)
        weighted_sum = 0.1 * jax.random.normal(k3, (O, I), dtype=jnp.float32)
        return {'x': x, 'weight': weight, 'weighted_sum': weighted_sum}
    _L0_tok_all = _L0_tok_setup()
    _L0_tok_in = {k: v for k, v in _L0_tok_all.items() if k in ('weight', 'weighted_sum')}
    del _L0_tok_all

    def _L0_attn_setup():
        import jax, jax.numpy as jnp
        import numpy as np
        H = 256
        NH = 16
        HD = H // NH
        BUCKETS = 64
        MAXREL = 128
        SPAN = BUCKETS
        B, S = (2, 512)

        def _log_bucket(rel, bucket_size, max_position):
            sign = jnp.sign(rel).astype(jnp.float32)
            mid = bucket_size // 2
            abs_pos = jnp.where((rel < mid) & (rel > -mid), mid - 1, jnp.abs(rel)).astype(jnp.float32)
            log_pos = jnp.ceil(jnp.log(abs_pos / mid) / np.float32(np.log((max_position - 1) / mid)) * (mid - 1)) + mid
            bucket = jnp.where(abs_pos <= mid, rel.astype(jnp.float32), log_pos * sign)
            return bucket.astype(jnp.int32)

        def _split_heads(x, b, s):
            return x.reshape(b, s, NH, HD).transpose(0, 2, 1, 3)
        key = jax.random.key(seed)
        ks = jax.random.split(key, 10)
        s = 0.02
        return {'hidden_states': jax.random.normal(ks[0], (B, S, H), jnp.float32), 'Wq': jax.random.normal(ks[1], (H, H), jnp.float32) * s, 'bq': jnp.zeros((H,), jnp.float32), 'Wk': jax.random.normal(ks[2], (H, H), jnp.float32) * s, 'bk': jnp.zeros((H,), jnp.float32), 'Wv': jax.random.normal(ks[3], (H, H), jnp.float32) * s, 'bv': jnp.zeros((H,), jnp.float32), 'Wo': jax.random.normal(ks[4], (H, H), jnp.float32) * s, 'bo': jnp.zeros((H,), jnp.float32), 'Wpk': jax.random.normal(ks[5], (H, H), jnp.float32) * s, 'bpk': jnp.zeros((H,), jnp.float32), 'Wpq': jax.random.normal(ks[6], (H, H), jnp.float32) * s, 'bpq': jnp.zeros((H,), jnp.float32), 'rel_emb': jax.random.normal(ks[7], (2 * SPAN, H), jnp.float32) * s, 'ln_g': jnp.ones((H,), jnp.float32), 'ln_b': jnp.zeros((H,), jnp.float32)}
    _L0_attn_all = _L0_attn_setup()
    _L0_attn_in = {k: v for k, v in _L0_attn_all.items() if k in ('Wq', 'bq', 'Wk', 'bk', 'Wv', 'bv', 'Wo', 'bo', 'Wpk', 'bpk', 'Wpq', 'bpq', 'rel_emb', 'ln_g', 'ln_b')}
    del _L0_attn_all

    def _L0_ffn_setup():
        import jax, jax.numpy as jnp
        import numpy as np
        B, S, HID, DFF, E, K = (4, 512, 256, 1024, 8, 512)
        key = jax.random.key(seed)
        ks = jax.random.split(key, 4)
        sc_h = 1.0 / np.sqrt(HID)
        sc_f = 1.0 / np.sqrt(DFF)
        return {'x': jax.random.normal(ks[0], (B, S, HID), jnp.float32), 'router_w': jax.random.normal(ks[1], (HID, E), jnp.float32) * sc_h, 'router_b': jnp.zeros((E,), jnp.float32), 'w1': jax.random.normal(ks[2], (E, HID, DFF), jnp.float32) * sc_h, 'b1': jnp.zeros((E, DFF), jnp.float32), 'w2': jax.random.normal(ks[3], (E, DFF, HID), jnp.float32) * sc_f, 'b2': jnp.zeros((E, HID), jnp.float32)}
    _L0_ffn_all = _L0_ffn_setup()
    _L0_ffn_in = {k: v for k, v in _L0_ffn_all.items() if k in ('router_w', 'router_b', 'w1', 'b1', 'w2', 'b2')}
    del _L0_ffn_all
    return {'x': x, 'L0_tok_weight': _L0_tok_in['weight'], 'L0_tok_weighted_sum': _L0_tok_in['weighted_sum'], 'L0_attn_Wq': _L0_attn_in['Wq'], 'L0_attn_bq': _L0_attn_in['bq'], 'L0_attn_Wk': _L0_attn_in['Wk'], 'L0_attn_bk': _L0_attn_in['bk'], 'L0_attn_Wv': _L0_attn_in['Wv'], 'L0_attn_bv': _L0_attn_in['bv'], 'L0_attn_Wo': _L0_attn_in['Wo'], 'L0_attn_bo': _L0_attn_in['bo'], 'L0_attn_Wpk': _L0_attn_in['Wpk'], 'L0_attn_bpk': _L0_attn_in['bpk'], 'L0_attn_Wpq': _L0_attn_in['Wpq'], 'L0_attn_bpq': _L0_attn_in['bpq'], 'L0_attn_rel_emb': _L0_attn_in['rel_emb'], 'L0_attn_ln_g': _L0_attn_in['ln_g'], 'L0_attn_ln_b': _L0_attn_in['ln_b'], 'L0_ffn_router_w': _L0_ffn_in['router_w'], 'L0_ffn_router_b': _L0_ffn_in['router_b'], 'L0_ffn_w1': _L0_ffn_in['w1'], 'L0_ffn_b1': _L0_ffn_in['b1'], 'L0_ffn_w2': _L0_ffn_in['w2'], 'L0_ffn_b2': _L0_ffn_in['b2']}

def reference(x, L0_tok_weight, L0_tok_weighted_sum, L0_attn_Wq, L0_attn_bq, L0_attn_Wk, L0_attn_bk, L0_attn_Wv, L0_attn_bv, L0_attn_Wo, L0_attn_bo, L0_attn_Wpk, L0_attn_bpk, L0_attn_Wpq, L0_attn_bpq, L0_attn_rel_emb, L0_attn_ln_g, L0_attn_ln_b, L0_ffn_router_w, L0_ffn_router_b, L0_ffn_w1, L0_ffn_b1, L0_ffn_w2, L0_ffn_b2):
    import jax
    import jax.numpy as jnp

    def _L0_tok_ref(x, weight, weighted_sum):
        import jax, jax.numpy as jnp
        import numpy as np
        return jnp.einsum('bhid,oi,od->bho', x, weighted_sum, weight)

    def _L0_attn_ref(hidden_states, Wq, bq, Wk, bk, Wv, bv, Wo, bo, Wpk, bpk, Wpq, bpq, rel_emb, ln_g, ln_b):
        import jax, jax.numpy as jnp
        import numpy as np
        H = 256
        NH = 16
        HD = H // NH
        BUCKETS = 64
        MAXREL = 128
        SPAN = BUCKETS
        B, S = (2, 512)

        def _log_bucket(rel, bucket_size, max_position):
            sign = jnp.sign(rel).astype(jnp.float32)
            mid = bucket_size // 2
            abs_pos = jnp.where((rel < mid) & (rel > -mid), mid - 1, jnp.abs(rel)).astype(jnp.float32)
            log_pos = jnp.ceil(jnp.log(abs_pos / mid) / np.float32(np.log((max_position - 1) / mid)) * (mid - 1)) + mid
            bucket = jnp.where(abs_pos <= mid, rel.astype(jnp.float32), log_pos * sign)
            return bucket.astype(jnp.int32)

        def _split_heads(x, b, s):
            return x.reshape(b, s, NH, HD).transpose(0, 2, 1, 3)
        b, s, _ = hidden_states.shape
        q = _split_heads(hidden_states @ Wq + bq, b, s)
        k = _split_heads(hidden_states @ Wk + bk, b, s)
        v = _split_heads(hidden_states @ Wv + bv, b, s)
        scale = jnp.sqrt(jnp.asarray(HD * 3, jnp.float32))
        scores = jnp.einsum('bhqd,bhkd->bhqk', q, k) / scale
        ids = jnp.arange(s)
        rel = _log_bucket(ids[:, None] - ids[None, :], BUCKETS, MAXREL)
        mu = rel_emb.mean(-1, keepdims=True)
        var = rel_emb.var(-1, keepdims=True)
        re = (rel_emb - mu) / jnp.sqrt(var + 1e-05) * ln_g + ln_b
        pos_k = (re @ Wpk + bpk).reshape(2 * SPAN, NH, HD).transpose(1, 0, 2)
        pos_q = (re @ Wpq + bpq).reshape(2 * SPAN, NH, HD).transpose(1, 0, 2)
        c2p = jnp.einsum('bhqd,hpd->bhqp', q, pos_k)
        c2p_idx = jnp.clip(rel + SPAN, 0, 2 * SPAN - 1)
        c2p = jnp.take_along_axis(c2p, jnp.broadcast_to(c2p_idx[None, None], (b, NH, s, s)), axis=-1) / scale
        p2c = jnp.einsum('bhkd,hpd->bhkp', k, pos_q)
        p2c_idx = jnp.clip(-rel + SPAN, 0, 2 * SPAN - 1)
        p2c = jnp.take_along_axis(p2c, jnp.broadcast_to(p2c_idx[None, None], (b, NH, s, s)), axis=-1)
        p2c = jnp.swapaxes(p2c, -1, -2) / scale
        scores = scores + c2p + p2c
        probs = jax.nn.softmax(scores.astype(jnp.float32), axis=-1).astype(q.dtype)
        ctx = jnp.einsum('bhqk,bhkd->bhqd', probs, v)
        ctx = ctx.transpose(0, 2, 1, 3).reshape(b, s, H)
        return ctx @ Wo + bo

    def _L0_ffn_ref(x, router_w, router_b, w1, b1, w2, b2):
        import jax, jax.numpy as jnp
        import numpy as np
        B, S, HID, DFF, E, K = (4, 512, 256, 1024, 8, 512)
        b, s, h = x.shape
        xf = x.reshape(-1, h)
        logits = xf @ router_w + router_b
        scores = jax.nn.softmax(logits, axis=-1)
        G, idx = jax.lax.top_k(scores.T, K)
        toks = xf[idx]
        h1 = jax.nn.relu(jnp.einsum('ekh,ehf->ekf', toks, w1) + b1[:, None, :])
        eo = jnp.einsum('ekf,efh->ekh', h1, w2) + b2[:, None, :]
        contrib = (eo * G[..., None]).reshape(-1, h)
        y = jnp.zeros_like(xf).at[idx.reshape(-1)].add(contrib)
        return y.reshape(b, s, h)
    h = _L0_tok_ref(x, L0_tok_weight, L0_tok_weighted_sum)
    h = h + _L0_attn_ref(_layernorm(h, axis=-1), L0_attn_Wq, L0_attn_bq, L0_attn_Wk, L0_attn_bk, L0_attn_Wv, L0_attn_bv, L0_attn_Wo, L0_attn_bo, L0_attn_Wpk, L0_attn_bpk, L0_attn_Wpq, L0_attn_bpq, L0_attn_rel_emb, L0_attn_ln_g, L0_attn_ln_b)
    h = h + _L0_ffn_ref(_layernorm(h, axis=-1), L0_ffn_router_w, L0_ffn_router_b, L0_ffn_w1, L0_ffn_b1, L0_ffn_w2, L0_ffn_b2)
    return h

_drawn_inputs = setup_inputs


def setup_inputs(seed=0):
    import zlib

    import numpy as np

    out = dict(_drawn_inputs(seed))
    spreads = {'L0_attn_bq': (0.0, 0.8),
     'L0_attn_bk': (0.0, 0.8),
     'L0_attn_bv': (0.0, 0.1),
     'L0_attn_bo': (0.0, 0.1),
     'L0_attn_bpk': (0.0, 0.8),
     'L0_attn_bpq': (0.0, 0.8),
     'L0_attn_ln_g': (1.0, 0.6),
     'L0_attn_ln_b': (0.0, 0.8),
     'L0_ffn_router_b': (0.0, 0.1),
     'L0_ffn_b1': (0.0, 0.1),
     'L0_ffn_b2': (0.0, 0.1)}
    factors = {'L0_attn_Wq': 3.277,
     'L0_attn_Wk': 3.251,
     'L0_attn_Wpk': 5.54,
     'L0_attn_Wpq': 3.786,
     'L0_attn_rel_emb': 3.66}
    for name, (base, spread) in spreads.items():
        noise = np.random.default_rng([zlib.crc32(name.encode()), seed]).standard_normal(out[name].shape)
        drawn = base * np.exp(spread * noise) if base else spread * noise
        out[name] = jnp.asarray(drawn.astype(out[name].dtype))
    for name, factor in factors.items():
        out[name] = (out[name] * factor).astype(out[name].dtype)
    return out
```

```python
from contextlib import ExitStack

import numpy as np
import concourse.bass as bass
from concourse import mybir

F32 = mybir.dt.float32
BF16 = mybir.dt.bfloat16
I32 = mybir.dt.int32
U32 = mybir.dt.uint32
ALU = mybir.AluOpType
ACT = mybir.ActivationFunctionType
AX = mybir.AxisListType

P = 128
S = 512
H = 256
ND = 4
NH = 16
HD = H // NH
QT = S // P
HC = H // P
SPAN = 64
NP = 2 * SPAN
DFF = 1024
NE = 8
TOPK = 512
FC = DFF // P
CT = TOPK // P
EPS = 1e-5
SCALE = float(1.0 / np.sqrt(np.float32(HD * 3)))

TLOW = 128
TW = 3 * P
PITCH = 4 * P
NEAR = 3 * P
BW = 6 * P
SLOTS = 6
SIDE_A = (0, 0, 1, 0, 2, 1)
SIDE_B = (0, 1, 0, 2, 0, 1)
ST = SLOTS * HD
KW = 2 * S + S // 2
SW = S + KW
RING = 4
LEAD = 3
GH = 4
NG = NH // GH
CROW = 32
XG = H + NE
BITS = 30


def after(eng, sem, count):
    if not isinstance(count, int) or count > 0:
        eng.wait_ge(sem, count)


def settled(eng, sem, count, passed):
    after(eng, sem, count)
    if not isinstance(count, int):
        eng.sem_inc(passed, 1)


def peeled(eng, steps, body):
    body(0, steps == 1)
    if steps > 2:
        with eng.Fori(1, steps - 1, 1) as i:
            body(i, False)
    if steps > 1:
        body(steps - 1, True)


def build(nc, io, B):
    T = B * S
    NT = T // P
    with ExitStack() as top:
        def sem(name):
            return top.enter_context(nc.semaphore(name))

        def dram(name, shape, dt=F32):
            return nc.dram_tensor(name, shape, dt).ap()

        passed = sem("passed")
        d_tab = dram("d_tab", (2, 3, H, TW), BF16)
        d_stack = dram("d_stack", (B, SLOTS, H, SW), BF16)
        d_kterm = dram("d_kterm", (B, 3, NH, S + S // 2), BF16)
        d_v = dram("d_v", (B, S, NH * CROW))
        d_h = dram("d_h", (B, S, H))
        d_skew = dram("d_skew", (RING, 2, QT, P, PITCH))
        d_ctx = dram("d_ctx", (B, NG, P, S))
        d_xg = dram("d_xg", (T, XG))

        with ExitStack() as ctx:
            project(nc, io, B, ctx, sem, passed, d_tab, d_stack, d_kterm, d_v, d_h)
        with ExitStack() as ctx:
            attend(nc, io, B, ctx, sem, passed, d_tab, d_stack, d_kterm, d_v, d_skew, d_ctx)
        with ExitStack() as ctx:
            scores = ctx.enter_context(nc.sbuf_tensor("scores", [P, NE, NT], F32))
            with ExitStack() as inner:
                output(nc, io, B, inner, sem, passed, scores, d_h, d_ctx, d_xg)
            chosen = ctx.enter_context(nc.sbuf_tensor("chosen", [P, NE, CT], U32))
            with ExitStack() as inner:
                choose(nc, io, NT, inner, sem, passed, scores, chosen)
            with ExitStack() as inner:
                experts(nc, io, T, inner, sem, passed, chosen, d_xg)


def project(nc, io, B, ctx, sem, passed, d_tab, d_stack, d_kterm, d_v, d_h):
    def sb(name, shape, dt=F32):
        return ctx.enter_context(nc.sbuf_tensor("p_" + name, shape, dt))

    def ps(name, shape):
        return ctx.enter_context(nc.psum_tensor("p_ps_" + name, shape, F32))

    mix = sb("mix", [P, ND * HC, H])
    ident = sb("ident", [P, P])
    wq, wk, wv = (sb(n, [P, HC, H]) for n in ("wq", "wk", "wv"))
    bv_row = sb("bv_row", [P, H])
    qk_bias = sb("qk_bias", [P, 4, HC])
    kterm_w = sb("kterm_w", [P, HC, 2 * NH])
    minus_half = sb("minus_half", [P, QT])

    with ExitStack() as tctx:
        def tsb(name, shape, dt=F32):
            return tctx.enter_context(nc.sbuf_tensor("t_" + name, shape, dt))

        def tps(name, shape):
            return tctx.enter_context(nc.psum_tensor("t_ps_" + name, shape, F32))

        ws = tsb("ws", [P, HC, H])
        wd = tsb("wd", [P, ND, H])
        rel = tsb("rel", [P, H])
        lng, lnb = tsb("lng", [P, H]), tsb("lnb", [P, H])
        wp = tsb("wp", [P, 2, HC, H])
        bp = tsb("bp", [P, 2, H])
        pick = tsb("pick", [P, 2, TW])
        ends = tsb("ends", [P, 2])
        own = tsb("own", [P, HC, NH])
        stats, moments = tsb("stats", [P, 6]), tsb("moments", [P, 2])
        rstd, relT, pos = tsb("rstd", [P, 2]), tsb("relT", [P, HC, P]), tsb("pos", [P, 2, H])
        rest = tsb("rest", [P, 2, HC, TW])
        parts = tsb("parts", [P, 2, HC, 3, TW], BF16)
        consts = tsb("consts", [P, 2, HC, 2])
        t_turn = tps("turn", [P, S])
        t_pos = tps("pos", [P, 2, H])
        t_tab = tps("tab", [P, 2 * HC, S])
        t_end = tps("end", [P, 2, HC, 2])
        t_in, t_const, t_dve, t_pe, t_pool, t_out = (
            sem("t_" + n) for n in ("in", "const", "dve", "pe", "pool", "out"))
        loads = [
            (ws, io["wsT"].rearrange("(c p) o -> p c o", p=P)),
            (wd, io["tok_weight"].partition_broadcast(P)),
            (rel, io["rel_emb"]), (lng, io["ln_g"].partition_broadcast(P)),
            (lnb, io["ln_b"].partition_broadcast(P)),
            (wp[:, 0], io["Wpk"].rearrange("(c p) o -> p c o", p=P)),
            (wp[:, 1], io["Wpq"].rearrange("(c p) o -> p c o", p=P)),
            (bp[:, 0], io["bpk"].partition_broadcast(P)),
            (bp[:, 1], io["bpq"].partition_broadcast(P)),
            (pick, io["pick"]), (ends, io["ends"]), (own, io["own"]), (ident, io["ident"]),
            (wq, io["Wq"].rearrange("(c p) o -> p c o", p=P)),
            (wk, io["Wk"].rearrange("(c p) o -> p c o", p=P)),
            (wv, io["Wv"].rearrange("(c p) o -> p c o", p=P)),
            (bv_row, io["bv"].partition_broadcast(P)),
            (qk_bias[:, 0], io["bq_col"]), (qk_bias[:, 1], io["bk_col"]),
        ]
        with nc.Block() as block:
            @block.sync
            def _(sp):
                for dst, src in loads:
                    sp.dma_start(dst[:], src).then_inc(t_in, 16)
                sp.wait_ge(t_dve, 18)
                for w in range(2):
                    for c in range(HC):
                        sp.dma_start(d_tab[w, :, c * P:(c + 1) * P, :].rearrange("t p x -> p t x"),
                                     parts[:, w, c]).then_inc(t_out, 16)
                sp.wait_ge(t_out, 16 * 2 * HC)

            @block.gpsimd
            def _(pool):
                nc.gpsimd.memset(minus_half[:], -0.5).then_inc(t_const, 1)
                pool.wait_ge(t_const, 1)
                pool.wait_ge(t_dve, 3)
                nc.gpsimd.tensor_tensor(rstd[:, 1:2], rstd[:, 0:1], minus_half[:, 0:1],
                                        ALU.pow).then_inc(t_pool, 1)

            @block.vector
            def _(dve):
                done = [0]

                def step(ins, wait=True):
                    done[0] += 1
                    ins.then_inc(t_dve, 1)
                    if wait:
                        dve.wait_ge(t_dve, done[0])

                dve.wait_ge(t_in, 16 * len(loads))
                step(nc.vector.bn_stats(stats[:], rel[:]))
                step(nc.vector.bn_aggr(moments[:], stats[:]))
                step(nc.vector.tensor_scalar_add(rstd[:, 0:1], moments[:, 1:2], EPS))
                for d in range(ND):
                    for c in range(HC):
                        nc.vector.tensor_tensor(mix[:, d * HC + c], ws[:, c], wd[:, d], ALU.mult)
                dve.wait_ge(t_pool, 1)
                step(nc.vector.tensor_scalar(rel[:], rel[:], moments[:, 0:1], rstd[:, 1:2],
                                             ALU.subtract, ALU.mult))
                step(nc.vector.tensor_tensor(rel[:], rel[:], lng[:], ALU.mult))
                step(nc.vector.tensor_tensor(rel[:], rel[:], lnb[:], ALU.add))
                dve.wait_ge(t_pe, 1)
                step(nc.vector.tensor_copy(relT[:], t_turn[:, 0:HC * P].rearrange(
                    "p (c q) -> p c q", c=HC)))
                dve.wait_ge(t_pe, 2)
                step(nc.vector.tensor_tensor(pos[:], t_pos[:], bp[:], ALU.add))
                dve.wait_ge(t_pe, 3)
                step(nc.vector.tensor_copy(consts[:], t_end[:]))
                tab = t_tab[:, :, 0:TW].rearrange("p (w c) x -> p w c x", w=2)
                step(nc.vector.tensor_copy(parts[:, :, :, 0], tab))
                step(nc.vector.tensor_tensor(rest[:], tab, parts[:, :, :, 0], ALU.subtract))
                step(nc.vector.tensor_copy(parts[:, :, :, 1], rest[:]))
                step(nc.vector.tensor_tensor(rest[:], rest[:], parts[:, :, :, 1], ALU.subtract))
                step(nc.vector.tensor_copy(parts[:, :, :, 2], rest[:]))
                for side in range(2):
                    step(nc.vector.tensor_tensor(qk_bias[:, 2 + side], qk_bias[:, 1],
                                                 consts[:, 0, :, side], ALU.add))
                for c in range(HC):
                    for side in range(2):
                        ins = nc.vector.tensor_scalar(
                            kterm_w[:, c, side * NH:(side + 1) * NH], own[:, c],
                            consts[:, 1, c, side:side + 1], None, ALU.mult)
                step(ins)
                step(nc.vector.tensor_copy(rstd[:, 0:1], rstd[:, 1:2]))

            @block.tensor
            def _(pe):
                pe.wait_ge(t_dve, 6)
                for c in range(HC):
                    mm = pe.transpose(t_turn[:, c * P:(c + 1) * P], rel[:, c * P:(c + 1) * P], ident[:])
                mm.then_inc(t_pe, 1)
                pe.wait_ge(t_dve, 7)
                for w in range(2):
                    for c in range(HC):
                        mm = pe.matmul(t_pos[:, w], relT[:, c], wp[:, w, c], start=(c == 0),
                                       stop=(c == HC - 1))
                mm.then_inc(t_pe, 1)
                pe.wait_ge(t_dve, 8)
                for w in range(2):
                    for c in range(HC):
                        of = pos[:, w, c * P:(c + 1) * P]
                        pe.matmul(t_end[:, w, c], of, ends[:], start=True, stop=True)
                        mm = pe.matmul(t_tab[:, w * HC + c, 0:TW], of, pick[:, w], start=True, stop=True)
                mm.then_inc(t_pe, 1)

    xt = sb("xt", [P, 2, ND * HC, S])
    h_sb = sb("h_sb", [P, 2, QT, H])
    stats = sb("stats", [P, QT, 6])
    moments = sb("moments", [P, QT, 2])
    var_eps, rstd = sb("var_eps", [P, QT]), sb("rstd", [P, QT])
    xn = sb("xn", [P, QT, H])
    xnT = sb("xnT", [P, HC, S])
    full_q = sb("full_q", [P, HC, S])
    full_k = sb("full_k", [P, HC, KW])
    part_q = sb("part_q", [P, 2, 3, HC, S], BF16)
    part_k = sb("part_k", [P, 2, 3, HC, KW], BF16)
    full_t = sb("full_t", [2 * NH, S])
    part_t = sb("part_t", [2 * NH, 3, S], BF16)
    v_sb = sb("v_sb", [P, QT, NH, CROW])
    m_h = ps("m_h", [P, QT, H])
    m_turn = ps("m_turn", [P, HC, S])
    m_qk = ps("m_qk", [P, 2, S])
    m_v = ps("m_v", [P, 2, H])
    m_t = ps("m_t", [2 * NH, S])
    x_in = [sem(f"p_x_in{u}") for u in range(2)]
    (h_done, h_kept, st_done, mo_done, ve_done, rs_done, xn_done, turn_done, turnA, turnD,
     qk_done, qk_kept, t_done, t_kept, low_done, mid_done, parts_done, v_done, v_kept,
     v_const) = (sem("p_" + n) for n in (
         "h_done", "h_kept", "st_done", "mo_done", "ve_done", "rs_done", "xn_done", "turn_done",
         "turnA", "turnD", "qk_done", "qk_kept", "t_done", "t_kept", "low_done", "mid_done",
         "parts_done", "v_done", "v_kept", "v_const"))
    h_out = [sem(f"p_h_out{u}") for u in range(2)]
    v_out, t_out = sem("p_v_out"), sem("p_t_out")
    parts_out = [sem(f"p_parts_out{u}") for u in range(2)]
    DMAS = 2 * SLOTS
    CH = 2 * HC
    xT = io["xT"]
    pairs = B // 2

    with nc.Block() as block:
        @block.sync
        def _(sp):
            for u in range(2):
                sp.dma_start(xt[:, u], xT[u].rearrange("d (c p) s -> p (d c) s", p=P)).then_inc(x_in[u], 16)

            def body(i, last):
                for u in range(2):
                    n = 2 * i + u
                    if not last:
                        settled(sp, h_done, 2 * (n + 1), passed)
                        sp.dma_start(xt[:, u], xT[n + 2].rearrange("d (c p) s -> p (d c) s", p=P)
                                     ).then_inc(x_in[u], 16)
                    settled(sp, h_kept, 2 * (n + 1), passed)
                    sp.dma_start(d_h[n].rearrange("(t p) o -> p t o", p=P), h_sb[:, u]).then_inc(h_out[u], 16)
                    settled(sp, v_kept, 2 * (n + 1), passed)
                    sp.dma_start(d_v[n].rearrange("(t p) o -> p t o", p=P),
                                 v_sb[:].rearrange("p t h r -> p t (h r)")).then_inc(v_out, 16)
                    settled(sp, parts_done, (CH + 1) * (n + 1), passed)
                    for j in range(SLOTS):
                        to = d_stack[n, j].rearrange("(c p) x -> p c x", p=P)
                        sp.dma_start(to[:, :, 0:S], part_q[:, u, SIDE_A[j]]).then_inc(parts_out[u], 16)
                        sp.dma_start(to[:, :, S:SW], part_k[:, u, SIDE_B[j]]).then_inc(parts_out[u], 16)
                    to = d_kterm[n].rearrange("t h x -> h t x")
                    sp.dma_start(to[:, :, 0:S], part_t[0:NH]).then_inc(t_out, 16)
                    sp.dma_start(to[:, :, S:], part_t[NH:, :, 0:S // 2]).then_inc(t_out, 16)

            peeled(sp, pairs, body)
            sp.wait_ge(v_out, 16 * B)
            sp.wait_ge(t_out, 32 * B)
            for u in range(2):
                sp.wait_ge(parts_out[u], 16 * DMAS * pairs)
                sp.wait_ge(h_out[u], 16 * pairs)

        @block.tensor
        def _(pe):
            def mixing(n, i, u):
                after(pe, x_in[u], 16 * (i + 1))
                for t in range(QT):
                    if t % 2 == 0:
                        after(pe, h_kept, 2 * (n - 1) + t // 2 + 1 if not isinstance(n, int) or n else 0)
                    for k in range(ND * HC):
                        mm = pe.matmul(m_h[:, t], xt[:, u, k, t * P:(t + 1) * P], mix[:, k],
                                       start=(k == 0), stop=(k == ND * HC - 1))
                    if t % 2:
                        mm.then_inc(h_done, 1)

            def projections(n):
                after(pe, xn_done, n + 1)
                after(pe, turnA, n)
                after(pe, turnD, n)
                for c in range(HC):
                    for t in range(QT):
                        mm = pe.transpose(m_turn[:, c, t * P:(t + 1) * P], xn[:, t, c * P:(c + 1) * P], ident[:])
                    mm.then_inc(turn_done, 1)
                after(pe, turnA, n + 1)
                after(pe, turnD, n + 1)
                for m in range(CH):
                    after(pe, qk_kept, CH * n + m - 1)
                    w = (wq, wk)[m // HC]
                    for c in range(HC):
                        mm = pe.matmul(m_qk[:, m % 2], w[:, c, (m % HC) * P:(m % HC + 1) * P], xnT[:, c],
                                       start=(c == 0), stop=(c == HC - 1))
                    mm.then_inc(qk_done, 1)
                for half in range(2):
                    after(pe, v_kept, 2 * n + half)
                    for t in range(2):
                        at = (2 * half + t) * P
                        for c in range(HC):
                            mm = pe.matmul(m_v[:, t], xnT[:, c, at:at + P], wv[:, c], start=(c == 0),
                                           stop=(c == HC - 1))
                    mm.then_inc(v_done, 1)
                after(pe, qk_kept, CH * (n + 1))
                after(pe, t_kept, n)
                for c in range(HC):
                    mm = pe.matmul(m_t[:], kterm_w[:, c], full_k[:, c, 0:S], start=(c == 0), stop=(c == HC - 1))
                mm.then_inc(t_done, 1)

            mixing(0, 0, 0)

            def body(i, last):
                mixing(2 * i + 1, i, 1)
                projections(2 * i)
                if not last:
                    mixing(2 * i + 2, i + 1, 0)
                projections(2 * i + 1)

            peeled(pe, pairs, body)

        @block.scalar
        def _(act):
            def keep_h(n, i, u):
                if not (isinstance(n, int) and n < 2):
                    after(act, h_out[u], 16 * i)
                    after(act, xn_done, n - 1)
                for half in range(2):
                    after(act, h_done, 2 * n + half + 1)
                    nc.scalar.activation(h_sb[:, u, 2 * half:2 * half + 2], m_h[:, 2 * half:2 * half + 2],
                                         ACT.Identity).then_inc(h_kept, 1)

            def keep_qk(n, i, u):
                after(act, turn_done, HC * n + 1)
                nc.scalar.activation(xnT[:, 0], m_turn[:, 0], ACT.Identity).then_inc(turnA, 1)
                after(act, parts_out[u], 16 * DMAS * i)
                for m in range(CH):
                    c = m % HC
                    after(act, qk_done, CH * n + m + 1)
                    after(act, parts_done, (CH + 1) * (n - 1) + m + 1 if not isinstance(n, int) or n else 0)
                    src = m_qk[:, m % 2]
                    if m < HC:
                        nc.scalar.activation(full_q[:, c], src, ACT.Identity, bias=qk_bias[:, 0, c:c + 1])
                        ins = nc.scalar.activation(part_q[:, u, 0, c], src, ACT.Identity,
                                                   bias=qk_bias[:, 0, c:c + 1])
                    else:
                        for out in (full_k[:, c], part_k[:, u, 0, c]):
                            nc.scalar.activation(out[:, 0:S], src, ACT.Identity, bias=qk_bias[:, 1, c:c + 1])
                            nc.scalar.activation(out[:, S:2 * S], src, ACT.Identity,
                                                 bias=qk_bias[:, 2, c:c + 1])
                            ins = nc.scalar.activation(out[:, 2 * S:], src[:, 0:S // 2], ACT.Identity,
                                                       bias=qk_bias[:, 3, c:c + 1])
                    ins.then_inc(qk_kept, 1)
                after(act, t_done, n + 1)
                after(act, parts_done, (CH + 1) * n)
                after(act, t_out, 32 * n)
                nc.scalar.activation(full_t[:], m_t[:], ACT.Identity)
                nc.scalar.activation(part_t[:, 0], m_t[:], ACT.Identity).then_inc(t_kept, 1)

            keep_h(0, 0, 0)

            def body(i, last):
                keep_h(2 * i + 1, i, 1)
                keep_qk(2 * i, i, 0)
                if not last:
                    keep_h(2 * i + 2, i + 1, 0)
                keep_qk(2 * i + 1, i, 1)

            peeled(act, pairs, body)

        @block.gpsimd
        def _(pool):
            nc.gpsimd.memset(v_sb[:], 0.0).then_inc(v_const, 1)
            pool.wait_ge(v_const, 1)
            nc.gpsimd.memset(v_sb[:, :, :, HD:HD + 1], 1.0).then_inc(v_const, 1)

            def power(n):
                after(pool, ve_done, n + 1)
                nc.gpsimd.tensor_tensor(rstd[:], var_eps[:], minus_half[:], ALU.pow).then_inc(rs_done, 1)

            def lower(n, i, u):
                for m in range(CH):
                    c = m % HC
                    after(pool, qk_kept, CH * n + m + 1)
                    if m == HC:
                        after(pool, t_done, n + 1)
                    a, p = (full_q[:, c], part_q[:, u, 0, c]) if m < HC else (full_k[:, c], part_k[:, u, 0, c])
                    nc.gpsimd.tensor_tensor(a, a, p, ALU.subtract).then_inc(low_done, 1)
                after(pool, t_kept, n + 1)
                nc.gpsimd.tensor_tensor(full_t[:], full_t[:], part_t[:, 0], ALU.subtract).then_inc(low_done, 1)

            power(0)

            def body(i, last):
                power(2 * i + 1)
                lower(2 * i, i, 0)
                if not last:
                    power(2 * i + 2)
                lower(2 * i + 1, i, 1)

            peeled(pool, pairs, body)

        @block.vector
        def _(dve):
            def norm(n, u):
                for t in range(QT):
                    after(dve, h_kept, 2 * n + t // 2 + 1)
                    nc.vector.bn_stats(stats[:, t], h_sb[:, u, t]).then_inc(st_done, 1)
                settled(dve, st_done, QT * (n + 1), passed)
                for t in range(QT):
                    nc.vector.bn_aggr(moments[:, t], stats[:, t]).then_inc(mo_done, 1)
                after(dve, mo_done, QT * (n + 1))
                nc.vector.tensor_scalar_add(var_eps[:], moments[:, :, 1], EPS).then_inc(ve_done, 1)
                after(dve, rs_done, n + 1)
                after(dve, turn_done, HC * n)
                for t in range(QT):
                    ins = nc.vector.tensor_scalar(xn[:, t], h_sb[:, u, t], moments[:, t, 0:1], rstd[:, t:t + 1],
                                                  ALU.subtract, ALU.mult)
                ins.then_inc(xn_done, 1)

            def split(n, i, u):
                after(dve, turn_done, HC * n + 2)
                nc.vector.tensor_copy(xnT[:, 1], m_turn[:, 1]).then_inc(turnD, 1)
                for half in range(2):
                    after(dve, v_done, 2 * n + half + 1)
                    if half == 0:
                        after(dve, v_out, 16 * n)
                    nc.vector.tensor_tensor(
                        v_sb[:, 2 * half:2 * half + 2, :, 0:HD],
                        m_v[:].rearrange("p t (h d) -> p t h d", d=HD),
                        bv_row[:].rearrange("p (h d) -> p h d", d=HD).unsqueeze(1).to_broadcast([P, 2, NH, HD]),
                        ALU.add).then_inc(v_kept, 1)
                for m in range(CH + 1):
                    c = m % HC
                    after(dve, low_done, (CH + 1) * n + m + 1)
                    if m < HC:
                        a, mid, low = full_q[:, c], part_q[:, u, 1, c], part_q[:, u, 2, c]
                    elif m < CH:
                        a, mid, low = full_k[:, c], part_k[:, u, 1, c], part_k[:, u, 2, c]
                    else:
                        a, mid, low = full_t[:], part_t[:, 1], part_t[:, 2]
                    nc.vector.tensor_copy(mid, a).then_inc(mid_done, 1)
                    after(dve, mid_done, (CH + 1) * n + m + 1)
                    nc.vector.tensor_tensor(low, a, mid, ALU.subtract).then_inc(parts_done, 1)

            dve.wait_ge(v_const, 2)
            norm(0, 0)

            def body(i, last):
                norm(2 * i + 1, 1)
                split(2 * i, i, 0)
                if not last:
                    norm(2 * i + 2, 0)
                split(2 * i + 1, i, 1)

            peeled(dve, pairs, body)


def attend(nc, io, B, ctx, sem, passed, d_tab, d_stack, d_kterm, d_v, d_skew, d_ctx):
    def sb(name, shape, dt=F32):
        return ctx.enter_context(nc.sbuf_tensor("a_" + name, shape, dt))

    def ps(name, shape):
        return ctx.enter_context(nc.psum_tensor("a_ps_" + name, shape, F32))

    ident = sb("ident", [P, P])
    tabs = sb("tabs", [ST, 2, NH, TW], BF16)
    stack = sb("stack", [ST + 3, 2, GH, SW], BF16)
    skew_in = sb("skew_in", [P, 2, 2, QT, TW])
    bias_c = sb("bias_c", [P, 2, QT, BW])
    bias_p = sb("bias_p", [P, 2, QT, BW])
    scored = sb("scored", [P, QT, S])
    top_of = sb("top_of", [P, 2, QT])
    shift = sb("shift", [P, 2, QT])
    probs = sb("probs", [P, 2, QT, S])
    probsT = sb("probsT", [P, QT, S])
    values = sb("values", [P, 2, QT, NH // 2, CROW])
    ctx_sb = sb("ctx_sb", [P, 2, S])
    m_tab = ps("m_tab", [P, 2, S])
    m_s = ps("m_s", [P, 2, S])
    m_t = ps("m_t", [P, 2, S])
    m_ctx = ps("m_ctx", [P, S])

    const_in, zeroed, zeroed_p, zero_out = (sem("a_" + n) for n in ("const_in", "zeroed", "zeroed_p", "zero_out"))
    stack_in = [sem(f"a_stack_in{u}") for u in range(2)]
    values_in = [sem(f"a_values_in{u}") for u in range(2)]
    skew_out = [sem(f"a_skew_out{u}") for u in range(2)]
    bias_in = [sem(f"a_bias_in{u}") for u in range(2)]
    (tab_done, tab_c, tab_p, s_done, s_kept, shifted, exp_done, turn_done, turnA, turnD, pv_done,
     ctx_kept, ctx_out) = (sem("a_" + n) for n in (
         "tab_done", "tab_c", "tab_p", "s_done", "s_kept", "shifted", "exp_done", "turn_done", "turnA",
         "turnD", "pv_done", "ctx_kept", "ctx_out"))
    STACKS = SLOTS + 1
    HEADS = B * NH
    READS = 6
    scratch = d_skew.tensor
    plane = P * PITCH

    with nc.Block() as block:
        @block.sync
        def _(sp):
            sp.dma_start(ident[:], io["ident"]).then_inc(const_in, 16)
            for w in range(2):
                for j in range(SLOTS):
                    part = (SIDE_B if w == 0 else SIDE_A)[j]
                    sp.dma_start(tabs[j * HD:(j + 1) * HD, w],
                                 d_tab[w, part].rearrange("(h d) x -> d h x", d=HD)).then_inc(const_in, 16)

            def load_stack(b, g):
                u = g % 2
                for j in range(SLOTS):
                    sp.dma_start(stack[j * HD:(j + 1) * HD, u],
                                 d_stack[b, j, g * GH * HD:(g + 1) * GH * HD].rearrange("(h d) x -> d h x", d=HD)
                                 ).then_inc(stack_in[u], 16)
                sp.dma_start(stack[ST:ST + 3, u, :, 2 * S:], d_kterm[b, :, g * GH:(g + 1) * GH]
                             ).then_inc(stack_in[u], 16)

            def load_values(b, half):
                sp.dma_start(values[:, half],
                             d_v[b].rearrange("(t p) x -> p t x", p=P)[
                                 :, :, half * NH // 2 * CROW:(half + 1) * NH // 2 * CROW]
                             .rearrange("p t (h r) -> p t h r", r=CROW)).then_inc(values_in[half], 16)

            def write_tables(n, hh):
                u, slot = hh % 2, hh % RING
                for w, kept in ((0, tab_c), (1, tab_p)):
                    settled(sp, kept, QT * (n + 1), passed)
                    at = 0 if w == 0 else PITCH - 1 - TW
                    sp.dma_start(d_skew[slot, w].rearrange("t p x -> p t x")[:, :, at:at + TW],
                                 skew_in[:, u, w]).then_inc(skew_out[u], 16)

            def read_tables(n, b, hh):
                u, slot = hh % 2, hh % RING
                settled(sp, skew_out[u], 32 * (NH // 2 * b + hh // 2 + 1), passed)
                settled(sp, s_kept, QT * (n - 1), passed)
                for w, bias in enumerate((bias_c, bias_p)):
                    base = (slot * 2 + w) * QT * plane + P - 1
                    for t, count, skip, width in ((0, 1, P, 2 * P), (1, QT - 2, 0, NEAR), (QT - 1, 1, 0, 2 * P)):
                        src = bass.AP(scratch, base + t * plane + skip,
                                      [[PITCH - 1, P], [plane, count], [1, width]])
                        row = t * (BW + P) + skip
                        flat = bias[:, u].rearrange("p t x -> p (t x)")
                        if count == 1:
                            dst = flat[:, row:row + width].unsqueeze(1)
                        else:
                            dst = bass.AP(flat.tensor, flat.offset + row,
                                          [list(flat.ap[0]), [BW + P, count], [1, width]])
                        sp.dma_start(dst, src).then_inc(bias_in[u], 16)

            load_stack(0, 0)
            load_stack(0, 1)
            load_values(0, 0)
            load_values(0, 1)
            sp.wait_ge(zeroed, 3)
            sp.wait_ge(zeroed_p, 1)
            for slot in range(RING):
                for w, at in ((0, TW), (1, 0)):
                    sp.dma_start(d_skew[slot, w].rearrange("t p x -> p t x")[:, :, at:at + PITCH - 1 - TW],
                                 skew_in[:, 0, 0, :, 0:PITCH - 1 - TW]).then_inc(zero_out, 16)
            sp.wait_ge(zero_out, 16 * 2 * RING)
            for m in range(LEAD):
                write_tables(m, m)
                if m:
                    read_tables(m - 1, 0, m - 1)

            def body(b, last):
                for hh in range(NH):
                    n = NH * b + hh
                    if hh % GH == 0 and not (isinstance(b, int) and b == 0 and hh == 0):
                        g = hh // GH + 1
                        if not (last and g == NG):
                            settled(sp, s_done, QT * n, passed)
                            load_stack(b + g // NG, g % NG)
                    if not (last and hh + LEAD >= NH):
                        write_tables(n + LEAD, (hh + LEAD) % NH)
                    if not (last and hh + LEAD - 1 >= NH):
                        m = hh + LEAD - 1
                        read_tables(n + LEAD - 1, b + m // NH, m % NH)
                    if hh == 1 and not (isinstance(b, int) and b == 0):
                        settled(sp, pv_done, n - 1, passed)
                        load_values(b, 1)
                    if hh == NH // 2 + 1 and not last:
                        settled(sp, pv_done, n - 1, passed)
                        load_values(b + 1, 0)
                    if hh % GH == 1 and not (isinstance(b, int) and b == 0 and hh == 1):
                        store_ctx(b, hh // GH - 1)

            def store_ctx(b, g):
                G = NG * b + g
                settled(sp, ctx_kept, G + 1, passed)
                to = d_ctx[b, g] if g >= 0 else d_ctx[b - 1, NG - 1]
                sp.dma_start(to, ctx_sb[:, g % 2]).then_inc(ctx_out, 16)

            peeled(sp, B, body)
            store_ctx(B - 1, NG - 1)
            sp.wait_ge(ctx_out, 16 * NG * B)

        @block.gpsimd
        def _(pool):
            nc.gpsimd.memset(skew_in[:, 0], 0.0).then_inc(zeroed, 1)
            nc.gpsimd.memset(bias_c[:], 0.0).then_inc(zeroed, 1)
            pool.wait_ge(zeroed, 2)
            nc.gpsimd.memset(stack[ST:ST + 3, :, :, 0:S], 1.0).then_inc(zeroed, 1)

        @block.tensor
        def _(pe):
            def tables(n, b, hh):
                g = hh // GH
                if hh % GH == 0:
                    after(pe, stack_in[g % 2], 16 * STACKS * (NG // 2 * b + g // 2 + 1))
                for t in range(QT):
                    for w, kept in ((0, tab_c), (1, tab_p)):
                        after(pe, kept, QT * n + t)
                        at = (S if w else 0) + t * P
                        pe.matmul(m_tab[:, w, 0:TW], stack[0:ST, g % 2, hh % GH, at:at + P],
                                  tabs[:, w, hh], start=True, stop=True).then_inc(tab_done, 1)

            def scores(n, b, hh):
                u, g = hh % 2, hh // GH
                after(pe, bias_in[u], 16 * READS * (NH // 2 * b + hh // 2 + 1))
                for t in range(QT):
                    after(pe, s_kept, QT * n + t - 1)
                    bank = m_s[:, t % 2]
                    row = stack[0:ST + 3, g % 2, hh % GH]
                    q = row[:, t * P:(t + 1) * P]
                    far = max(0, t - 1) * P
                    if far:
                        pe.matmul(bank[:, 0:far], q, row[:, 3 * S:3 * S + far], start=True, stop=False,
                                  skip_group_check=True)
                    pe.matmul(bank[:, far:], q, row[:, 2 * S + far:3 * S], start=not far, stop=False,
                              skip_group_check=True)
                    near = [k for k in range(QT) if abs(k - t) <= 1]
                    for k in near:
                        mm = pe.matmul(bank[:, k * P:(k + 1) * P], bias_p[:, u, k, (t + 1) * P:(t + 2) * P],
                                       ident[:], start=False, stop=(k == near[-1]), is_transpose=True,
                                       skip_group_check=True)
                    mm.then_inc(s_done, 1)

            def context(n, b, hh):
                u, half, j = hh % 2, hh // (NH // 2), hh % GH
                after(pe, exp_done, QT * (n + 1))
                for k in range(QT):
                    after(pe, (turnA, turnD)[k % 2], 2 * n + k // 2)
                    for t in range(QT):
                        mm = pe.transpose(m_t[:, k % 2, t * P:(t + 1) * P], probs[:, u, t, k * P:(k + 1) * P],
                                          ident[:])
                    mm.then_inc(turn_done, 1)
                if hh % (NH // 2) == 0:
                    after(pe, values_in[half], 16 * (b + 1))
                if j == 0:
                    after(pe, ctx_kept, NG * b + hh // GH)
                for k in range(QT):
                    after(pe, (turnA, turnD)[k % 2], 2 * n + k // 2 + 1)
                    mm = pe.matmul(m_ctx[j * CROW:(j + 1) * CROW], values[:, half, k, hh % (NH // 2)],
                                   probsT[:, k], start=(k == 0), stop=(k == QT - 1))
                mm.then_inc(pv_done, 1)

            pe.wait_ge(const_in, 16 * (1 + 2 * SLOTS))
            pe.wait_ge(zeroed, 3)
            for m in range(LEAD):
                tables(m, 0, m)

            def body(b, last):
                for hh in range(NH):
                    n = NH * b + hh
                    m = hh + LEAD
                    if not (last and m >= NH):
                        tables(n + LEAD, b + m // NH, m % NH)
                    scores(n, b, hh)
                    if hh == 0:
                        if not (isinstance(b, int) and b == 0):
                            context(n - 1, b - 1, NH - 1)
                    else:
                        context(n - 1, b, hh - 1)

            peeled(pe, B, body)
            context(HEADS - 1, B - 1, NH - 1)

        @block.scalar
        def _(act):
            def keep_tables(n, hh):
                u = hh % 2
                for t in range(QT):
                    after(act, tab_done, 2 * (QT * n + t) + 1)
                    if t == 0:
                        wait_tables(act, skew_out, n, hh)
                    nc.scalar.activation(skew_in[:, u, 0, t], m_tab[:, 0, 0:TW], ACT.Identity
                                         ).then_inc(tab_c, 1)

            def softmax(n, hh):
                u = hh % 2
                after(act, shifted, n + 1)
                after(act, turn_done, QT * (n - 1))
                for t in range(QT):
                    nc.scalar.activation(probs[:, u, t], scored[:, t], ACT.Exp, bias=shift[:, u, t:t + 1],
                                         scale=SCALE).then_inc(exp_done, 1)

            def keep_turned(n):
                for k in (0, 2):
                    after(act, turn_done, QT * n + k + 1)
                    after(act, pv_done, n)
                    nc.scalar.activation(probsT[:, k], m_t[:, 0], ACT.Identity).then_inc(turnA, 1)

            def keep_context(n, b, hh):
                g = hh // GH
                after(act, pv_done, n + 1)
                after(act, ctx_out, 16 * (NG * b + g))
                nc.scalar.activation(ctx_sb[:, g % 2], m_ctx[:], ACT.Identity).then_inc(ctx_kept, 1)

            act.wait_ge(zero_out, 16 * 2 * RING)
            for m in range(LEAD):
                keep_tables(m, m)

            def body(b, last):
                for hh in range(NH):
                    n, m = NH * b + hh, hh + LEAD
                    if not (last and m >= NH):
                        keep_tables(n + LEAD, m % NH)
                    if hh or not (isinstance(b, int) and b == 0):
                        keep_turned(n - 1)
                        if hh % GH == 0:
                            keep_context(n - 1, b if hh else b - 1, hh - 1 if hh else NH - 1)
                    softmax(n, hh)

            peeled(act, B, body)
            keep_turned(HEADS - 1)
            keep_context(HEADS - 1, B - 1, NH - 1)

        @block.vector
        def _(dve):
            nc.vector.memset(bias_p[:], 0.0).then_inc(zeroed_p, 1)

            def keep_tables(n, hh):
                u = hh % 2
                for t in range(QT):
                    after(dve, tab_done, 2 * (QT * n + t) + 2)
                    if t == 0:
                        wait_tables(dve, skew_out, n, hh)
                    nc.vector.tensor_copy(skew_in[:, u, 1, t], m_tab[:, 1, 0:TW]).then_inc(tab_p, 1)

            def add_bias(n, b, hh):
                u = hh % 2
                after(dve, bias_in[u], 16 * READS * (NH // 2 * b + hh // 2 + 1))
                for t in range(QT):
                    after(dve, exp_done, QT * (n - 1) + t + 1 if not isinstance(n, int) or n else 0)
                    settled(dve, s_done, QT * n + t + 1, passed)
                    nc.vector.tensor_tensor_reduce(scored[:, t], m_s[:, t % 2], bias_c[:, u, t, P:P + S], 1.0,
                                                   -3.0e38, ALU.add, ALU.max, top_of[:, u, t:t + 1]
                                                   ).then_inc(s_kept, 1)
                after(dve, s_kept, QT * (n + 1))
                nc.vector.tensor_scalar(shift[:, u], top_of[:, u], -SCALE, None, ALU.mult).then_inc(shifted, 1)

            def keep_turned(n):
                for k in (1, 3):
                    after(dve, turn_done, QT * n + k + 1)
                    after(dve, pv_done, n)
                    nc.vector.tensor_copy(probsT[:, k], m_t[:, 1]).then_inc(turnD, 1)

            dve.wait_ge(zero_out, 16 * 2 * RING)
            for m in range(LEAD):
                keep_tables(m, m)

            def body(b, last):
                for hh in range(NH):
                    n, m = NH * b + hh, hh + LEAD
                    if not (last and m >= NH):
                        keep_tables(n + LEAD, m % NH)
                    add_bias(n, b, hh)
                    if hh or not (isinstance(b, int) and b == 0):
                        keep_turned(n - 1)

            peeled(dve, B, body)
            keep_turned(HEADS - 1)


def wait_tables(eng, skew_out, n, hh):
    if not (isinstance(n, int) and n < 2):
        eng.wait_ge(skew_out[hh % 2], 16 * (n - hh % 2))


def output(nc, io, B, ctx, sem, passed, scores, d_h, d_ctx, d_xg):
    def sb(name, shape, dt=F32):
        return ctx.enter_context(nc.sbuf_tensor("o_" + name, shape, dt))

    def ps(name, shape):
        return ctx.enter_context(nc.psum_tensor("o_ps_" + name, shape, F32))

    ident, wo = sb("ident", [P, P]), sb("wo", [P, HC, H])
    bo_row, wr, br_row = sb("bo_row", [P, H]), sb("wr", [P, HC, NE]), sb("br_row", [P, NE])
    minus_half = sb("minus_half", [P, QT])
    h_in, h_new = sb("h_in", [P, 2, QT, H]), sb("h_new", [P, 2, QT, H])
    c_in, sums = sb("c_in", [P, 2, HC, S]), sb("sums", [P, 2, HC, S])
    ctxn = sb("ctxn", [P, HC, S])
    stats, moments = sb("stats", [P, QT, 6]), sb("moments", [P, QT, 2])
    var_eps, rstd = sb("var_eps", [P, QT]), sb("rstd", [P, QT])
    xg, xT = sb("xg", [P, 2, QT, XG]), sb("xT", [P, HC, S])
    logits, expd = sb("logits", [P, QT, NE]), sb("expd", [P, QT, NE])
    top_of, total, share = sb("top_of", [P, QT]), sb("total", [P, QT]), sb("share", [P, QT])
    m_o, m_turn, m_r = ps("m_o", [P, QT, H]), ps("m_turn", [P, HC, S]), ps("m_r", [P, QT, NE])
    const_in, half_set = sem("o_const_in"), sem("o_half_set")
    batch_in = [sem(f"o_batch_in{u}") for u in range(2)]
    stored = [sem(f"o_stored{u}") for u in range(2)]
    (scaled, scale_step, o_done, h_added, h_done, st_done, mo_done, ve_done, rs_done, xn_done, turn_done,
     turnA, turnD, r_done, soft, exp_done, xg_done) = (sem("o_" + n) for n in (
         "scaled", "scale_step", "o_done", "h_added", "h_done", "st_done", "mo_done", "ve_done", "rs_done",
         "xn_done", "turn_done", "turnA", "turnD", "r_done", "soft", "exp_done", "xg_done"))
    consts = [(ident[:], io["ident"]), (wo[:], io["Wo"].rearrange("(c p) o -> p c o", p=P)),
              (bo_row[:], io["bo"].partition_broadcast(P)),
              (wr[:], io["router_w"].rearrange("(c p) o -> p c o", p=P)),
              (br_row[:], io["router_b"].partition_broadcast(P))]
    LOADS = 1 + 2 * HC
    SOFT = 6
    pairs = B // 2

    with nc.Block() as block:
        @block.sync
        def _(sp):
            for dst, src in consts:
                sp.dma_start(dst, src).then_inc(const_in, 16)

            def load(n, u):
                sp.dma_start(h_in[:, u], d_h[n].rearrange("(t p) o -> p t o", p=P)).then_inc(batch_in[u], 16)
                for c in range(HC):
                    at = d_ctx[n, c * (NG // HC)]
                    heads = [CROW * S, NH // HC]
                    sp.dma_start(c_in[:, u, c], bass.AP(at.tensor, at.offset, [heads, [S, HD], [1, S]])
                                 ).then_inc(batch_in[u], 16)
                    sp.dma_start(sums[:, u, c], bass.AP(at.tensor, at.offset + HD * S,
                                                        [heads, [0, HD], [1, S]])).then_inc(batch_in[u], 16)

            load(0, 0)
            load(1, 1)

            def body(i, last):
                for u in range(2):
                    n = 2 * i + u
                    if not last:
                        settled(sp, h_done, n + 1, passed)
                        load(n + 2, u)
                    settled(sp, h_done, n + 1, passed)
                    sp.dma_start(io["out"][n].rearrange("(t p) o -> p t o", p=P), h_new[:, u]
                                 ).then_inc(stored[u], 16)
                    settled(sp, xg_done, n + 1, passed)
                    sp.dma_start(d_xg.rearrange("(b t p) o -> b p t o", t=QT, p=P)[n], xg[:, u]
                                 ).then_inc(stored[u], 16)

            peeled(sp, pairs, body)
            for u in range(2):
                sp.wait_ge(stored[u], 32 * pairs)

        @block.gpsimd
        def _(pool):
            nc.gpsimd.memset(minus_half[:], -0.5).then_inc(half_set, 1)
            pool.wait_ge(half_set, 1)
            pool.wait_ge(const_in, 16 * len(consts))

            def body(i, last):
                for u in range(2):
                    n = 2 * i + u
                    after(pool, batch_in[u], 16 * LOADS * (i + 1))
                    nc.gpsimd.tensor_tensor(h_in[:, u], h_in[:, u],
                                            bo_row[:].unsqueeze(1).to_broadcast([P, QT, H]), ALU.add
                                            ).then_inc(h_added, 1)
                    after(pool, ve_done, n + 1)
                    nc.gpsimd.tensor_tensor(rstd[:], var_eps[:], minus_half[:], ALU.pow).then_inc(rs_done, 1)

            peeled(pool, pairs, body)

        @block.tensor
        def _(pe):
            def project_out(n):
                after(pe, scaled, n + 1)
                after(pe, h_done, n)
                for t in range(QT):
                    for c in range(HC):
                        mm = pe.matmul(m_o[:, t], ctxn[:, c, t * P:(t + 1) * P], wo[:, c], start=(c == 0),
                                       stop=(c == HC - 1))
                mm.then_inc(o_done, 1)

            def turn(n, u):
                after(pe, xn_done, n + 1)
                after(pe, turnA, n)
                after(pe, turnD, n)
                for c in range(HC):
                    for t in range(QT):
                        mm = pe.transpose(m_turn[:, c, t * P:(t + 1) * P], xg[:, u, t, c * P:(c + 1) * P],
                                          ident[:])
                    mm.then_inc(turn_done, 1)

            def route(n):
                after(pe, turnA, n + 1)
                after(pe, turnD, n + 1)
                after(pe, soft, SOFT * n)
                for t in range(QT):
                    for c in range(HC):
                        mm = pe.matmul(m_r[:, t], xT[:, c, t * P:(t + 1) * P], wr[:, c], start=(c == 0),
                                       stop=(c == HC - 1))
                mm.then_inc(r_done, 1)

            pe.wait_ge(const_in, 16 * len(consts))
            project_out(0)

            def body(i, last):
                for u in range(2):
                    n = 2 * i + u
                    turn(n, u)
                    if not (last and u == 1):
                        project_out(n + 1)
                    route(n)

            peeled(pe, pairs, body)

        @block.scalar
        def _(act):
            def body(i, last):
                for u in range(2):
                    n = 2 * i + u
                    after(act, turn_done, HC * n + 1)
                    after(act, r_done, n)
                    nc.scalar.activation(xT[:, 0], m_turn[:, 0], ACT.Identity).then_inc(turnA, 1)
                    after(act, soft, SOFT * n + 3)
                    nc.scalar.activation(expd[:], logits[:], ACT.Exp).then_inc(exp_done, 1)

            peeled(act, pairs, body)

        @block.vector
        def _(dve):
            dve.wait_ge(const_in, 16 * len(consts))

            def scale_context(n, i, u):
                after(dve, batch_in[u], 16 * LOADS * (i + 1))
                after(dve, o_done, n)
                nc.vector.reciprocal(sums[:, u], sums[:, u]).then_inc(scale_step, 1)
                after(dve, scale_step, n + 1)
                nc.vector.tensor_tensor(ctxn[:], c_in[:, u], sums[:, u], ALU.mult).then_inc(scaled, 1)

            def norm(n, i, u):
                after(dve, o_done, n + 1)
                after(dve, h_added, n + 1)
                after(dve, stored[u], 32 * i)
                nc.vector.tensor_tensor(h_new[:, u], m_o[:], h_in[:, u], ALU.add).then_inc(h_done, 1)
                after(dve, h_done, n + 1)
                for t in range(QT):
                    nc.vector.bn_stats(stats[:, t], h_new[:, u, t]).then_inc(st_done, 1)
                settled(dve, st_done, QT * (n + 1), passed)
                for t in range(QT):
                    nc.vector.bn_aggr(moments[:, t], stats[:, t]).then_inc(mo_done, 1)
                after(dve, mo_done, QT * (n + 1))
                nc.vector.tensor_scalar_add(var_eps[:], moments[:, :, 1], EPS).then_inc(ve_done, 1)
                after(dve, rs_done, n + 1)
                for t in range(QT):
                    ins = nc.vector.tensor_scalar(xg[:, u, t, 0:H], h_new[:, u, t], moments[:, t, 0:1],
                                                  rstd[:, t:t + 1], ALU.subtract, ALU.mult)
                ins.then_inc(xn_done, 1)

            def soft_scores(n, u):
                def step(ins, k):
                    ins.then_inc(soft, 1)
                    after(dve, soft, SOFT * n + k)

                after(dve, turn_done, HC * n + 2)
                after(dve, r_done, n)
                nc.vector.tensor_copy(xT[:, 1], m_turn[:, 1]).then_inc(turnD, 1)
                after(dve, r_done, n + 1)
                step(nc.vector.tensor_tensor(logits[:], m_r[:], br_row[:].unsqueeze(1).to_broadcast([P, QT, NE]),
                                             ALU.add), 1)
                step(nc.vector.tensor_reduce(top_of[:], logits[:], AX.X, ALU.max), 2)
                step(nc.vector.tensor_tensor(logits[:], logits[:], top_of[:].unsqueeze(2).to_broadcast([P, QT, NE]),
                                             ALU.subtract), 3)
                after(dve, exp_done, n + 1)
                step(nc.vector.tensor_reduce(total[:], expd[:], AX.X, ALU.add), 4)
                step(nc.vector.reciprocal(share[:], total[:]), 5)
                nc.vector.tensor_tensor(xg[:, u, :, H:], expd[:], share[:].unsqueeze(2).to_broadcast([P, QT, NE]),
                                        ALU.mult).then_inc(xg_done, 1)
                step(nc.vector.tensor_tensor(scores[:, :, bass.ts(n, QT)].rearrange("p e t -> p t e"), expd[:],
                                             share[:].unsqueeze(2).to_broadcast([P, QT, NE]), ALU.mult), 6)

            scale_context(0, 0, 0)

            def body(i, last):
                for u in range(2):
                    n = 2 * i + u
                    norm(n, i, u)
                    if not (last and u == 1):
                        scale_context(n + 1, i + u, 1 - u)
                    soft_scores(n, u)

            peeled(dve, pairs, body)


def choose(nc, io, NT, ctx, sem, passed, scores, chosen):
    def sb(name, shape, dt=F32):
        return ctx.enter_context(nc.sbuf_tensor("c_" + name, shape, dt))

    def ps(name, shape):
        return ctx.enter_context(nc.psum_tensor("c_ps_" + name, shape, F32))

    ET = NE * NT
    before = sb("before", [P, P], BF16)
    ones = sb("ones", [P, P], BF16)
    before_f, iota, place = sb("before_f", [P, P]), sb("iota", [P, P]), sb("place", [P, 2, NT])
    restart = sb("restart", [P, NE, NT])
    least, trial, bit = sb("least", [P, NE], I32), sb("trial", [P, NE], I32), sb("bit", [P, NE], I32)
    enough, held = sb("enough", [P, NE], I32), sb("held", [P, NE])
    held_b = sb("held_b", [P, 2, NE], BF16)
    mask = sb("mask", [P, NE, NT], BF16)
    above, equal = sb("above", [P, NE, NT]), sb("equal", [P, NE, NT])
    run, rank, sel = sb("run", [P, NE, NT]), sb("rank", [P, NE, NT]), sb("sel", [P, NE, NT])
    room = sb("room", [P, NE])
    quarter = sb("quarter", [P, CT, NE, NT])
    what = sb("what", [P, NE, NT, 2 * CT], BF16)
    TG = 16 if NT % 16 == 0 else NT
    hot = sb("hot", [P, 2, TG, P], BF16)
    index = sb("index", [P, NE, CT])
    m_count = ps("m_count", [P, NE])
    GB = min(ET, S)
    m_below, m_all = ps("m_below", [P, ET // GB, GB]), ps("m_all", [P, ET // GB, GB])
    m_list = ps("m_list", [P, NE, 2 * CT])
    c_in, c_dve, c_pe, c_hot, c_listed = (sem("c_" + n) for n in ("in", "dve", "pe", "hot", "listed"))
    wide = lambda ap: ap.unsqueeze(2).to_broadcast([P, NE, NT])
    ROUND = 7
    START = 4

    with nc.Block() as block:
        @block.sync
        def _(sp):
            for dst, src in ((before_f, io["before"]), (iota, io["iota"]), (place, io["place"])):
                sp.dma_start(dst[:], src).then_inc(c_in, 16)

        @block.tensor
        def _(pe):
            pe.wait_ge(c_dve, START)

            with pe.Fori(0, BITS, 1) as r:
                after(pe, c_dve, START + ROUND * r + 4)
                for k in range(2):
                    mm = pe.matmul(m_count[:], ones[:], held_b[:, k], start=(k == 0), stop=(k == 1))
                mm.then_inc(c_pe, 1)
            base = START + ROUND * BITS
            pe.wait_ge(c_dve, base + 4)
            for k in range(2):
                mm = pe.matmul(m_count[:], ones[:], held_b[:, k], start=(k == 0), stop=(k == 1))
            mm.then_inc(c_pe, 1)
            for stage, ready in ((0, base + 6), (1, base + 13)):
                pe.wait_ge(c_dve, ready)
                flat = mask[:].rearrange("p e t -> p (e t)")
                for g in range(ET // GB):
                    pe.matmul(m_below[:, g], before[:], flat[:, g * GB:(g + 1) * GB], start=True, stop=True)
                    mm = pe.matmul(m_all[:, g], ones[:], flat[:, g * GB:(g + 1) * GB], start=True, stop=True)
                mm.then_inc(c_pe, 1)
            for e in range(NE):
                for g in range(NT // TG):
                    k = e * (NT // TG) + g
                    pe.wait_ge(c_hot, k + 1)
                    for t in range(TG):
                        at = g * TG + t
                        mm = pe.matmul(m_list[:, e], hot[:, k % 2, t], what[:, e, at], start=(at == 0),
                                       stop=(at == NT - 1), skip_group_check=True)
                    mm.then_inc(c_listed, 1)

        @block.vector
        def _(dve):
            count = [0]

            def step(ins):
                count[0] += 1
                ins.then_inc(c_dve, 1)
                dve.wait_ge(c_dve, count[0])

            dve.wait_ge(c_in, 48)
            nc.vector.memset(least[:], 0)
            nc.vector.memset(bit[:], 1 << (BITS - 1))
            step(nc.vector.memset(ones[:], 1.0))
            step(nc.vector.tensor_copy(before[:], before_f[:]))
            nc.vector.memset(restart[:], 1.0)
            step(nc.vector.memset(rank[:], 0.0))
            step(nc.vector.memset(restart[:, :, 0:1], 0.0))

            with dve.Fori(0, BITS, 1) as r:
                def chain(ins, k):
                    ins.then_inc(c_dve, 1)
                    settled(dve, c_dve, START + ROUND * r + k, passed)

                chain(nc.vector.tensor_tensor(trial[:], least[:], bit[:], ALU.bitwise_or), 1)
                chain(nc.vector.tensor_tensor(above[:], scores[:], wide(trial[:].bitcast(F32)), ALU.is_ge), 2)
                chain(nc.vector.tensor_reduce(held[:], above[:], AX.X, ALU.add), 3)
                nc.vector.memset(held_b[:, 1], 0.0)
                chain(nc.vector.tensor_copy(held_b[:, 0], held[:]), 4)
                after(dve, c_pe, r + 1)
                chain(nc.vector.tensor_scalar(enough[:], m_count[:], float(TOPK), None, ALU.is_ge), 5)
                chain(nc.vector.copy_predicated(least[:], enough[:], trial[:]), 6)
                chain(nc.vector.tensor_scalar(bit[:], bit[:], 1, None, ALU.logical_shift_right), 7)
            count[0] = START + ROUND * BITS
            floor = wide(least[:].bitcast(F32))
            step(nc.vector.tensor_tensor(above[:], scores[:], floor, ALU.is_gt))
            step(nc.vector.tensor_tensor(equal[:], scores[:], floor, ALU.is_equal))
            step(nc.vector.tensor_reduce(held[:], above[:], AX.X, ALU.add))
            step(nc.vector.tensor_copy(held_b[:, 0], held[:]))
            dve.wait_ge(c_pe, BITS + 1)
            step(nc.vector.tensor_scalar(room[:], m_count[:], -1.0, float(TOPK), ALU.mult, ALU.add))
            step(nc.vector.tensor_copy(mask[:], equal[:]))

            def ranks():
                below = m_below[:].rearrange("p g x -> p (g x)")
                every = m_all[:].rearrange("p g x -> p (g x)")
                flat = lambda x: x[:].rearrange("p e t -> p (e t)")
                step(nc.vector.tensor_copy(flat(run), every))
                step(nc.vector.tensor_tensor_scan(flat(rank), flat(restart), flat(run), 0.0, ALU.mult, ALU.add))
                step(nc.vector.tensor_tensor(flat(rank), flat(rank), flat(run), ALU.subtract))
                step(nc.vector.tensor_tensor(flat(rank), flat(rank), below, ALU.add))

            dve.wait_ge(c_pe, BITS + 2)
            ranks()
            step(nc.vector.tensor_tensor(sel[:], rank[:], wide(room[:]), ALU.is_lt))
            step(nc.vector.tensor_tensor(sel[:], sel[:], equal[:], ALU.mult))
            step(nc.vector.tensor_tensor(mask[:], sel[:], above[:], ALU.add))
            dve.wait_ge(c_pe, BITS + 3)
            ranks()
            step(nc.vector.tensor_tensor(sel[:], sel[:], above[:], ALU.add))
            step(nc.vector.tensor_scalar_add(rank[:], rank[:], 1.0))
            step(nc.vector.tensor_tensor(rank[:], rank[:], sel[:], ALU.mult))
            step(nc.vector.tensor_scalar_add(rank[:], rank[:], -1.0))
            for c in range(1, CT):
                ins = nc.vector.tensor_scalar(quarter[:, c], rank[:], float(c * P), None, ALU.is_ge)
            step(ins)
            for c in range(1, CT):
                step(nc.vector.scalar_tensor_tensor(rank[:], quarter[:, c], -float(P), rank[:], ALU.mult, ALU.add))
            step(nc.vector.tensor_copy(quarter[:, 0], sel[:]))
            for c in range(CT - 1):
                step(nc.vector.tensor_tensor(quarter[:, c], quarter[:, c], quarter[:, c + 1], ALU.subtract))
            for c in range(CT):
                for k in range(2):
                    ins = nc.vector.tensor_tensor(what[:, :, :, 2 * c + k], quarter[:, c],
                                                  place[:, k].unsqueeze(1).to_broadcast([P, NE, NT]), ALU.mult)
            step(ins)
            for e in range(NE):
                for g in range(NT // TG):
                    k = e * (NT // TG) + g
                    if k >= 2:
                        dve.wait_ge(c_listed, k - 1)
                    nc.vector.tensor_tensor(
                        hot[:, k % 2], iota[:].unsqueeze(1).to_broadcast([P, TG, P]),
                        rank[:, e, g * TG:(g + 1) * TG].unsqueeze(2).to_broadcast([P, TG, P]),
                        ALU.is_equal).then_inc(c_hot, 1)
            dve.wait_ge(c_listed, NE * (NT // TG))
            pairs = m_list[:].rearrange("p e (c k) -> p e c k", k=2)
            step(nc.vector.tensor_copy(index[:], pairs[:, :, :, 1]))
            step(nc.vector.scalar_tensor_tensor(chosen[:], pairs[:, :, :, 0], float(P), index[:], ALU.mult, ALU.add))


def experts(nc, io, T, ctx, sem, passed, chosen, d_xg):
    def sb(name, shape, dt=F32):
        return ctx.enter_context(nc.sbuf_tensor("e_" + name, shape, dt))

    def ps(name, shape):
        return ctx.enter_context(nc.psum_tensor("e_ps_" + name, shape, F32))

    ident = sb("ident", [P, P])
    w1, w2 = sb("w1", [P, 2, HC, DFF]), sb("w2", [P, 2, FC, H])
    b1, b2 = sb("b1", [P, NE, FC]), sb("b2", [P, 2, H])
    index, gate = sb("index", [P, 2, CT], U32), sb("gate", [P, 2, CT])
    rows, rowsT = sb("rows", [P, 2, CT, XG]), sb("rowsT", [P, HC, TOPK])
    hidden = sb("hidden", [P, FC, TOPK])
    result = sb("result", [P, 2, CT, H])
    m_turn, m_1, m_2 = ps("m_turn", [P, HC, TOPK]), ps("m_1", [P, 2, TOPK]), ps("m_2", [P, 2, H * 2])
    const_in = sem("e_const_in")
    w_in = [sem(f"e_w_in{u}") for u in range(2)]
    rows_in = [sem(f"e_rows_in{u}") for u in range(2)]
    (picked, gated, turn_done, turnA, turnD, one_done, one_kept, two_done, two_kept, ready, added) = (
        sem("e_" + n) for n in ("picked", "gated", "turn_done", "turnA", "turnD", "one_done", "one_kept",
                                "two_done", "two_kept", "ready", "added"))
    out_rows = io["out"].rearrange("b s o -> (b s) o")
    W = 3

    with nc.Block() as block:
        @block.sync
        def _(sp):
            sp.dma_start(ident[:], io["ident"]).then_inc(const_in, 16)
            sp.dma_start(b1[:], io["b1T"]).then_inc(const_in, 16)

            def load(e, u):
                sp.dma_start(w1[:, u], io["w1"][e].rearrange("(c p) f -> p c f", p=P)).then_inc(w_in[u], 16)
                sp.dma_start(w2[:, u], io["w2"][e].rearrange("(c p) o -> p c o", p=P)).then_inc(w_in[u], 16)
                sp.dma_start(b2[:, u], io["b2"][e].partition_broadcast(P)).then_inc(w_in[u], 16)

            load(0, 0)
            load(1, 1)

            def body(i, last):
                for u in range(2):
                    if not last:
                        settled(sp, ready, CT * (2 * i + u + 1), passed)
                        load(2 * i + u + 2, u)

            peeled(sp, NE // 2, body)

        @block.gpsimd
        def _(pool):
            def gather(e, i, u):
                settled(pool, picked, e + 1, passed)
                for c in range(CT):
                    nc.gpsimd.indirect_dma_start(
                        out=rows[:, u, c], out_offset=None, in_=d_xg,
                        in_offset=bass.IndirectOffsetOnAxis(ap=index[:, u, c:c + 1], axis=0)
                    ).then_inc(rows_in[u], 16)

            def add_to_out(e, u):
                for c in range(CT):
                    settled(pool, ready, CT * e + c + 1, passed)
                    nc.gpsimd.indirect_dma_start(
                        out=out_rows, out_offset=bass.IndirectOffsetOnAxis(ap=index[:, u, c:c + 1], axis=0),
                        in_=result[:, u, c], in_offset=None, compute_op=ALU.add).then_inc(added, 16)
                settled(pool, added, 16 * CT * (e + 1), passed)

            gather(0, 0, 0)

            def body(i, last):
                gather(2 * i + 1, i, 1)
                add_to_out(2 * i, 0)
                if not last:
                    gather(2 * i + 2, i + 1, 0)
                add_to_out(2 * i + 1, 1)

            peeled(pool, NE // 2, body)

        @block.tensor
        def _(pe):
            pe.wait_ge(const_in, 32)

            def body(i, last):
                for u in range(2):
                    e = 2 * i + u
                    after(pe, rows_in[u], 16 * CT * (i + 1))
                    for c in range(HC):
                        for t in range(CT):
                            mm = pe.transpose(m_turn[:, c, t * P:(t + 1) * P], rows[:, u, t, c * P:(c + 1) * P],
                                              ident[:])
                        mm.then_inc(turn_done, 1)
                    after(pe, w_in[u], 16 * W * (i + 1))
                    after(pe, turnA, e + 1)
                    after(pe, turnD, e + 1)
                    for f in range(FC):
                        after(pe, one_kept, FC * e + f - 1)
                        for c in range(HC):
                            mm = pe.matmul(m_1[:, f % 2], w1[:, u, c, f * P:(f + 1) * P], rowsT[:, c],
                                           start=(c == 0), stop=(c == HC - 1))
                        mm.then_inc(one_done, 1)
                    after(pe, one_kept, FC * (e + 1))
                    for t in range(CT):
                        after(pe, two_kept, CT * e + t - 1)
                        for f in range(FC):
                            mm = pe.matmul(m_2[:, t % 2, 0:H], hidden[:, f, t * P:(t + 1) * P], w2[:, u, f],
                                           start=(f == 0), stop=(f == FC - 1))
                        mm.then_inc(two_done, 1)

            peeled(pe, NE // 2, body)

        @block.scalar
        def _(act):
            act.wait_ge(const_in, 32)

            def body(i, last):
                for u in range(2):
                    e = 2 * i + u
                    after(act, turn_done, HC * e + 1)
                    nc.scalar.activation(rowsT[:, 0], m_turn[:, 0], ACT.Identity).then_inc(turnA, 1)
                    after(act, two_done, CT * e)
                    for f in range(FC):
                        after(act, one_done, FC * e + f + 1)
                        nc.scalar.activation(hidden[:, f], m_1[:, f % 2], ACT.Relu,
                                             bias=b1[:, e, f:f + 1]).then_inc(one_kept, 1)

            body(0, False)
            for i in range(1, NE // 2):
                body(i, i == NE // 2 - 1)

        @block.vector
        def _(dve):
            def pick(e, u):
                if not (isinstance(e, int) and e < 2):
                    after(dve, added, 16 * CT * (e - 1))
                nc.vector.tensor_copy(index[:, u], chosen[:, e]).then_inc(picked, 1)

            def body(i, last):
                for u in range(2):
                    e = 2 * i + u
                    if not (last and u == 1):
                        pick(e + 1, 1 - u)
                    after(dve, turn_done, HC * e + 2)
                    nc.vector.tensor_copy(rowsT[:, 1], m_turn[:, 1]).then_inc(turnD, 1)
                    nc.vector.tensor_copy(gate[:, u], rows[:, u, :, H + e]).then_inc(gated, 1)
                    after(dve, gated, e + 1)
                    for t in range(CT):
                        after(dve, two_done, CT * e + t + 1)
                        nc.vector.tensor_tensor(result[:, u, t], m_2[:, t % 2, 0:H], b2[:, u], ALU.add
                                                ).then_inc(two_kept, 1)
                        after(dve, two_kept, CT * e + t + 1)
                        nc.vector.tensor_scalar(result[:, u, t], result[:, u, t], gate[:, u, t:t + 1], None,
                                                ALU.mult).then_inc(ready, 1)

            pick(0, 0)
            body(0, False)
            for i in range(1, NE // 2):
                body(i, i == NE // 2 - 1)
            dve.wait_ge(added, 16 * CT * NE)


def distances():
    d = np.arange(1 - S, S)
    mid, reach = SPAN // 2, NP
    a = np.abs(d).astype(np.float64)
    far = np.ceil(np.log(np.maximum(a, 1) / mid) / np.log((reach - 1) / mid) * (mid - 1) - 1e-6) + mid
    bucket = np.where(a <= mid, d, far * np.sign(d)).astype(np.int64)
    return np.clip(bucket + SPAN, 0, NP - 1)


def shape_constants(B):
    row = distances()
    low, high = row[0], row[-1]
    assert (row[:S - TLOW] == low).all() and (row[S - 1 + TLOW:] == high).all()
    pick = np.zeros((P, 2, TW), np.float32)
    for x in range(TW):
        d = x - TLOW
        for w, at in ((0, TW - 1 - x), (1, x)):
            pick[row[d + S - 1], w, at] += 1
            pick[low, w, at] -= 1
    ends = np.zeros((P, 2), np.float32)
    ends[low, 0] = ends[high, 1] = 1
    p = np.arange(P)
    own = np.zeros((P, HC, NH), np.float32)
    for c in range(HC):
        own[p, c, (c * P + p) // HD] = 1
    place = np.stack([np.broadcast_to(np.arange(B * QT, dtype=np.float32), (P, B * QT)),
                      np.broadcast_to(p[:, None].astype(np.float32), (P, B * QT))], 1)
    return {"pick": pick, "ends": ends, "own": own, "ident": np.eye(P, dtype=np.float32),
            "before": (p[:, None] < p[None, :]).astype(np.float32),
            "iota": np.ascontiguousarray(np.broadcast_to(p.astype(np.float32), (P, P))),
            "place": np.ascontiguousarray(place)}


def kernel(**inputs):
    import concourse.bacc as bacc
    from concourse.bass_utils import run_bass_kernel_spmd

    g = {k.replace("L0_", "").replace("attn_", "").replace("ffn_", ""): np.asarray(v) for k, v in inputs.items()}
    B = g["x"].shape[0]
    turn = np.ascontiguousarray
    arrays = {
        "xT": turn(g["x"].transpose(0, 3, 2, 1)),
        "tok_weight": turn(g["tok_weight"].T), "wsT": turn(g["tok_weighted_sum"].T),
        "bq_col": turn(g["bq"].reshape(HC, P).T), "bk_col": turn(g["bk"].reshape(HC, P).T),
        "b1T": turn(g["b1"].reshape(NE, FC, P).transpose(2, 0, 1)),
        **{k: turn(g[k]) for k in ("Wq", "Wk", "Wv", "Wo", "Wpk", "Wpq", "bv", "bo", "bpk", "bpq", "rel_emb",
                                   "ln_g", "ln_b", "router_w", "router_b", "w1", "w2", "b2")},
        **shape_constants(B),
    }
    nc = bacc.Bacc("TRN2", target_bir_lowering=False, num_devices=1)
    io = {k: nc.dram_tensor("in_" + k, a.shape, mybir.dt.from_np(a.dtype), kind="ExternalInput").ap()
          for k, a in arrays.items()}
    io["out"] = nc.dram_tensor("out", (B, S, H), F32, kind="ExternalOutput").ap()
    build(nc, io, B)
    result = run_bass_kernel_spmd(nc, [{"in_" + k: a for k, a in arrays.items()}], core_ids=[0])
    return result.results[0]["out"]
```

```python
from contextlib import ExitStack

import numpy as np
import concourse.bass as bass
from concourse import mybir

F32 = mybir.dt.float32
BF16 = mybir.dt.bfloat16
I32 = mybir.dt.int32
U32 = mybir.dt.uint32
ALU = mybir.AluOpType
ACT = mybir.ActivationFunctionType
AX = mybir.AxisListType

P = 128
S = 512
H = 256
ND = 4
NH = 16
HD = H // NH
QT = S // P
HC = H // P
SPAN = 64
NP = 2 * SPAN
DFF = 1024
NE = 8
TOPK = 512
FC = DFF // P
CT = TOPK // P
EPS = 1e-5
SCALE = float(1.0 / np.sqrt(np.float32(HD * 3)))

TLOW = P
TW = 2 * TLOW
PITCH = 4 * P
NEAR = 3 * P
AHEAD = 4
SLOTS = 6
SIDE_A = (0, 0, 1, 0, 2, 1)
SIDE_B = (0, 1, 0, 2, 0, 1)
ST = SLOTS * HD
KW = 2 * S + S // 2
SW = S + KW
RING = 4
LEAD = 3
GH = 4
NG = NH // GH
CROW = 32
XG = H + NE
BITS = 30


def after(eng, sem, count):
    if not isinstance(count, int) or count > 0:
        eng.wait_ge(sem, count)


def settled(eng, sem, count, passed):
    after(eng, sem, count)
    if not isinstance(count, int):
        eng.sem_inc(passed, 1)


def peeled(eng, steps, body):
    body(0, steps == 1)
    if steps > 2:
        with eng.Fori(1, steps - 1, 1) as i:
            body(i, False)
    if steps > 1:
        body(steps - 1, True)


def build(nc, io, B):
    T = B * S
    NT = T // P
    with ExitStack() as top:
        def sem(name):
            return top.enter_context(nc.semaphore(name))

        def dram(name, shape, dt=F32):
            return nc.dram_tensor(name, shape, dt).ap()

        passed = sem("passed")
        d_tab = dram("d_tab", (2, 3, H, TW), BF16)
        d_stack = dram("d_stack", (B, SLOTS, H, SW), BF16)
        d_kterm = dram("d_kterm", (B, 3, NH, S + S // 2), BF16)
        d_v = dram("d_v", (B, S, NH * CROW))
        d_h = dram("d_h", (B, S, H))
        d_skew = dram("d_skew", (RING, 2, QT, P, PITCH))
        d_ctx = dram("d_ctx", (B, NG, P, S))
        d_xg = dram("d_xg", (T, XG))

        with ExitStack() as ctx:
            project(nc, io, B, ctx, sem, passed, d_tab, d_stack, d_kterm, d_v, d_h)
        with ExitStack() as ctx:
            attend(nc, io, B, ctx, sem, passed, d_tab, d_stack, d_kterm, d_v, d_skew, d_ctx)
        with ExitStack() as ctx:
            scores = ctx.enter_context(nc.sbuf_tensor("scores", [P, NE, NT], F32))
            with ExitStack() as inner:
                output(nc, io, B, inner, sem, passed, scores, d_h, d_ctx, d_xg)
            chosen = ctx.enter_context(nc.sbuf_tensor("chosen", [P, NE, CT], U32))
            with ExitStack() as inner:
                choose(nc, io, NT, inner, sem, passed, scores, chosen)
            with ExitStack() as inner:
                experts(nc, io, T, inner, sem, passed, chosen, d_xg)


def project(nc, io, B, ctx, sem, passed, d_tab, d_stack, d_kterm, d_v, d_h):
    def sb(name, shape, dt=F32):
        return ctx.enter_context(nc.sbuf_tensor("p_" + name, shape, dt))

    def ps(name, shape):
        return ctx.enter_context(nc.psum_tensor("p_ps_" + name, shape, F32))

    mix = sb("mix", [P, ND * HC, H])
    ident = sb("ident", [P, P])
    wq, wk, wv = (sb(n, [P, HC, H]) for n in ("wq", "wk", "wv"))
    bv_row = sb("bv_row", [P, H])
    qk_bias = sb("qk_bias", [P, 4, HC])
    kterm_w = sb("kterm_w", [P, HC, 2 * NH])
    minus_half = sb("minus_half", [P, QT])

    with ExitStack() as tctx:
        def tsb(name, shape, dt=F32):
            return tctx.enter_context(nc.sbuf_tensor("t_" + name, shape, dt))

        def tps(name, shape):
            return tctx.enter_context(nc.psum_tensor("t_ps_" + name, shape, F32))

        ws = tsb("ws", [P, HC, H])
        wd = tsb("wd", [P, ND, H])
        rel = tsb("rel", [P, H])
        lng, lnb = tsb("lng", [P, H]), tsb("lnb", [P, H])
        wp = tsb("wp", [P, 2, HC, H])
        bp = tsb("bp", [P, 2, H])
        pick = tsb("pick", [P, 2, TW])
        ends = tsb("ends", [P, 2])
        own = tsb("own", [P, HC, NH])
        stats, moments = tsb("stats", [P, 6]), tsb("moments", [P, 2])
        rstd, relT, pos = tsb("rstd", [P, 2]), tsb("relT", [P, HC, P]), tsb("pos", [P, 2, H])
        rest = tsb("rest", [P, 2, HC, TW])
        parts = tsb("parts", [P, 2, HC, 3, TW], BF16)
        consts = tsb("consts", [P, 2, HC, 2])
        t_turn = tps("turn", [P, S])
        t_pos = tps("pos", [P, 2, H])
        t_tab = tps("tab", [P, 2 * HC, S])
        t_end = tps("end", [P, 2, HC, 2])
        t_in, t_const, t_dve, t_pe, t_pool, t_out = (
            sem("t_" + n) for n in ("in", "const", "dve", "pe", "pool", "out"))
        loads = [
            (ws, io["wsT"].rearrange("(c p) o -> p c o", p=P)),
            (wd, io["tok_weight"].partition_broadcast(P)),
            (rel, io["rel_emb"]), (lng, io["ln_g"].partition_broadcast(P)),
            (lnb, io["ln_b"].partition_broadcast(P)),
            (wp[:, 0], io["Wpk"].rearrange("(c p) o -> p c o", p=P)),
            (wp[:, 1], io["Wpq"].rearrange("(c p) o -> p c o", p=P)),
            (bp[:, 0], io["bpk"].partition_broadcast(P)),
            (bp[:, 1], io["bpq"].partition_broadcast(P)),
            (pick, io["pick"]), (ends, io["ends"]), (own, io["own"]), (ident, io["ident"]),
            (wq, io["Wq"].rearrange("(c p) o -> p c o", p=P)),
            (wk, io["Wk"].rearrange("(c p) o -> p c o", p=P)),
            (wv, io["Wv"].rearrange("(c p) o -> p c o", p=P)),
            (bv_row, io["bv"].partition_broadcast(P)),
            (qk_bias[:, 0], io["bq_col"]), (qk_bias[:, 1], io["bk_col"]),
        ]
        with nc.Block() as block:
            @block.sync
            def _(sp):
                for dst, src in loads:
                    sp.dma_start(dst[:], src).then_inc(t_in, 16)
                sp.wait_ge(t_dve, 18)
                for w in range(2):
                    for c in range(HC):
                        sp.dma_start(d_tab[w, :, c * P:(c + 1) * P, :].rearrange("t p x -> p t x"),
                                     parts[:, w, c]).then_inc(t_out, 16)
                sp.wait_ge(t_out, 16 * 2 * HC)

            @block.gpsimd
            def _(pool):
                nc.gpsimd.memset(minus_half[:], -0.5).then_inc(t_const, 1)
                pool.wait_ge(t_const, 1)
                pool.wait_ge(t_dve, 3)
                nc.gpsimd.tensor_tensor(rstd[:, 1:2], rstd[:, 0:1], minus_half[:, 0:1],
                                        ALU.pow).then_inc(t_pool, 1)

            @block.vector
            def _(dve):
                done = [0]

                def step(ins, wait=True):
                    done[0] += 1
                    ins.then_inc(t_dve, 1)
                    if wait:
                        dve.wait_ge(t_dve, done[0])

                dve.wait_ge(t_in, 16 * len(loads))
                step(nc.vector.bn_stats(stats[:], rel[:]))
                step(nc.vector.bn_aggr(moments[:], stats[:]))
                step(nc.vector.tensor_scalar_add(rstd[:, 0:1], moments[:, 1:2], EPS))
                for d in range(ND):
                    for c in range(HC):
                        nc.vector.tensor_tensor(mix[:, d * HC + c], ws[:, c], wd[:, d], ALU.mult)
                dve.wait_ge(t_pool, 1)
                step(nc.vector.tensor_scalar(rel[:], rel[:], moments[:, 0:1], rstd[:, 1:2],
                                             ALU.subtract, ALU.mult))
                step(nc.vector.tensor_tensor(rel[:], rel[:], lng[:], ALU.mult))
                step(nc.vector.tensor_tensor(rel[:], rel[:], lnb[:], ALU.add))
                dve.wait_ge(t_pe, 1)
                step(nc.vector.tensor_copy(relT[:], t_turn[:, 0:HC * P].rearrange(
                    "p (c q) -> p c q", c=HC)))
                dve.wait_ge(t_pe, 2)
                step(nc.vector.tensor_tensor(pos[:], t_pos[:], bp[:], ALU.add))
                dve.wait_ge(t_pe, 3)
                step(nc.vector.tensor_copy(consts[:], t_end[:]))
                tab = t_tab[:, :, 0:TW].rearrange("p (w c) x -> p w c x", w=2)
                step(nc.vector.tensor_copy(parts[:, :, :, 0], tab))
                step(nc.vector.tensor_tensor(rest[:], tab, parts[:, :, :, 0], ALU.subtract))
                step(nc.vector.tensor_copy(parts[:, :, :, 1], rest[:]))
                step(nc.vector.tensor_tensor(rest[:], rest[:], parts[:, :, :, 1], ALU.subtract))
                step(nc.vector.tensor_copy(parts[:, :, :, 2], rest[:]))
                for side in range(2):
                    step(nc.vector.tensor_tensor(qk_bias[:, 2 + side], qk_bias[:, 1],
                                                 consts[:, 0, :, side], ALU.add))
                for c in range(HC):
                    for side in range(2):
                        ins = nc.vector.tensor_scalar(
                            kterm_w[:, c, side * NH:(side + 1) * NH], own[:, c],
                            consts[:, 1, c, side:side + 1], None, ALU.mult)
                step(ins)
                step(nc.vector.tensor_copy(rstd[:, 0:1], rstd[:, 1:2]))

            @block.tensor
            def _(pe):
                pe.wait_ge(t_dve, 6)
                for c in range(HC):
                    mm = pe.transpose(t_turn[:, c * P:(c + 1) * P], rel[:, c * P:(c + 1) * P], ident[:])
                mm.then_inc(t_pe, 1)
                pe.wait_ge(t_dve, 7)
                for w in range(2):
                    for c in range(HC):
                        mm = pe.matmul(t_pos[:, w], relT[:, c], wp[:, w, c], start=(c == 0),
                                       stop=(c == HC - 1))
                mm.then_inc(t_pe, 1)
                pe.wait_ge(t_dve, 8)
                for w in range(2):
                    for c in range(HC):
                        of = pos[:, w, c * P:(c + 1) * P]
                        pe.matmul(t_end[:, w, c], of, ends[:], start=True, stop=True)
                        mm = pe.matmul(t_tab[:, w * HC + c, 0:TW], of, pick[:, w], start=True, stop=True)
                mm.then_inc(t_pe, 1)

    xt = sb("xt", [P, 2, ND * HC, S])
    h_sb = sb("h_sb", [P, 2, QT, H])
    stats = sb("stats", [P, QT, 6])
    moments = sb("moments", [P, QT, 2])
    var_eps, rstd = sb("var_eps", [P, QT]), sb("rstd", [P, QT])
    xn = sb("xn", [P, QT, H])
    xnT = sb("xnT", [P, HC, S])
    full_q = sb("full_q", [P, HC, S])
    full_k = sb("full_k", [P, HC, KW])
    part_q = sb("part_q", [P, 2, 3, HC, S], BF16)
    part_k = sb("part_k", [P, 2, 3, HC, KW], BF16)
    full_t = sb("full_t", [2 * NH, S])
    part_t = sb("part_t", [2 * NH, 3, S], BF16)
    v_sb = sb("v_sb", [P, QT, NH, CROW])
    m_h = ps("m_h", [P, QT, H])
    m_turn = ps("m_turn", [P, HC, S])
    m_qk = ps("m_qk", [P, 2, S])
    m_v = ps("m_v", [P, 2, H])
    m_t = ps("m_t", [2 * NH, S])
    x_in = [sem(f"p_x_in{u}") for u in range(2)]
    (h_done, h_kept, st_done, mo_done, ve_done, rs_done, xn_done, turn_done, turnA, turnD,
     qk_done, qk_kept, t_done, t_kept, low_done, mid_done, parts_done, v_done, v_kept,
     v_const) = (sem("p_" + n) for n in (
         "h_done", "h_kept", "st_done", "mo_done", "ve_done", "rs_done", "xn_done", "turn_done",
         "turnA", "turnD", "qk_done", "qk_kept", "t_done", "t_kept", "low_done", "mid_done",
         "parts_done", "v_done", "v_kept", "v_const"))
    h_out = [sem(f"p_h_out{u}") for u in range(2)]
    v_out, t_out = sem("p_v_out"), sem("p_t_out")
    parts_out = [sem(f"p_parts_out{u}") for u in range(2)]
    DMAS = 2 * SLOTS
    CH = 2 * HC
    xT = io["xT"]
    pairs = B // 2

    with nc.Block() as block:
        @block.sync
        def _(sp):
            for u in range(2):
                sp.dma_start(xt[:, u], xT[u].rearrange("d (c p) s -> p (d c) s", p=P)).then_inc(x_in[u], 16)

            def body(i, last):
                for u in range(2):
                    n = 2 * i + u
                    if not last:
                        settled(sp, h_done, 2 * (n + 1), passed)
                        sp.dma_start(xt[:, u], xT[n + 2].rearrange("d (c p) s -> p (d c) s", p=P)
                                     ).then_inc(x_in[u], 16)
                    settled(sp, h_kept, 2 * (n + 1), passed)
                    sp.dma_start(d_h[n].rearrange("(t p) o -> p t o", p=P), h_sb[:, u]).then_inc(h_out[u], 16)
                    settled(sp, v_kept, 2 * (n + 1), passed)
                    sp.dma_start(d_v[n].rearrange("(t p) o -> p t o", p=P),
                                 v_sb[:].rearrange("p t h r -> p t (h r)")).then_inc(v_out, 16)
                    settled(sp, parts_done, (CH + 1) * (n + 1), passed)
                    for j in range(SLOTS):
                        to = d_stack[n, j].rearrange("(c p) x -> p c x", p=P)
                        sp.dma_start(to[:, :, 0:S], part_q[:, u, SIDE_A[j]]).then_inc(parts_out[u], 16)
                        sp.dma_start(to[:, :, S:SW], part_k[:, u, SIDE_B[j]]).then_inc(parts_out[u], 16)
                    to = d_kterm[n].rearrange("t h x -> h t x")
                    sp.dma_start(to[:, :, 0:S], part_t[0:NH]).then_inc(t_out, 16)
                    sp.dma_start(to[:, :, S:], part_t[NH:, :, 0:S // 2]).then_inc(t_out, 16)

            peeled(sp, pairs, body)
            sp.wait_ge(v_out, 16 * B)
            sp.wait_ge(t_out, 32 * B)
            for u in range(2):
                sp.wait_ge(parts_out[u], 16 * DMAS * pairs)
                sp.wait_ge(h_out[u], 16 * pairs)

        @block.tensor
        def _(pe):
            def mixing(n, i, u):
                after(pe, x_in[u], 16 * (i + 1))
                for t in range(QT):
                    if t % 2 == 0:
                        after(pe, h_kept, 2 * (n - 1) + t // 2 + 1 if not isinstance(n, int) or n else 0)
                    for k in range(ND * HC):
                        mm = pe.matmul(m_h[:, t], xt[:, u, k, t * P:(t + 1) * P], mix[:, k],
                                       start=(k == 0), stop=(k == ND * HC - 1))
                    if t % 2:
                        mm.then_inc(h_done, 1)

            def projections(n):
                after(pe, xn_done, n + 1)
                after(pe, turnA, n)
                after(pe, turnD, n)
                for c in range(HC):
                    for t in range(QT):
                        mm = pe.transpose(m_turn[:, c, t * P:(t + 1) * P], xn[:, t, c * P:(c + 1) * P], ident[:])
                    mm.then_inc(turn_done, 1)
                after(pe, turnA, n + 1)
                after(pe, turnD, n + 1)
                for m in range(CH):
                    after(pe, qk_kept, CH * n + m - 1)
                    w = (wq, wk)[m // HC]
                    for c in range(HC):
                        mm = pe.matmul(m_qk[:, m % 2], w[:, c, (m % HC) * P:(m % HC + 1) * P], xnT[:, c],
                                       start=(c == 0), stop=(c == HC - 1))
                    mm.then_inc(qk_done, 1)
                for half in range(2):
                    after(pe, v_kept, 2 * n + half)
                    for t in range(2):
                        at = (2 * half + t) * P
                        for c in range(HC):
                            mm = pe.matmul(m_v[:, t], xnT[:, c, at:at + P], wv[:, c], start=(c == 0),
                                           stop=(c == HC - 1))
                    mm.then_inc(v_done, 1)
                after(pe, qk_kept, CH * (n + 1))
                after(pe, t_kept, n)
                for c in range(HC):
                    mm = pe.matmul(m_t[:], kterm_w[:, c], full_k[:, c, 0:S], start=(c == 0), stop=(c == HC - 1))
                mm.then_inc(t_done, 1)

            mixing(0, 0, 0)

            def body(i, last):
                mixing(2 * i + 1, i, 1)
                projections(2 * i)
                if not last:
                    mixing(2 * i + 2, i + 1, 0)
                projections(2 * i + 1)

            peeled(pe, pairs, body)

        @block.scalar
        def _(act):
            def keep_h(n, i, u):
                if not (isinstance(n, int) and n < 2):
                    after(act, h_out[u], 16 * i)
                    after(act, xn_done, n - 1)
                for half in range(2):
                    after(act, h_done, 2 * n + half + 1)
                    nc.scalar.activation(h_sb[:, u, 2 * half:2 * half + 2], m_h[:, 2 * half:2 * half + 2],
                                         ACT.Identity).then_inc(h_kept, 1)

            def keep_qk(n, i, u):
                after(act, turn_done, HC * n + 1)
                nc.scalar.activation(xnT[:, 0], m_turn[:, 0], ACT.Identity).then_inc(turnA, 1)
                after(act, parts_out[u], 16 * DMAS * i)
                for m in range(CH):
                    c = m % HC
                    after(act, qk_done, CH * n + m + 1)
                    after(act, parts_done, (CH + 1) * (n - 1) + m + 1 if not isinstance(n, int) or n else 0)
                    src = m_qk[:, m % 2]
                    if m < HC:
                        nc.scalar.activation(full_q[:, c], src, ACT.Identity, bias=qk_bias[:, 0, c:c + 1])
                        ins = nc.scalar.activation(part_q[:, u, 0, c], src, ACT.Identity,
                                                   bias=qk_bias[:, 0, c:c + 1])
                    else:
                        for out in (full_k[:, c], part_k[:, u, 0, c]):
                            nc.scalar.activation(out[:, 0:S], src, ACT.Identity, bias=qk_bias[:, 1, c:c + 1])
                            nc.scalar.activation(out[:, S:2 * S], src, ACT.Identity,
                                                 bias=qk_bias[:, 2, c:c + 1])
                            ins = nc.scalar.activation(out[:, 2 * S:], src[:, 0:S // 2], ACT.Identity,
                                                       bias=qk_bias[:, 3, c:c + 1])
                    ins.then_inc(qk_kept, 1)
                after(act, t_done, n + 1)
                after(act, parts_done, (CH + 1) * n)
                after(act, t_out, 32 * n)
                nc.scalar.activation(full_t[:], m_t[:], ACT.Identity)
                nc.scalar.activation(part_t[:, 0], m_t[:], ACT.Identity).then_inc(t_kept, 1)

            keep_h(0, 0, 0)

            def body(i, last):
                keep_h(2 * i + 1, i, 1)
                keep_qk(2 * i, i, 0)
                if not last:
                    keep_h(2 * i + 2, i + 1, 0)
                keep_qk(2 * i + 1, i, 1)

            peeled(act, pairs, body)

        @block.gpsimd
        def _(pool):
            nc.gpsimd.memset(v_sb[:], 0.0).then_inc(v_const, 1)
            pool.wait_ge(v_const, 1)
            nc.gpsimd.memset(v_sb[:, :, :, HD:HD + 1], 1.0).then_inc(v_const, 1)

            def power(n):
                after(pool, ve_done, n + 1)
                nc.gpsimd.tensor_tensor(rstd[:], var_eps[:], minus_half[:], ALU.pow).then_inc(rs_done, 1)

            def lower(n, i, u):
                for m in range(CH):
                    c = m % HC
                    after(pool, qk_kept, CH * n + m + 1)
                    if m == HC:
                        after(pool, t_done, n + 1)
                    a, p = (full_q[:, c], part_q[:, u, 0, c]) if m < HC else (full_k[:, c], part_k[:, u, 0, c])
                    nc.gpsimd.tensor_tensor(a, a, p, ALU.subtract).then_inc(low_done, 1)
                after(pool, t_kept, n + 1)
                nc.gpsimd.tensor_tensor(full_t[:], full_t[:], part_t[:, 0], ALU.subtract).then_inc(low_done, 1)

            power(0)

            def body(i, last):
                power(2 * i + 1)
                lower(2 * i, i, 0)
                if not last:
                    power(2 * i + 2)
                lower(2 * i + 1, i, 1)

            peeled(pool, pairs, body)

        @block.vector
        def _(dve):
            def norm(n, u):
                for t in range(QT):
                    after(dve, h_kept, 2 * n + t // 2 + 1)
                    nc.vector.bn_stats(stats[:, t], h_sb[:, u, t]).then_inc(st_done, 1)
                settled(dve, st_done, QT * (n + 1), passed)
                for t in range(QT):
                    nc.vector.bn_aggr(moments[:, t], stats[:, t]).then_inc(mo_done, 1)
                after(dve, mo_done, QT * (n + 1))
                nc.vector.tensor_scalar_add(var_eps[:], moments[:, :, 1], EPS).then_inc(ve_done, 1)
                after(dve, rs_done, n + 1)
                after(dve, turn_done, HC * n)
                for t in range(QT):
                    ins = nc.vector.tensor_scalar(xn[:, t], h_sb[:, u, t], moments[:, t, 0:1], rstd[:, t:t + 1],
                                                  ALU.subtract, ALU.mult)
                ins.then_inc(xn_done, 1)

            def split(n, i, u):
                after(dve, turn_done, HC * n + 2)
                nc.vector.tensor_copy(xnT[:, 1], m_turn[:, 1]).then_inc(turnD, 1)
                for half in range(2):
                    after(dve, v_done, 2 * n + half + 1)
                    if half == 0:
                        after(dve, v_out, 16 * n)
                    nc.vector.tensor_tensor(
                        v_sb[:, 2 * half:2 * half + 2, :, 0:HD],
                        m_v[:].rearrange("p t (h d) -> p t h d", d=HD),
                        bv_row[:].rearrange("p (h d) -> p h d", d=HD).unsqueeze(1).to_broadcast([P, 2, NH, HD]),
                        ALU.add).then_inc(v_kept, 1)
                for m in range(CH + 1):
                    c = m % HC
                    after(dve, low_done, (CH + 1) * n + m + 1)
                    if m < HC:
                        a, mid, low = full_q[:, c], part_q[:, u, 1, c], part_q[:, u, 2, c]
                    elif m < CH:
                        a, mid, low = full_k[:, c], part_k[:, u, 1, c], part_k[:, u, 2, c]
                    else:
                        a, mid, low = full_t[:], part_t[:, 1], part_t[:, 2]
                    nc.vector.tensor_copy(mid, a).then_inc(mid_done, 1)
                    after(dve, mid_done, (CH + 1) * n + m + 1)
                    nc.vector.tensor_tensor(low, a, mid, ALU.subtract).then_inc(parts_done, 1)

            dve.wait_ge(v_const, 2)
            norm(0, 0)

            def body(i, last):
                norm(2 * i + 1, 1)
                split(2 * i, i, 0)
                if not last:
                    norm(2 * i + 2, 0)
                split(2 * i + 1, i, 1)

            peeled(dve, pairs, body)


def attend(nc, io, B, ctx, sem, passed, d_tab, d_stack, d_kterm, d_v, d_skew, d_ctx):
    def sb(name, shape, dt=F32):
        return ctx.enter_context(nc.sbuf_tensor("a_" + name, shape, dt))

    def ps(name, shape):
        return ctx.enter_context(nc.psum_tensor("a_ps_" + name, shape, F32))

    ident = sb("ident", [P, P])
    past = sb("past", [P, 2, P])
    tabs = sb("tabs", [ST, 2, NH, TW], BF16)
    stack = sb("stack", [ST + 3, 2, GH, SW], BF16)
    skew_in = sb("skew_in", [P, 2, 2, QT, TW])
    bias = sb("bias", [P, AHEAD, 2, QT, S])
    beyond = sb("beyond", [P, 2, 2, QT - 1, P])
    scored = sb("scored", [P, 2, QT, S])
    top_of = sb("top_of", [P, 2, QT])
    shift = sb("shift", [P, 2, QT])
    probs = sb("probs", [P, 2, QT, S])
    probsT = sb("probsT", [P, QT, S])
    values = sb("values", [P, 2, QT, NH // 2, CROW])
    ctx_sb = sb("ctx_sb", [P, 2, S])
    m_tab = ps("m_tab", [P, 2, 2, TW])
    m_s = ps("m_s", [P, 2, S])
    m_t = ps("m_t", [P, 2, S])
    m_ctx = ps("m_ctx", [P, S])

    const_in, zeroed, zeroed_p, zero_out = (sem("a_" + n) for n in ("const_in", "zeroed", "zeroed_p", "zero_out"))
    stack_in = [sem(f"a_stack_in{u}") for u in range(2)]
    values_in = [sem(f"a_values_in{u}") for u in range(2)]
    skew_out = [sem(f"a_skew_out{u}") for u in range(2)]
    bias_in = [sem(f"a_bias_in{u}") for u in range(AHEAD)]
    (tab_done, tab_c, tab_p, beyond_done, filled, s_done, s_kept, shifted, exp_done, turn_done, turnA, turnD,
     pv_done, ctx_kept, ctx_out) = (sem("a_" + n) for n in (
         "tab_done", "tab_c", "tab_p", "beyond_done", "filled", "s_done", "s_kept", "shifted", "exp_done",
         "turn_done", "turnA", "turnD", "pv_done", "ctx_kept", "ctx_out"))
    STACKS = SLOTS + 1
    HEADS = B * NH
    READS = 4
    TURN = 2
    scratch = d_skew.tensor
    plane = P * PITCH
    FIRST = P

    def early(b, hh, lag):
        return isinstance(b, int) and b == 0 and hh < lag

    with nc.Block() as block:
        @block.sync
        def _(sp):
            sp.dma_start(ident[:], io["ident"]).then_inc(const_in, 16)
            sp.dma_start(past[:], io["past"]).then_inc(const_in, 16)
            for w in range(2):
                for j in range(SLOTS):
                    part = (SIDE_B if w == 0 else SIDE_A)[j]
                    sp.dma_start(tabs[j * HD:(j + 1) * HD, w],
                                 d_tab[w, part].rearrange("(h d) x -> d h x", d=HD)).then_inc(const_in, 16)

            def load_stack(b, g):
                u = g % 2
                for j in range(SLOTS):
                    sp.dma_start(stack[j * HD:(j + 1) * HD, u],
                                 d_stack[b, j, g * GH * HD:(g + 1) * GH * HD].rearrange("(h d) x -> d h x", d=HD)
                                 ).then_inc(stack_in[u], 16)
                sp.dma_start(stack[ST:ST + 3, u, :, 2 * S:], d_kterm[b, :, g * GH:(g + 1) * GH]
                             ).then_inc(stack_in[u], 16)

            def load_values(b, half):
                sp.dma_start(values[:, half],
                             d_v[b].rearrange("(t p) x -> p t x", p=P)[
                                 :, :, half * NH // 2 * CROW:(half + 1) * NH // 2 * CROW]
                             .rearrange("p t (h r) -> p t h r", r=CROW)).then_inc(values_in[half], 16)

            def write_tables(n, hh):
                u, slot = hh % 2, hh % RING
                for kept in (tab_c, tab_p):
                    settled(sp, kept, 2 * (n + 1), passed)
                sp.dma_start(d_skew[slot].rearrange("w t p x -> p (w t) x")[:, :, FIRST:FIRST + TW],
                             skew_in[:, u].rearrange("p w t x -> p (w t) x")).then_inc(skew_out[u], 16)

            def read_tables(n, b, hh):
                u, v, slot = hh % 2, hh % AHEAD, hh % RING
                settled(sp, skew_out[u], 16 * (NH // 2 * b + hh // 2 + 1), passed)
                settled(sp, s_kept, QT * (n - AHEAD + 1), passed)
                for w in range(2):
                    base = (slot * 2 + w) * QT * plane + P - 1 + w
                    tile = bias[:, v, w, 0]
                    for width, at, to, skip, step in (
                            (2 * P, 0, (QT - 1) * S + (QT - 2) * P, P, (QT - 1) * plane - P),
                            (NEAR, S, S + P, plane, plane)):
                        sp.dma_start(bass.AP(tile.tensor, tile.offset + at, [list(tile.ap[0]), [to, 2], [1, width]]),
                                     bass.AP(scratch, base + skip, [[PITCH - 1, P], [step, 2], [1, width]])
                                     ).then_inc(bias_in[v], 16)

            def store_ctx(b, g):
                settled(sp, ctx_kept, NG * b + g + 1, passed)
                to = d_ctx[b, g] if g >= 0 else d_ctx[b - 1, NG - 1]
                sp.dma_start(to, ctx_sb[:, g % 2]).then_inc(ctx_out, 16)

            load_stack(0, 0)
            load_stack(0, 1)
            load_values(0, 0)
            load_values(0, 1)
            sp.wait_ge(zeroed, 3)
            sp.wait_ge(zeroed_p, 1)
            for slot in range(RING):
                rows = d_skew[slot].rearrange("w t p x -> p (w t) x")
                for a in (0, FIRST + TW):
                    sp.dma_start(rows[:, :, a:a + P], skew_in[:, 0].rearrange("p w t x -> p (w t) x")[:, :, 0:P]
                                 ).then_inc(zero_out, 16)
            sp.wait_ge(zero_out, 16 * 2 * RING)
            for m in range(LEAD):
                write_tables(m, m)
                if m:
                    read_tables(m - 1, 0, m - 1)

            def body(b, last):
                for hh in range(NH):
                    n = NH * b + hh
                    if hh % GH == 0 and not early(b, hh, 1):
                        g = hh // GH + 1
                        if not (last and g == NG):
                            settled(sp, s_done, QT * n, passed)
                            load_stack(b + g // NG, g % NG)
                    if not (last and hh + LEAD >= NH):
                        write_tables(n + LEAD, (hh + LEAD) % NH)
                    if not (last and hh + LEAD - 1 >= NH):
                        m = hh + LEAD - 1
                        read_tables(n + LEAD - 1, b + m // NH, m % NH)
                    if hh == TURN and not early(b, hh, NH):
                        settled(sp, pv_done, n - TURN, passed)
                        load_values(b, 1)
                    if hh == NH // 2 + TURN and not last:
                        settled(sp, pv_done, n - TURN, passed)
                        load_values(b + 1, 0)
                    if hh % GH == TURN and not early(b, hh, GH):
                        store_ctx(b, hh // GH - 1)

            peeled(sp, B, body)
            store_ctx(B - 1, NG - 1)
            sp.wait_ge(ctx_out, 16 * NG * B)

        @block.gpsimd
        def _(pool):
            nc.gpsimd.memset(skew_in[:, 0], 0.0).then_inc(zeroed, 1)
            nc.gpsimd.memset(bias[:, :, 0], 0.0).then_inc(zeroed, 1)
            pool.wait_ge(zeroed, 2)
            nc.gpsimd.memset(stack[ST:ST + 3, :, :, 0:S], 1.0).then_inc(zeroed, 1)
            pool.wait_ge(const_in, 16 * (2 + 2 * SLOTS))

            def constants(n, hh):
                u = hh % 2
                after(pool, filled, 2 * (n - 1))
                for w, kept in ((0, tab_c), (1, tab_p)):
                    after(pool, kept, 2 * (n + 1))
                    high = skew_in[:, u, w, 1:QT, 0:1] if w == 0 else skew_in[:, u, w, 0:QT - 1, TW - 1:TW]
                    nc.gpsimd.tensor_tensor(beyond[:, u, w], past[:, w].unsqueeze(1).to_broadcast([P, QT - 1, P]),
                                            high.to_broadcast([P, QT - 1, P]), ALU.mult).then_inc(beyond_done, 1)

            def fill(n, b, hh):
                u, v = hh % 2, hh % AHEAD
                after(pool, bias_in[v], 16 * READS * (NH // AHEAD * b + hh // AHEAD + 1))
                after(pool, beyond_done, 2 * (n + 1))
                for w in range(2):
                    tile = bias[:, v, w, 0]
                    block_of = bass.AP(tile.tensor, tile.offset + (S if w == 0 else P),
                                       [list(tile.ap[0]), [S + P, QT - 1], [1, P]])
                    nc.gpsimd.tensor_tensor(block_of, block_of, beyond[:, u, w], ALU.add).then_inc(filled, 1)

            for m in range(LEAD):
                constants(m, m)
                if m:
                    fill(m - 1, 0, m - 1)

            def body(b, last):
                for hh in range(NH):
                    n, m = NH * b + hh, hh + LEAD
                    if not (last and m >= NH):
                        constants(n + LEAD, m % NH)
                    if not (last and m - 1 >= NH):
                        fill(n + LEAD - 1, b + (m - 1) // NH, (m - 1) % NH)

            peeled(pool, B, body)

        @block.tensor
        def _(pe):
            def tables(n, b, hh, part):
                g, w, half = hh // GH, part % 2, part // 2
                if hh % GH == 0 and part == 0:
                    after(pe, stack_in[g % 2], 16 * STACKS * (NG // 2 * b + g // 2 + 1))
                after(pe, (tab_c, tab_p)[w], 2 * n + half)
                for k in range(2):
                    at = (S if w else 0) + (2 * half + k) * P
                    mm = pe.matmul(m_tab[:, w, k], stack[0:ST, g % 2, hh % GH, at:at + P], tabs[:, w, hh],
                                   start=True, stop=True)
                mm.then_inc(tab_done, 1)

            def scores(n, hh, t):
                g = hh // GH
                if t == 0:
                    after(pe, filled, 2 * (n + 1))
                after(pe, s_kept, QT * n + t - 1)
                bank = m_s[:, t % 2]
                row = stack[0:ST + 3, g % 2, hh % GH]
                q = row[:, t * P:(t + 1) * P]
                far = max(0, t - 1) * P
                if far:
                    pe.matmul(bank[:, 0:far], q, row[:, 3 * S:3 * S + far], start=True, stop=False,
                              skip_group_check=True)
                pe.matmul(bank[:, far:], q, row[:, 2 * S + far:3 * S], start=not far, stop=False,
                          skip_group_check=True)
                near = [k for k in range(QT) if abs(k - t) <= 1]
                for k in near:
                    mm = pe.matmul(bank[:, k * P:(k + 1) * P], bias[:, hh % AHEAD, 1, k, t * P:(t + 1) * P],
                                   ident[:], start=False, stop=(k == near[-1]), is_transpose=True,
                                   skip_group_check=True)
                mm.then_inc(s_done, 1)

            def turn(n, hh, k):
                if k == 0:
                    after(pe, exp_done, QT * (n + 1))
                after(pe, (turnA, turnD)[k % 2], 2 * n + k // 2)
                for t in range(QT):
                    mm = pe.transpose(m_t[:, k % 2, t * P:(t + 1) * P], probs[:, hh % 2, t, k * P:(k + 1) * P],
                                      ident[:])
                mm.then_inc(turn_done, 1)

            def context(n, b, hh, k):
                half, j = hh // (NH // 2), hh % GH
                if k == 0 and hh % (NH // 2) == 0:
                    after(pe, values_in[half], 16 * (b + 1))
                if k == 0 and j == 0:
                    after(pe, ctx_kept, NG * b + hh // GH)
                after(pe, (turnA, turnD)[k % 2], 2 * n + k // 2 + 1)
                mm = pe.matmul(m_ctx[j * CROW:(j + 1) * CROW], values[:, half, k, hh % (NH // 2)],
                               probsT[:, k], start=(k == 0), stop=(k == QT - 1))
                if k == QT - 1:
                    mm.then_inc(pv_done, 1)

            def turned(n, b, hh):
                for k in range(QT):
                    turn(n, hh, k)
                    if k:
                        context(n, b, hh, k - 1)
                context(n, b, hh, QT - 1)

            pe.wait_ge(const_in, 16 * (2 + 2 * SLOTS))
            pe.wait_ge(zeroed, 3)
            for m in range(LEAD):
                for part in range(4):
                    tables(m, 0, m, part)

            def body(b, last):
                for hh in range(NH):
                    n, m = NH * b + hh, hh + LEAD
                    old = not early(b, hh, TURN)
                    behind = (n - TURN, b - 1 if hh < TURN else b, (hh - TURN) % NH)
                    for t in range(QT):
                        scores(n, hh, t)
                        if t == 0 and not early(b, hh, TURN + 1):
                            at = hh - TURN - 1
                            context(n - TURN - 1, b - 1 if at < 0 else b, at % NH, QT - 1)
                        if old:
                            turn(behind[0], behind[2], t)
                        if t < 2 and not (last and m >= NH):
                            for part in (2 * t, 2 * t + 1):
                                tables(n + LEAD, b + m // NH, m % NH, part)
                        if old and t:
                            context(*behind, t - 1)

            peeled(pe, B, body)
            context(HEADS - TURN - 1, B - 1, NH - TURN - 1, QT - 1)
            for lag in range(TURN, 0, -1):
                turned(HEADS - lag, B - 1, NH - lag)

        @block.scalar
        def _(act):
            def keep_tables(n, hh, half):
                u = hh % 2
                after(act, tab_done, 4 * n + 2 * half + 1)
                if half == 0:
                    wait_tables(act, skew_out, n, hh)
                    after(act, beyond_done, 2 * (n - 1))
                nc.scalar.activation(skew_in[:, u, 0, 2 * half:2 * half + 2], m_tab[:, 0], ACT.Identity
                                     ).then_inc(tab_c, 1)

            def exponent(n, hh, t):
                u = hh % 2
                if t == 0:
                    after(act, shifted, n + 1)
                    after(act, turn_done, QT * (n - 1))
                nc.scalar.activation(probs[:, u, t], scored[:, u, t], ACT.Exp, bias=shift[:, u, t:t + 1],
                                     scale=SCALE).then_inc(exp_done, 1)

            def keep_turned(n, k):
                after(act, turn_done, QT * n + k + 1)
                after(act, pv_done, n)
                nc.scalar.activation(probsT[:, k], m_t[:, 0], ACT.Identity).then_inc(turnA, 1)

            def keep_context(n, b, hh):
                g = hh // GH
                after(act, pv_done, n + 1)
                after(act, ctx_out, 16 * (NG * b + g))
                nc.scalar.activation(ctx_sb[:, g % 2], m_ctx[:], ACT.Identity).then_inc(ctx_kept, 1)

            act.wait_ge(zero_out, 16 * 2 * RING)
            for m in range(LEAD):
                for half in range(2):
                    keep_tables(m, m, half)

            def body(b, last):
                for hh in range(NH):
                    n, m = NH * b + hh, hh + LEAD
                    old = not early(b, hh, TURN)
                    for t in range(QT):
                        if not early(b, hh, 1):
                            exponent(n - 1, (hh - 1) % NH, t)
                        if t == 0 and hh % GH == TURN and not early(b, hh, GH):
                            at = hh - TURN - 1
                            keep_context(n - TURN - 1, b - 1 if at < 0 else b, at % NH)
                        if old and t % 2 == 0:
                            keep_turned(n - TURN, t)
                        if t < 2 and not (last and m >= NH):
                            keep_tables(n + LEAD, m % NH, t)

            peeled(act, B, body)
            for t in range(QT):
                exponent(HEADS - 1, NH - 1, t)
            for lag in range(TURN, 0, -1):
                keep_turned(HEADS - lag, 0)
                keep_turned(HEADS - lag, 2)
            keep_context(HEADS - 1, B - 1, NH - 1)

        @block.vector
        def _(dve):
            nc.vector.memset(bias[:, :, 1], 0.0).then_inc(zeroed_p, 1)

            def keep_tables(n, hh, half):
                u = hh % 2
                after(dve, tab_done, 4 * n + 2 * half + 2)
                if half == 0:
                    wait_tables(dve, skew_out, n, hh)
                    after(dve, beyond_done, 2 * (n - 1))
                nc.vector.tensor_copy(skew_in[:, u, 1, 2 * half:2 * half + 2], m_tab[:, 1]).then_inc(tab_p, 1)

            def add_bias(n, hh, t):
                u = hh % 2
                if t == 0:
                    after(dve, filled, 2 * (n + 1))
                    after(dve, exp_done, QT * (n - 1))
                settled(dve, s_done, QT * n + t + 1, passed)
                nc.vector.tensor_tensor_reduce(scored[:, u, t], m_s[:, t % 2], bias[:, hh % AHEAD, 0, t], 1.0,
                                               -3.0e38, ALU.add, ALU.max, top_of[:, u, t:t + 1]
                                               ).then_inc(s_kept, 1)

            def shift_of(n, hh):
                u = hh % 2
                after(dve, s_kept, QT * (n + 1))
                nc.vector.tensor_scalar(shift[:, u], top_of[:, u], -SCALE, None, ALU.mult).then_inc(shifted, 1)

            def keep_turned(n, k):
                after(dve, turn_done, QT * n + k + 1)
                after(dve, pv_done, n)
                nc.vector.tensor_copy(probsT[:, k], m_t[:, 1]).then_inc(turnD, 1)

            dve.wait_ge(zero_out, 16 * 2 * RING)
            for m in range(LEAD):
                for half in range(2):
                    keep_tables(m, m, half)

            def body(b, last):
                for hh in range(NH):
                    n, m = NH * b + hh, hh + LEAD
                    for t in range(QT):
                        add_bias(n, hh, t)
                        if t == QT - 1:
                            shift_of(n, hh)
                        if t % 2 and not early(b, hh, TURN):
                            keep_turned(n - TURN, t)
                        if t < 2 and not (last and m >= NH):
                            keep_tables(n + LEAD, m % NH, t)

            peeled(dve, B, body)
            for lag in range(TURN, 0, -1):
                keep_turned(HEADS - lag, 1)
                keep_turned(HEADS - lag, 3)


def wait_tables(eng, skew_out, n, hh):
    if not (isinstance(n, int) and n < 2):
        eng.wait_ge(skew_out[hh % 2], 8 * (n - hh % 2))


def output(nc, io, B, ctx, sem, passed, scores, d_h, d_ctx, d_xg):
    def sb(name, shape, dt=F32):
        return ctx.enter_context(nc.sbuf_tensor("o_" + name, shape, dt))

    def ps(name, shape):
        return ctx.enter_context(nc.psum_tensor("o_ps_" + name, shape, F32))

    ident, wo = sb("ident", [P, P]), sb("wo", [P, HC, H])
    bo_row, wr, br_row = sb("bo_row", [P, H]), sb("wr", [P, HC, NE]), sb("br_row", [P, NE])
    minus_half = sb("minus_half", [P, QT])
    h_in, h_new = sb("h_in", [P, 2, QT, H]), sb("h_new", [P, 2, QT, H])
    c_in, sums = sb("c_in", [P, 2, HC, S]), sb("sums", [P, 2, HC, S])
    ctxn = sb("ctxn", [P, HC, S])
    stats, moments = sb("stats", [P, QT, 6]), sb("moments", [P, QT, 2])
    var_eps, rstd = sb("var_eps", [P, QT]), sb("rstd", [P, QT])
    xg, xT = sb("xg", [P, 2, QT, XG]), sb("xT", [P, HC, S])
    logits, expd = sb("logits", [P, QT, NE]), sb("expd", [P, QT, NE])
    top_of, total, share = sb("top_of", [P, QT]), sb("total", [P, QT]), sb("share", [P, QT])
    m_o, m_turn, m_r = ps("m_o", [P, QT, H]), ps("m_turn", [P, HC, S]), ps("m_r", [P, QT, NE])
    const_in, half_set = sem("o_const_in"), sem("o_half_set")
    batch_in = [sem(f"o_batch_in{u}") for u in range(2)]
    stored = [sem(f"o_stored{u}") for u in range(2)]
    (scaled, scale_step, o_done, h_added, h_done, st_done, mo_done, ve_done, rs_done, xn_done, turn_done,
     turnA, turnD, r_done, soft, exp_done, xg_done) = (sem("o_" + n) for n in (
         "scaled", "scale_step", "o_done", "h_added", "h_done", "st_done", "mo_done", "ve_done", "rs_done",
         "xn_done", "turn_done", "turnA", "turnD", "r_done", "soft", "exp_done", "xg_done"))
    consts = [(ident[:], io["ident"]), (wo[:], io["Wo"].rearrange("(c p) o -> p c o", p=P)),
              (bo_row[:], io["bo"].partition_broadcast(P)),
              (wr[:], io["router_w"].rearrange("(c p) o -> p c o", p=P)),
              (br_row[:], io["router_b"].partition_broadcast(P))]
    LOADS = 1 + 2 * HC
    SOFT = 6
    pairs = B // 2

    with nc.Block() as block:
        @block.sync
        def _(sp):
            for dst, src in consts:
                sp.dma_start(dst, src).then_inc(const_in, 16)

            def load(n, u):
                sp.dma_start(h_in[:, u], d_h[n].rearrange("(t p) o -> p t o", p=P)).then_inc(batch_in[u], 16)
                for c in range(HC):
                    at = d_ctx[n, c * (NG // HC)]
                    heads = [CROW * S, NH // HC]
                    sp.dma_start(c_in[:, u, c], bass.AP(at.tensor, at.offset, [heads, [S, HD], [1, S]])
                                 ).then_inc(batch_in[u], 16)
                    sp.dma_start(sums[:, u, c], bass.AP(at.tensor, at.offset + HD * S,
                                                        [heads, [0, HD], [1, S]])).then_inc(batch_in[u], 16)

            load(0, 0)
            load(1, 1)

            def body(i, last):
                for u in range(2):
                    n = 2 * i + u
                    if not last:
                        settled(sp, h_done, n + 1, passed)
                        load(n + 2, u)
                    settled(sp, h_done, n + 1, passed)
                    sp.dma_start(io["out"][n].rearrange("(t p) o -> p t o", p=P), h_new[:, u]
                                 ).then_inc(stored[u], 16)
                    settled(sp, xg_done, n + 1, passed)
                    sp.dma_start(d_xg.rearrange("(b t p) o -> b p t o", t=QT, p=P)[n], xg[:, u]
                                 ).then_inc(stored[u], 16)

            peeled(sp, pairs, body)
            for u in range(2):
                sp.wait_ge(stored[u], 32 * pairs)

        @block.gpsimd
        def _(pool):
            nc.gpsimd.memset(minus_half[:], -0.5).then_inc(half_set, 1)
            pool.wait_ge(half_set, 1)
            pool.wait_ge(const_in, 16 * len(consts))

            def body(i, last):
                for u in range(2):
                    n = 2 * i + u
                    after(pool, batch_in[u], 16 * LOADS * (i + 1))
                    nc.gpsimd.tensor_tensor(h_in[:, u], h_in[:, u],
                                            bo_row[:].unsqueeze(1).to_broadcast([P, QT, H]), ALU.add
                                            ).then_inc(h_added, 1)
                    after(pool, ve_done, n + 1)
                    nc.gpsimd.tensor_tensor(rstd[:], var_eps[:], minus_half[:], ALU.pow).then_inc(rs_done, 1)

            peeled(pool, pairs, body)

        @block.tensor
        def _(pe):
            def project_out(n):
                after(pe, scaled, n + 1)
                after(pe, h_done, n)
                for t in range(QT):
                    for c in range(HC):
                        mm = pe.matmul(m_o[:, t], ctxn[:, c, t * P:(t + 1) * P], wo[:, c], start=(c == 0),
                                       stop=(c == HC - 1))
                mm.then_inc(o_done, 1)

            def turn(n, u):
                after(pe, xn_done, n + 1)
                after(pe, turnA, n)
                after(pe, turnD, n)
                for c in range(HC):
                    for t in range(QT):
                        mm = pe.transpose(m_turn[:, c, t * P:(t + 1) * P], xg[:, u, t, c * P:(c + 1) * P],
                                          ident[:])
                    mm.then_inc(turn_done, 1)

            def route(n):
                after(pe, turnA, n + 1)
                after(pe, turnD, n + 1)
                after(pe, soft, SOFT * n)
                for t in range(QT):
                    for c in range(HC):
                        mm = pe.matmul(m_r[:, t], xT[:, c, t * P:(t + 1) * P], wr[:, c], start=(c == 0),
                                       stop=(c == HC - 1))
                mm.then_inc(r_done, 1)

            pe.wait_ge(const_in, 16 * len(consts))
            project_out(0)

            def body(i, last):
                for u in range(2):
                    n = 2 * i + u
                    turn(n, u)
                    if not (last and u == 1):
                        project_out(n + 1)
                    route(n)

            peeled(pe, pairs, body)

        @block.scalar
        def _(act):
            def body(i, last):
                for u in range(2):
                    n = 2 * i + u
                    after(act, turn_done, HC * n + 1)
                    after(act, r_done, n)
                    nc.scalar.activation(xT[:, 0], m_turn[:, 0], ACT.Identity).then_inc(turnA, 1)
                    after(act, soft, SOFT * n + 3)
                    nc.scalar.activation(expd[:], logits[:], ACT.Exp).then_inc(exp_done, 1)

            peeled(act, pairs, body)

        @block.vector
        def _(dve):
            dve.wait_ge(const_in, 16 * len(consts))

            def scale_context(n, i, u):
                after(dve, batch_in[u], 16 * LOADS * (i + 1))
                after(dve, o_done, n)
                nc.vector.reciprocal(sums[:, u], sums[:, u]).then_inc(scale_step, 1)
                after(dve, scale_step, n + 1)
                nc.vector.tensor_tensor(ctxn[:], c_in[:, u], sums[:, u], ALU.mult).then_inc(scaled, 1)

            def norm(n, i, u):
                after(dve, o_done, n + 1)
                after(dve, h_added, n + 1)
                after(dve, stored[u], 32 * i)
                nc.vector.tensor_tensor(h_new[:, u], m_o[:], h_in[:, u], ALU.add).then_inc(h_done, 1)
                after(dve, h_done, n + 1)
                for t in range(QT):
                    nc.vector.bn_stats(stats[:, t], h_new[:, u, t]).then_inc(st_done, 1)
                settled(dve, st_done, QT * (n + 1), passed)
                for t in range(QT):
                    nc.vector.bn_aggr(moments[:, t], stats[:, t]).then_inc(mo_done, 1)
                after(dve, mo_done, QT * (n + 1))
                nc.vector.tensor_scalar_add(var_eps[:], moments[:, :, 1], EPS).then_inc(ve_done, 1)
                after(dve, rs_done, n + 1)
                for t in range(QT):
                    ins = nc.vector.tensor_scalar(xg[:, u, t, 0:H], h_new[:, u, t], moments[:, t, 0:1],
                                                  rstd[:, t:t + 1], ALU.subtract, ALU.mult)
                ins.then_inc(xn_done, 1)

            def soft_scores(n, u):
                def step(ins, k):
                    ins.then_inc(soft, 1)
                    after(dve, soft, SOFT * n + k)

                after(dve, turn_done, HC * n + 2)
                after(dve, r_done, n)
                nc.vector.tensor_copy(xT[:, 1], m_turn[:, 1]).then_inc(turnD, 1)
                after(dve, r_done, n + 1)
                step(nc.vector.tensor_tensor(logits[:], m_r[:], br_row[:].unsqueeze(1).to_broadcast([P, QT, NE]),
                                             ALU.add), 1)
                step(nc.vector.tensor_reduce(top_of[:], logits[:], AX.X, ALU.max), 2)
                step(nc.vector.tensor_tensor(logits[:], logits[:], top_of[:].unsqueeze(2).to_broadcast([P, QT, NE]),
                                             ALU.subtract), 3)
                after(dve, exp_done, n + 1)
                step(nc.vector.tensor_reduce(total[:], expd[:], AX.X, ALU.add), 4)
                step(nc.vector.reciprocal(share[:], total[:]), 5)
                nc.vector.tensor_tensor(xg[:, u, :, H:], expd[:], share[:].unsqueeze(2).to_broadcast([P, QT, NE]),
                                        ALU.mult).then_inc(xg_done, 1)
                step(nc.vector.tensor_tensor(scores[:, :, bass.ts(n, QT)].rearrange("p e t -> p t e"), expd[:],
                                             share[:].unsqueeze(2).to_broadcast([P, QT, NE]), ALU.mult), 6)

            scale_context(0, 0, 0)

            def body(i, last):
                for u in range(2):
                    n = 2 * i + u
                    norm(n, i, u)
                    if not (last and u == 1):
                        scale_context(n + 1, i + u, 1 - u)
                    soft_scores(n, u)

            peeled(dve, pairs, body)


def choose(nc, io, NT, ctx, sem, passed, scores, chosen):
    def sb(name, shape, dt=F32):
        return ctx.enter_context(nc.sbuf_tensor("c_" + name, shape, dt))

    def ps(name, shape):
        return ctx.enter_context(nc.psum_tensor("c_ps_" + name, shape, F32))

    ET = NE * NT
    before = sb("before", [P, P], BF16)
    ones = sb("ones", [P, P], BF16)
    before_f, iota, place = sb("before_f", [P, P]), sb("iota", [P, P]), sb("place", [P, 2, NT])
    restart = sb("restart", [P, NE, NT])
    least, trial, bit = sb("least", [P, NE], I32), sb("trial", [P, NE], I32), sb("bit", [P, NE], I32)
    enough, held = sb("enough", [P, NE], I32), sb("held", [P, NE])
    held_b = sb("held_b", [P, 2, NE], BF16)
    mask = sb("mask", [P, NE, NT], BF16)
    above, equal = sb("above", [P, NE, NT]), sb("equal", [P, NE, NT])
    run, rank, sel = sb("run", [P, NE, NT]), sb("rank", [P, NE, NT]), sb("sel", [P, NE, NT])
    room = sb("room", [P, NE])
    quarter = sb("quarter", [P, CT, NE, NT])
    what = sb("what", [P, NE, NT, 2 * CT], BF16)
    TG = 16 if NT % 16 == 0 else NT
    hot = sb("hot", [P, 2, TG, P], BF16)
    index = sb("index", [P, NE, CT])
    m_count = ps("m_count", [P, NE])
    GB = min(ET, S)
    m_below, m_all = ps("m_below", [P, ET // GB, GB]), ps("m_all", [P, ET // GB, GB])
    m_list = ps("m_list", [P, NE, 2 * CT])
    c_in, c_dve, c_pe, c_hot, c_listed = (sem("c_" + n) for n in ("in", "dve", "pe", "hot", "listed"))
    wide = lambda ap: ap.unsqueeze(2).to_broadcast([P, NE, NT])
    ROUND = 7
    START = 4

    with nc.Block() as block:
        @block.sync
        def _(sp):
            for dst, src in ((before_f, io["before"]), (iota, io["iota"]), (place, io["place"])):
                sp.dma_start(dst[:], src).then_inc(c_in, 16)

        @block.tensor
        def _(pe):
            pe.wait_ge(c_dve, START)

            with pe.Fori(0, BITS, 1) as r:
                after(pe, c_dve, START + ROUND * r + 4)
                for k in range(2):
                    mm = pe.matmul(m_count[:], ones[:], held_b[:, k], start=(k == 0), stop=(k == 1))
                mm.then_inc(c_pe, 1)
            base = START + ROUND * BITS
            pe.wait_ge(c_dve, base + 4)
            for k in range(2):
                mm = pe.matmul(m_count[:], ones[:], held_b[:, k], start=(k == 0), stop=(k == 1))
            mm.then_inc(c_pe, 1)
            for stage, ready in ((0, base + 6), (1, base + 13)):
                pe.wait_ge(c_dve, ready)
                flat = mask[:].rearrange("p e t -> p (e t)")
                for g in range(ET // GB):
                    pe.matmul(m_below[:, g], before[:], flat[:, g * GB:(g + 1) * GB], start=True, stop=True)
                    mm = pe.matmul(m_all[:, g], ones[:], flat[:, g * GB:(g + 1) * GB], start=True, stop=True)
                mm.then_inc(c_pe, 1)
            for e in range(NE):
                for g in range(NT // TG):
                    k = e * (NT // TG) + g
                    pe.wait_ge(c_hot, k + 1)
                    for t in range(TG):
                        at = g * TG + t
                        mm = pe.matmul(m_list[:, e], hot[:, k % 2, t], what[:, e, at], start=(at == 0),
                                       stop=(at == NT - 1), skip_group_check=True)
                    mm.then_inc(c_listed, 1)

        @block.vector
        def _(dve):
            count = [0]

            def step(ins):
                count[0] += 1
                ins.then_inc(c_dve, 1)
                dve.wait_ge(c_dve, count[0])

            dve.wait_ge(c_in, 48)
            nc.vector.memset(least[:], 0)
            nc.vector.memset(bit[:], 1 << (BITS - 1))
            step(nc.vector.memset(ones[:], 1.0))
            step(nc.vector.tensor_copy(before[:], before_f[:]))
            nc.vector.memset(restart[:], 1.0)
            step(nc.vector.memset(rank[:], 0.0))
            step(nc.vector.memset(restart[:, :, 0:1], 0.0))

            with dve.Fori(0, BITS, 1) as r:
                def chain(ins, k):
                    ins.then_inc(c_dve, 1)
                    settled(dve, c_dve, START + ROUND * r + k, passed)

                chain(nc.vector.tensor_tensor(trial[:], least[:], bit[:], ALU.bitwise_or), 1)
                chain(nc.vector.tensor_tensor(above[:], scores[:], wide(trial[:].bitcast(F32)), ALU.is_ge), 2)
                chain(nc.vector.tensor_reduce(held[:], above[:], AX.X, ALU.add), 3)
                nc.vector.memset(held_b[:, 1], 0.0)
                chain(nc.vector.tensor_copy(held_b[:, 0], held[:]), 4)
                after(dve, c_pe, r + 1)
                chain(nc.vector.tensor_scalar(enough[:], m_count[:], float(TOPK), None, ALU.is_ge), 5)
                chain(nc.vector.copy_predicated(least[:], enough[:], trial[:]), 6)
                chain(nc.vector.tensor_scalar(bit[:], bit[:], 1, None, ALU.logical_shift_right), 7)
            count[0] = START + ROUND * BITS
            floor = wide(least[:].bitcast(F32))
            step(nc.vector.tensor_tensor(above[:], scores[:], floor, ALU.is_gt))
            step(nc.vector.tensor_tensor(equal[:], scores[:], floor, ALU.is_equal))
            step(nc.vector.tensor_reduce(held[:], above[:], AX.X, ALU.add))
            step(nc.vector.tensor_copy(held_b[:, 0], held[:]))
            dve.wait_ge(c_pe, BITS + 1)
            step(nc.vector.tensor_scalar(room[:], m_count[:], -1.0, float(TOPK), ALU.mult, ALU.add))
            step(nc.vector.tensor_copy(mask[:], equal[:]))

            def ranks():
                below = m_below[:].rearrange("p g x -> p (g x)")
                every = m_all[:].rearrange("p g x -> p (g x)")
                flat = lambda x: x[:].rearrange("p e t -> p (e t)")
                step(nc.vector.tensor_copy(flat(run), every))
                step(nc.vector.tensor_tensor_scan(flat(rank), flat(restart), flat(run), 0.0, ALU.mult, ALU.add))
                step(nc.vector.tensor_tensor(flat(rank), flat(rank), flat(run), ALU.subtract))
                step(nc.vector.tensor_tensor(flat(rank), flat(rank), below, ALU.add))

            dve.wait_ge(c_pe, BITS + 2)
            ranks()
            step(nc.vector.tensor_tensor(sel[:], rank[:], wide(room[:]), ALU.is_lt))
            step(nc.vector.tensor_tensor(sel[:], sel[:], equal[:], ALU.mult))
            step(nc.vector.tensor_tensor(mask[:], sel[:], above[:], ALU.add))
            dve.wait_ge(c_pe, BITS + 3)
            ranks()
            step(nc.vector.tensor_tensor(sel[:], sel[:], above[:], ALU.add))
            step(nc.vector.tensor_scalar_add(rank[:], rank[:], 1.0))
            step(nc.vector.tensor_tensor(rank[:], rank[:], sel[:], ALU.mult))
            step(nc.vector.tensor_scalar_add(rank[:], rank[:], -1.0))
            for c in range(1, CT):
                ins = nc.vector.tensor_scalar(quarter[:, c], rank[:], float(c * P), None, ALU.is_ge)
            step(ins)
            for c in range(1, CT):
                step(nc.vector.scalar_tensor_tensor(rank[:], quarter[:, c], -float(P), rank[:], ALU.mult, ALU.add))
            step(nc.vector.tensor_copy(quarter[:, 0], sel[:]))
            for c in range(CT - 1):
                step(nc.vector.tensor_tensor(quarter[:, c], quarter[:, c], quarter[:, c + 1], ALU.subtract))
            for c in range(CT):
                for k in range(2):
                    ins = nc.vector.tensor_tensor(what[:, :, :, 2 * c + k], quarter[:, c],
                                                  place[:, k].unsqueeze(1).to_broadcast([P, NE, NT]), ALU.mult)
            step(ins)
            for e in range(NE):
                for g in range(NT // TG):
                    k = e * (NT // TG) + g
                    if k >= 2:
                        dve.wait_ge(c_listed, k - 1)
                    nc.vector.tensor_tensor(
                        hot[:, k % 2], iota[:].unsqueeze(1).to_broadcast([P, TG, P]),
                        rank[:, e, g * TG:(g + 1) * TG].unsqueeze(2).to_broadcast([P, TG, P]),
                        ALU.is_equal).then_inc(c_hot, 1)
            dve.wait_ge(c_listed, NE * (NT // TG))
            pairs = m_list[:].rearrange("p e (c k) -> p e c k", k=2)
            step(nc.vector.tensor_copy(index[:], pairs[:, :, :, 1]))
            step(nc.vector.scalar_tensor_tensor(chosen[:], pairs[:, :, :, 0], float(P), index[:], ALU.mult, ALU.add))


def experts(nc, io, T, ctx, sem, passed, chosen, d_xg):
    def sb(name, shape, dt=F32):
        return ctx.enter_context(nc.sbuf_tensor("e_" + name, shape, dt))

    def ps(name, shape):
        return ctx.enter_context(nc.psum_tensor("e_ps_" + name, shape, F32))

    ident = sb("ident", [P, P])
    w1, w2 = sb("w1", [P, 2, HC, DFF]), sb("w2", [P, 2, FC, H])
    b1, b2 = sb("b1", [P, NE, FC]), sb("b2", [P, 2, H])
    index, gate = sb("index", [P, 2, CT], U32), sb("gate", [P, 2, CT])
    rows, rowsT = sb("rows", [P, 2, CT, XG]), sb("rowsT", [P, HC, TOPK])
    hidden = sb("hidden", [P, FC, TOPK])
    result = sb("result", [P, 2, CT, H])
    m_turn, m_1, m_2 = ps("m_turn", [P, HC, TOPK]), ps("m_1", [P, 2, TOPK]), ps("m_2", [P, 2, H * 2])
    const_in = sem("e_const_in")
    w_in = [sem(f"e_w_in{u}") for u in range(2)]
    rows_in = [sem(f"e_rows_in{u}") for u in range(2)]
    (picked, gated, turn_done, turnA, turnD, one_done, one_kept, two_done, two_kept, ready, added) = (
        sem("e_" + n) for n in ("picked", "gated", "turn_done", "turnA", "turnD", "one_done", "one_kept",
                                "two_done", "two_kept", "ready", "added"))
    out_rows = io["out"].rearrange("b s o -> (b s) o")
    W = 3

    with nc.Block() as block:
        @block.sync
        def _(sp):
            sp.dma_start(ident[:], io["ident"]).then_inc(const_in, 16)
            sp.dma_start(b1[:], io["b1T"]).then_inc(const_in, 16)

            def load(e, u):
                sp.dma_start(w1[:, u], io["w1"][e].rearrange("(c p) f -> p c f", p=P)).then_inc(w_in[u], 16)
                sp.dma_start(w2[:, u], io["w2"][e].rearrange("(c p) o -> p c o", p=P)).then_inc(w_in[u], 16)
                sp.dma_start(b2[:, u], io["b2"][e].partition_broadcast(P)).then_inc(w_in[u], 16)

            load(0, 0)
            load(1, 1)

            def body(i, last):
                for u in range(2):
                    if not last:
                        settled(sp, ready, CT * (2 * i + u + 1), passed)
                        load(2 * i + u + 2, u)

            peeled(sp, NE // 2, body)

        @block.gpsimd
        def _(pool):
            def gather(e, i, u):
                settled(pool, picked, e + 1, passed)
                for c in range(CT):
                    nc.gpsimd.indirect_dma_start(
                        out=rows[:, u, c], out_offset=None, in_=d_xg,
                        in_offset=bass.IndirectOffsetOnAxis(ap=index[:, u, c:c + 1], axis=0)
                    ).then_inc(rows_in[u], 16)

            def add_to_out(e, u):
                for c in range(CT):
                    settled(pool, ready, CT * e + c + 1, passed)
                    nc.gpsimd.indirect_dma_start(
                        out=out_rows, out_offset=bass.IndirectOffsetOnAxis(ap=index[:, u, c:c + 1], axis=0),
                        in_=result[:, u, c], in_offset=None, compute_op=ALU.add).then_inc(added, 16)
                settled(pool, added, 16 * CT * (e + 1), passed)

            gather(0, 0, 0)

            def body(i, last):
                gather(2 * i + 1, i, 1)
                add_to_out(2 * i, 0)
                if not last:
                    gather(2 * i + 2, i + 1, 0)
                add_to_out(2 * i + 1, 1)

            peeled(pool, NE // 2, body)

        @block.tensor
        def _(pe):
            pe.wait_ge(const_in, 32)

            def body(i, last):
                for u in range(2):
                    e = 2 * i + u
                    after(pe, rows_in[u], 16 * CT * (i + 1))
                    for c in range(HC):
                        for t in range(CT):
                            mm = pe.transpose(m_turn[:, c, t * P:(t + 1) * P], rows[:, u, t, c * P:(c + 1) * P],
                                              ident[:])
                        mm.then_inc(turn_done, 1)
                    after(pe, w_in[u], 16 * W * (i + 1))
                    after(pe, turnA, e + 1)
                    after(pe, turnD, e + 1)
                    for f in range(FC):
                        after(pe, one_kept, FC * e + f - 1)
                        for c in range(HC):
                            mm = pe.matmul(m_1[:, f % 2], w1[:, u, c, f * P:(f + 1) * P], rowsT[:, c],
                                           start=(c == 0), stop=(c == HC - 1))
                        mm.then_inc(one_done, 1)
                    after(pe, one_kept, FC * (e + 1))
                    for t in range(CT):
                        after(pe, two_kept, CT * e + t - 1)
                        for f in range(FC):
                            mm = pe.matmul(m_2[:, t % 2, 0:H], hidden[:, f, t * P:(t + 1) * P], w2[:, u, f],
                                           start=(f == 0), stop=(f == FC - 1))
                        mm.then_inc(two_done, 1)

            peeled(pe, NE // 2, body)

        @block.scalar
        def _(act):
            act.wait_ge(const_in, 32)

            def body(i, last):
                for u in range(2):
                    e = 2 * i + u
                    after(act, turn_done, HC * e + 1)
                    nc.scalar.activation(rowsT[:, 0], m_turn[:, 0], ACT.Identity).then_inc(turnA, 1)
                    after(act, two_done, CT * e)
                    for f in range(FC):
                        after(act, one_done, FC * e + f + 1)
                        nc.scalar.activation(hidden[:, f], m_1[:, f % 2], ACT.Relu,
                                             bias=b1[:, e, f:f + 1]).then_inc(one_kept, 1)

            body(0, False)
            for i in range(1, NE // 2):
                body(i, i == NE // 2 - 1)

        @block.vector
        def _(dve):
            def pick(e, u):
                if not (isinstance(e, int) and e < 2):
                    after(dve, added, 16 * CT * (e - 1))
                nc.vector.tensor_copy(index[:, u], chosen[:, e]).then_inc(picked, 1)

            def body(i, last):
                for u in range(2):
                    e = 2 * i + u
                    if not (last and u == 1):
                        pick(e + 1, 1 - u)
                    after(dve, turn_done, HC * e + 2)
                    nc.vector.tensor_copy(rowsT[:, 1], m_turn[:, 1]).then_inc(turnD, 1)
                    nc.vector.tensor_copy(gate[:, u], rows[:, u, :, H + e]).then_inc(gated, 1)
                    after(dve, gated, e + 1)
                    for t in range(CT):
                        after(dve, two_done, CT * e + t + 1)
                        nc.vector.tensor_tensor(result[:, u, t], m_2[:, t % 2, 0:H], b2[:, u], ALU.add
                                                ).then_inc(two_kept, 1)
                        after(dve, two_kept, CT * e + t + 1)
                        nc.vector.tensor_scalar(result[:, u, t], result[:, u, t], gate[:, u, t:t + 1], None,
                                                ALU.mult).then_inc(ready, 1)

            pick(0, 0)
            body(0, False)
            for i in range(1, NE // 2):
                body(i, i == NE // 2 - 1)
            dve.wait_ge(added, 16 * CT * NE)


def distances():
    d = np.arange(1 - S, S)
    mid, reach = SPAN // 2, NP
    a = np.abs(d).astype(np.float64)
    far = np.ceil(np.log(np.maximum(a, 1) / mid) / np.log((reach - 1) / mid) * (mid - 1) - 1e-6) + mid
    bucket = np.where(a <= mid, d, far * np.sign(d)).astype(np.int64)
    return np.clip(bucket + SPAN, 0, NP - 1)


def shape_constants(B):
    row = distances()
    low, high = row[0], row[-1]
    assert (row[:S - TLOW] == low).all() and (row[S - 2 + TLOW:] == high).all()
    pick = np.zeros((P, 2, TW), np.float32)
    for x in range(TW):
        d = x - TLOW
        for w, at in ((0, TW - 1 - x), (1, x)):
            pick[row[d + S - 1], w, at] += 1
            pick[low, w, at] -= 1
    ends = np.zeros((P, 2), np.float32)
    ends[low, 0] = ends[high, 1] = 1
    p = np.arange(P)
    own = np.zeros((P, HC, NH), np.float32)
    for c in range(HC):
        own[p, c, (c * P + p) // HD] = 1
    place = np.stack([np.broadcast_to(np.arange(B * QT, dtype=np.float32), (P, B * QT)),
                      np.broadcast_to(p[:, None].astype(np.float32), (P, B * QT))], 1)
    return {"pick": pick, "ends": ends, "own": own, "ident": np.eye(P, dtype=np.float32),
            "past": np.stack([p[None, :] <= p[:, None], p[None, :] >= p[:, None]], 1).astype(np.float32),
            "before": (p[:, None] < p[None, :]).astype(np.float32),
            "iota": np.ascontiguousarray(np.broadcast_to(p.astype(np.float32), (P, P))),
            "place": np.ascontiguousarray(place)}


def kernel(**inputs):
    import concourse.bacc as bacc
    from concourse.bass_utils import run_bass_kernel_spmd

    g = {k.replace("L0_", "").replace("attn_", "").replace("ffn_", ""): np.asarray(v) for k, v in inputs.items()}
    B = g["x"].shape[0]
    turn = np.ascontiguousarray
    arrays = {
        "xT": turn(g["x"].transpose(0, 3, 2, 1)),
        "tok_weight": turn(g["tok_weight"].T), "wsT": turn(g["tok_weighted_sum"].T),
        "bq_col": turn(g["bq"].reshape(HC, P).T), "bk_col": turn(g["bk"].reshape(HC, P).T),
        "b1T": turn(g["b1"].reshape(NE, FC, P).transpose(2, 0, 1)),
        **{k: turn(g[k]) for k in ("Wq", "Wk", "Wv", "Wo", "Wpk", "Wpq", "bv", "bo", "bpk", "bpq", "rel_emb",
                                   "ln_g", "ln_b", "router_w", "router_b", "w1", "w2", "b2")},
        **shape_constants(B),
    }
    nc = bacc.Bacc("TRN2", target_bir_lowering=False, num_devices=1)
    io = {k: nc.dram_tensor("in_" + k, a.shape, mybir.dt.from_np(a.dtype), kind="ExternalInput").ap()
          for k, a in arrays.items()}
    io["out"] = nc.dram_tensor("out", (B, S, H), F32, kind="ExternalOutput").ap()
    build(nc, io, B)
    result = run_bass_kernel_spmd(nc, [{"in_" + k: a for k, a in arrays.items()}], core_ids=[0])
    return result.results[0]["out"]
```

```python
from contextlib import ExitStack

import numpy as np
import concourse.bass as bass
from concourse import mybir

F32 = mybir.dt.float32
BF16 = mybir.dt.bfloat16
I32 = mybir.dt.int32
U32 = mybir.dt.uint32
ALU = mybir.AluOpType
ACT = mybir.ActivationFunctionType
AX = mybir.AxisListType

P = 128
S = 512
H = 256
ND = 4
NH = 16
HD = H // NH
QT = S // P
HC = H // P
SPAN = 64
NP = 2 * SPAN
DFF = 1024
NE = 8
TOPK = 512
FC = DFF // P
CT = TOPK // P
EPS = 1e-5
SCALE = float(1.0 / np.sqrt(np.float32(HD * 3)))

TLOW = P
TW = 2 * TLOW
PITCH = 4 * P
NEAR = 3 * P
AHEAD = 4
SLOTS = 6
SIDE_A = (0, 0, 1, 0, 2, 1)
SIDE_B = (0, 1, 0, 2, 0, 1)
ST = SLOTS * HD
PLAIN = 3
KW = S + S // 2
SW = S + KW
RING = 4
LEAD = 4
NEXT = 2
SH = 2
SR = 4
GH = 4
NG = NH // GH
NS = NH // SH
VROW = HD + 1
CROW = 32
XG = H + NE
BITS = 30


def after(eng, sem, count):
    if not isinstance(count, int) or count > 0:
        eng.wait_ge(sem, count)


def settled(eng, sem, count, passed):
    after(eng, sem, count)
    if not isinstance(count, int):
        eng.sem_inc(passed, 1)


def peeled(eng, steps, body):
    body(0, steps == 1)
    if steps > 2:
        with eng.Fori(1, steps - 1, 1) as i:
            body(i, False)
    if steps > 1:
        body(steps - 1, True)


def build(nc, io, B):
    T = B * S
    NT = T // P
    with ExitStack() as top:
        def sem(name):
            return top.enter_context(nc.semaphore(name))

        def dram(name, shape, dt=F32):
            return nc.dram_tensor(name, shape, dt).ap()

        passed = sem("passed")
        d_tab = dram("d_tab", (2, 3, H, TW), BF16)
        d_stack = dram("d_stack", (B, SLOTS, H, SW), BF16)
        d_plain = dram("d_plain", (PLAIN, NH, TW), BF16)
        d_kterm = dram("d_kterm", (B, 3, NH, KW), BF16)
        d_v = dram("d_v", (B, S, NH * VROW))
        d_h = dram("d_h", (B, S, H))
        d_skew = dram("d_skew", (RING, 2, QT, P, PITCH))
        d_ctx = dram("d_ctx", (B, NG, P, S))
        d_share = dram("d_share", (B, NH, S))
        d_xg = dram("d_xg", (T, XG))
        d_scores = dram("d_scores", (P, NE, NT))
        d_floor = dram("d_floor", (P, 2))

        with ExitStack() as ctx:
            project(nc, io, B, ctx, sem, passed, d_tab, d_plain, d_stack, d_kterm, d_v, d_h)
        with ExitStack() as ctx:
            attend(nc, io, B, ctx, sem, passed, d_tab, d_plain, d_stack, d_kterm, d_v, d_skew, d_ctx)
        with ExitStack() as ctx:
            scores = ctx.enter_context(nc.sbuf_tensor("scores", [P, NE, NT], F32))
            with ExitStack() as inner:
                output(nc, io, B, inner, sem, passed, scores, d_h, d_ctx, d_share, d_xg)
            chosen = ctx.enter_context(nc.sbuf_tensor("chosen", [P, NE, CT], U32))
            w1, w2, b2 = (ctx.enter_context(nc.sbuf_tensor(name, shape, F32)) for name, shape in (
                ("w1", [P, 2, HC, DFF]), ("w2", [P, 2, FC, H]), ("b2", [P, 2, H])))
            w_in = [sem(f"e_w_in{u}") for u in range(2)]

            def load_expert(sp, e, u):
                sp.dma_start(w1[:, u], io["w1"][e].rearrange("(c p) f -> p c f", p=P)).then_inc(w_in[u], 16)
                sp.dma_start(w2[:, u], io["w2"][e].rearrange("(c p) o -> p c o", p=P)).then_inc(w_in[u], 16)
                sp.dma_start(b2[:, u], io["b2"][e].partition_broadcast(P)).then_inc(w_in[u], 16)

            with ExitStack() as inner:
                choose(nc, io, NT, inner, sem, passed, scores, chosen, d_scores, d_floor, load_expert)
            with ExitStack() as inner:
                experts(nc, io, T, inner, sem, passed, chosen, d_xg, w1, w2, b2, w_in, load_expert)


def project(nc, io, B, ctx, sem, passed, d_tab, d_plain, d_stack, d_kterm, d_v, d_h):
    def sb(name, shape, dt=F32):
        return ctx.enter_context(nc.sbuf_tensor("p_" + name, shape, dt))

    def ps(name, shape):
        return ctx.enter_context(nc.psum_tensor("p_ps_" + name, shape, F32))

    mix = sb("mix", [P, ND * HC, H])
    ident = sb("ident", [P, P])
    wq, wk, wv = (sb(n, [P, HC, H]) for n in ("wq", "wk", "wv"))
    bv_row = sb("bv_row", [P, H])
    qk_bias = sb("qk_bias", [P, 4, HC])
    kterm_w = sb("kterm_w", [P, HC, 2 * NH])
    kterm_bias = sb("kterm_bias", [2 * NH, 1])
    minus_half = sb("minus_half", [P, QT])
    xt = sb("xt", [P, 2, ND * HC, S])
    xT = io["xT"]
    x_in = [sem(f"p_x_in{u}") for u in range(2)]

    with ExitStack() as tctx:
        def tsb(name, shape, dt=F32):
            return tctx.enter_context(nc.sbuf_tensor("t_" + name, shape, dt))

        def tps(name, shape):
            return tctx.enter_context(nc.psum_tensor("t_ps_" + name, shape, F32))

        ws = tsb("ws", [P, HC, H])
        wd = tsb("wd", [P, ND, H])
        rel = tsb("rel", [P, H])
        lng, lnb = tsb("lng", [P, H]), tsb("lnb", [P, H])
        wp = tsb("wp", [P, 2, HC, H])
        bp = tsb("bp", [P, 2, H])
        pick = tsb("pick", [P, 2, TW])
        ends = tsb("ends", [P, 2])
        own = tsb("own", [P, HC, NH])
        stats, moments = tsb("stats", [P, 6]), tsb("moments", [P, 2])
        rstd, relT, pos = tsb("rstd", [P, 2]), tsb("relT", [P, HC, P]), tsb("pos", [P, 2, H])
        rest = tsb("rest", [P, 2, HC, TW])
        parts = tsb("parts", [P, 2, HC, 3, TW], BF16)
        consts = tsb("consts", [P, 2, HC, 2])
        own_low = tsb("own_low", [P, HC, NH])
        tab_q = tsb("tab_q", [P, HC, TW])
        plain = tsb("plain", [NH, TW])
        plain_parts = tsb("plain_parts", [NH, PLAIN, TW], BF16)
        t_turn = tps("turn", [P, S])
        t_pos = tps("pos", [P, 2, H])
        t_tab = tps("tab", [P, 2 * HC, S])
        t_end = tps("end", [P, 2, HC, 2])
        t_low = tps("low", [2 * NH, 2 * TW])
        t_in, t_const, t_dve, t_pe, t_pool, t_out = (
            sem("t_" + n) for n in ("in", "const", "dve", "pe", "pool", "out"))
        loads = [
            (ws, io["wsT"].rearrange("(c p) o -> p c o", p=P)),
            (wd, io["tok_weight"].partition_broadcast(P)),
            (rel, io["rel_emb"]), (lng, io["ln_g"].partition_broadcast(P)),
            (lnb, io["ln_b"].partition_broadcast(P)),
            (wp[:, 0], io["Wpk"].rearrange("(c p) o -> p c o", p=P)),
            (wp[:, 1], io["Wpq"].rearrange("(c p) o -> p c o", p=P)),
            (bp[:, 0], io["bpk"].partition_broadcast(P)),
            (bp[:, 1], io["bpq"].partition_broadcast(P)),
            (pick, io["pick"]), (ends, io["ends"]), (own, io["own"]), (ident, io["ident"]),
            (wq, io["Wq"].rearrange("(c p) o -> p c o", p=P)),
            (wk, io["Wk"].rearrange("(c p) o -> p c o", p=P)),
            (wv, io["Wv"].rearrange("(c p) o -> p c o", p=P)),
            (bv_row, io["bv"].partition_broadcast(P)),
            (qk_bias[:, 0], io["bq_col"]), (qk_bias[:, 1], io["bk_col"]),
        ]
        with nc.Block() as block:
            @block.sync
            def _(sp):
                for dst, src in loads:
                    sp.dma_start(dst[:], src).then_inc(t_in, 16)
                for u in range(2):
                    sp.dma_start(xt[:, u], xT[u].rearrange("d (c p) s -> p (d c) s", p=P)).then_inc(x_in[u], 16)
                sp.wait_ge(t_dve, 26)
                for w in range(2):
                    for c in range(HC):
                        sp.dma_start(d_tab[w, :, c * P:(c + 1) * P, :].rearrange("t p x -> p t x"),
                                     parts[:, w, c]).then_inc(t_out, 16)
                sp.dma_start(d_plain.rearrange("t h x -> h t x"), plain_parts[:]).then_inc(t_out, 16)
                sp.wait_ge(t_out, 16 * (2 * HC + 1))

            @block.gpsimd
            def _(pool):
                nc.gpsimd.memset(minus_half[:], -0.5).then_inc(t_const, 1)
                pool.wait_ge(t_const, 1)
                pool.wait_ge(t_dve, 3)
                nc.gpsimd.tensor_tensor(rstd[:, 1:2], rstd[:, 0:1], minus_half[:, 0:1],
                                        ALU.pow).then_inc(t_pool, 1)

            @block.vector
            def _(dve):
                done = [0]

                def step(ins, wait=True):
                    done[0] += 1
                    ins.then_inc(t_dve, 1)
                    if wait:
                        dve.wait_ge(t_dve, done[0])

                dve.wait_ge(t_in, 16 * len(loads))
                step(nc.vector.bn_stats(stats[:], rel[:]))
                step(nc.vector.bn_aggr(moments[:], stats[:]))
                step(nc.vector.tensor_scalar_add(rstd[:, 0:1], moments[:, 1:2], EPS))
                for d in range(ND):
                    for c in range(HC):
                        nc.vector.tensor_tensor(mix[:, d * HC + c], ws[:, c], wd[:, d], ALU.mult)
                dve.wait_ge(t_pool, 1)
                step(nc.vector.tensor_scalar(rel[:], rel[:], moments[:, 0:1], rstd[:, 1:2],
                                             ALU.subtract, ALU.mult))
                step(nc.vector.tensor_tensor(rel[:], rel[:], lng[:], ALU.mult))
                step(nc.vector.tensor_tensor(rel[:], rel[:], lnb[:], ALU.add))
                dve.wait_ge(t_pe, 1)
                step(nc.vector.tensor_copy(relT[:], t_turn[:, 0:HC * P].rearrange(
                    "p (c q) -> p c q", c=HC)))
                dve.wait_ge(t_pe, 2)
                step(nc.vector.tensor_tensor(pos[:], t_pos[:], bp[:], ALU.add))
                dve.wait_ge(t_pe, 3)
                step(nc.vector.tensor_copy(consts[:], t_end[:]))
                tab = t_tab[:, :, 0:TW].rearrange("p (w c) x -> p w c x", w=2)
                step(nc.vector.tensor_copy(parts[:, :, :, 0], tab))
                step(nc.vector.tensor_tensor(rest[:], tab, parts[:, :, :, 0], ALU.subtract))
                step(nc.vector.tensor_copy(parts[:, :, :, 1], rest[:]))
                step(nc.vector.tensor_tensor(rest[:], rest[:], parts[:, :, :, 1], ALU.subtract))
                step(nc.vector.tensor_copy(parts[:, :, :, 2], rest[:]))
                for side in range(2):
                    step(nc.vector.tensor_tensor(qk_bias[:, 2 + side], qk_bias[:, 1],
                                                 consts[:, 0, :, side], ALU.add))
                for c in range(HC):
                    for side in range(2):
                        ins = nc.vector.tensor_scalar(
                            kterm_w[:, c, side * NH:(side + 1) * NH], own[:, c],
                            consts[:, 1, c, side:side + 1], None, ALU.mult)
                step(ins)
                for c in range(HC):
                    ins = nc.vector.tensor_scalar(own_low[:, c], own[:, c], consts[:, 0, c, 0:1], None, ALU.mult)
                step(ins)
                step(nc.vector.tensor_copy(tab_q[:], tab[:, 1]))
                dve.wait_ge(t_pe, 4)
                step(nc.vector.tensor_scalar(kterm_bias[:], t_low[:, TW:TW + 1], -1.0, None, ALU.mult))
                step(nc.vector.tensor_scalar(plain[:], t_low[0:NH, 0:TW], -1.0, None, ALU.mult))
                step(nc.vector.tensor_copy(plain_parts[:, 0], plain[:]))
                step(nc.vector.tensor_tensor(plain[:], plain[:], plain_parts[:, 0], ALU.subtract))
                step(nc.vector.tensor_copy(plain_parts[:, 1], plain[:]))
                step(nc.vector.tensor_tensor(plain[:], plain[:], plain_parts[:, 1], ALU.subtract))
                step(nc.vector.tensor_copy(plain_parts[:, 2], plain[:]))

            @block.tensor
            def _(pe):
                pe.wait_ge(t_dve, 6)
                for c in range(HC):
                    mm = pe.transpose(t_turn[:, c * P:(c + 1) * P], rel[:, c * P:(c + 1) * P], ident[:])
                mm.then_inc(t_pe, 1)
                pe.wait_ge(t_dve, 7)
                for w in range(2):
                    for c in range(HC):
                        mm = pe.matmul(t_pos[:, w], relT[:, c], wp[:, w, c], start=(c == 0),
                                       stop=(c == HC - 1))
                mm.then_inc(t_pe, 1)
                pe.wait_ge(t_dve, 8)
                for w in range(2):
                    for c in range(HC):
                        of = pos[:, w, c * P:(c + 1) * P]
                        pe.matmul(t_end[:, w, c], of, ends[:], start=True, stop=True)
                        mm = pe.matmul(t_tab[:, w * HC + c, 0:TW], of, pick[:, w], start=True, stop=True)
                mm.then_inc(t_pe, 1)
                pe.wait_ge(t_dve, 19)
                for c in range(HC):
                    pe.matmul(t_low[0:NH, 0:TW], own_low[:, c], tab_q[:, c], start=(c == 0), stop=(c == HC - 1))
                for c in range(HC):
                    mm = pe.matmul(t_low[:, TW:TW + 1], kterm_w[:, c], consts[:, 0, c, 0:1], start=(c == 0),
                                   stop=(c == HC - 1))
                mm.then_inc(t_pe, 1)

    h_sb = sb("h_sb", [P, 2, QT, H])
    stats = sb("stats", [P, QT, 6])
    moments = sb("moments", [P, QT, 2])
    var_eps, rstd = sb("var_eps", [P, QT]), sb("rstd", [P, QT])
    xn = sb("xn", [P, QT, H])
    xnT = sb("xnT", [P, HC, S])
    full_q = sb("full_q", [P, HC, S])
    full_k = sb("full_k", [P, HC, KW])
    rest_q, rest_k = sb("rest_q", [P, HC, S]), sb("rest_k", [P, HC, KW])
    part_q = sb("part_q", [P, 2, 3, HC, S], BF16)
    part_k = sb("part_k", [P, 2, 3, HC, KW], BF16)
    full_t = sb("full_t", [2 * NH, S])
    part_t = sb("part_t", [2 * NH, 3, S], BF16)
    v_sb = sb("v_sb", [P, QT, NH, VROW])
    m_h = ps("m_h", [P, QT, H])
    m_turn = ps("m_turn", [P, HC, S])
    m_qk = ps("m_qk", [P, 2, S])
    m_v = ps("m_v", [P, 2, H])
    m_t = ps("m_t", [2 * NH, S])
    (h_done, h_kept, st_done, mo_done, ve_done, rs_done, xn_done, turn_done, turnA, turnD,
     qk_done, qk_kept, t_done, t_kept, low_done, mid_done, parts_done, v_done, v_kept,
     v_const) = (sem("p_" + n) for n in (
         "h_done", "h_kept", "st_done", "mo_done", "ve_done", "rs_done", "xn_done", "turn_done",
         "turnA", "turnD", "qk_done", "qk_kept", "t_done", "t_kept", "low_done", "mid_done",
         "parts_done", "v_done", "v_kept", "v_const"))
    h_out = [sem(f"p_h_out{u}") for u in range(2)]
    v_out, t_out = sem("p_v_out"), sem("p_t_out")
    parts_out = [sem(f"p_parts_out{u}") for u in range(2)]
    DMAS = 2 * SLOTS
    CH = 2 * HC
    pairs = B // 2

    with nc.Block() as block:
        @block.sync
        def _(sp):
            def body(i, last):
                for u in range(2):
                    n = 2 * i + u
                    if not last:
                        settled(sp, h_done, 2 * (n + 1), passed)
                        sp.dma_start(xt[:, u], xT[n + 2].rearrange("d (c p) s -> p (d c) s", p=P)
                                     ).then_inc(x_in[u], 16)
                    settled(sp, h_kept, 2 * (n + 1), passed)
                    sp.dma_start(d_h[n].rearrange("(t p) o -> p t o", p=P), h_sb[:, u]).then_inc(h_out[u], 16)
                    settled(sp, v_kept, 2 * (n + 1), passed)
                    sp.dma_start(d_v[n].rearrange("(t p) o -> p t o", p=P),
                                 v_sb[:].rearrange("p t h r -> p t (h r)")).then_inc(v_out, 16)
                    settled(sp, parts_done, (CH + 1) * (n + 1), passed)
                    for j in range(SLOTS):
                        to = d_stack[n, j].rearrange("(c p) x -> p c x", p=P)
                        sp.dma_start(to[:, :, 0:S], part_q[:, u, SIDE_A[j]]).then_inc(parts_out[u], 16)
                        sp.dma_start(to[:, :, S:SW], part_k[:, u, SIDE_B[j]]).then_inc(parts_out[u], 16)
                    to = d_kterm[n].rearrange("t h x -> h t x")
                    sp.dma_start(to[:, :, 0:S], part_t[0:NH]).then_inc(t_out, 16)
                    sp.dma_start(to[:, :, S:], part_t[NH:, :, 0:KW - S]).then_inc(t_out, 16)

            peeled(sp, pairs, body)
            sp.wait_ge(v_out, 16 * B)
            sp.wait_ge(t_out, 32 * B)
            for u in range(2):
                sp.wait_ge(parts_out[u], 16 * DMAS * pairs)
                sp.wait_ge(h_out[u], 16 * pairs)

        @block.tensor
        def _(pe):
            def mixing(n, i, u, t):
                if t == 0:
                    after(pe, x_in[u], 16 * (i + 1))
                if t % 2 == 0:
                    after(pe, h_kept, 2 * (n - 1) + t // 2 + 1 if not isinstance(n, int) or n else 0)
                for k in range(ND * HC):
                    mm = pe.matmul(m_h[:, t], xt[:, u, k, t * P:(t + 1) * P], mix[:, k],
                                   start=(k == 0), stop=(k == ND * HC - 1))
                if t % 2:
                    mm.then_inc(h_done, 1)

            def turn(n):
                after(pe, xn_done, n + 1)
                after(pe, turnA, n)
                after(pe, turnD, n)
                for c in range(HC):
                    for t in range(QT):
                        mm = pe.transpose(m_turn[:, c, t * P:(t + 1) * P], xn[:, t, c * P:(c + 1) * P], ident[:])
                    mm.then_inc(turn_done, 1)

            def project_qk(n, m):
                if m == 0:
                    after(pe, turnA, n + 1)
                    after(pe, turnD, n + 1)
                after(pe, qk_kept, CH * n + m - 1)
                w = (wq, wk)[m // HC]
                for c in range(HC):
                    mm = pe.matmul(m_qk[:, m % 2], w[:, c, (m % HC) * P:(m % HC + 1) * P], xnT[:, c],
                                   start=(c == 0), stop=(c == HC - 1))
                mm.then_inc(qk_done, 1)

            def key_terms(n):
                after(pe, qk_kept, CH * (n + 1))
                after(pe, t_kept, n)
                for c in range(HC):
                    mm = pe.matmul(m_t[:], kterm_w[:, c], full_k[:, c, 0:S], start=(c == 0), stop=(c == HC - 1))
                mm.then_inc(t_done, 1)

            def project_v(n):
                for half in range(2):
                    after(pe, v_kept, 2 * n + half)
                    for t in range(2):
                        at = (2 * half + t) * P
                        for c in range(HC):
                            mm = pe.matmul(m_v[:, t], xnT[:, c, at:at + P], wv[:, c], start=(c == 0),
                                           stop=(c == HC - 1))
                    mm.then_inc(v_done, 1)

            def batch(n, i, u, more):
                turn(n)
                for t in range(QT):
                    if more:
                        mixing(n + 1, i + u, 1 - u, t)
                    if t == 0:
                        project_qk(n, 0)
                        project_qk(n, 1)
                    elif t < QT - 1:
                        project_qk(n, t + 1)
                key_terms(n)
                project_v(n)

            for t in range(QT):
                mixing(0, 0, 0, t)

            def body(i, last):
                batch(2 * i, i, 0, True)
                batch(2 * i + 1, i, 1, not last)

            peeled(pe, pairs, body)

        @block.scalar
        def _(act):
            def keep_h(n, i, u, half):
                if half == 0 and not (isinstance(n, int) and n < 2):
                    after(act, h_out[u], 16 * i)
                    after(act, xn_done, n - 1)
                after(act, h_done, 2 * n + half + 1)
                nc.scalar.activation(h_sb[:, u, 2 * half:2 * half + 2], m_h[:, 2 * half:2 * half + 2],
                                     ACT.Identity).then_inc(h_kept, 1)

            def keep_turned(n):
                after(act, turn_done, HC * n + 1)
                nc.scalar.activation(xnT[:, 0], m_turn[:, 0], ACT.Identity).then_inc(turnA, 1)

            def keep_qk(n, i, u, m):
                c = m % HC
                if m == 0:
                    after(act, parts_out[u], 16 * DMAS * i)
                if m == HC:
                    after(act, t_done, n)
                after(act, qk_done, CH * n + m + 1)
                after(act, low_done, (CH + 1) * (n - 1) + m + 1 if not isinstance(n, int) or n else 0)
                src = m_qk[:, m % 2]
                if m < HC:
                    nc.scalar.activation(full_q[:, c], src, ACT.Identity, bias=qk_bias[:, 0, c:c + 1])
                    ins = nc.scalar.activation(part_q[:, u, 0, c], src, ACT.Identity,
                                               bias=qk_bias[:, 0, c:c + 1])
                else:
                    for out in (full_k[:, c], part_k[:, u, 0, c]):
                        nc.scalar.activation(out[:, 0:S], src, ACT.Identity, bias=qk_bias[:, 2, c:c + 1])
                        ins = nc.scalar.activation(out[:, S:], src[:, 0:KW - S], ACT.Identity,
                                                   bias=qk_bias[:, 3, c:c + 1])
                ins.then_inc(qk_kept, 1)

            def keep_terms(n):
                after(act, t_done, n + 1)
                after(act, parts_done, (CH + 1) * n)
                after(act, t_out, 32 * n)
                nc.scalar.activation(full_t[:], m_t[:], ACT.Identity, bias=kterm_bias[:])
                nc.scalar.activation(part_t[:, 0], m_t[:], ACT.Identity, bias=kterm_bias[:]).then_inc(t_kept, 1)

            def batch(n, i, u, more):
                keep_turned(n)
                keep_qk(n, i, u, 0)
                keep_qk(n, i, u, 1)
                if more:
                    keep_h(n + 1, i + u, 1 - u, 0)
                keep_qk(n, i, u, 2)
                keep_qk(n, i, u, 3)
                if more:
                    keep_h(n + 1, i + u, 1 - u, 1)
                keep_terms(n)

            keep_h(0, 0, 0, 0)
            keep_h(0, 0, 0, 1)

            def body(i, last):
                batch(2 * i, i, 0, True)
                batch(2 * i + 1, i, 1, not last)

            peeled(act, pairs, body)

        @block.gpsimd
        def _(pool):
            nc.gpsimd.memset(v_sb[:, :, :, HD:HD + 1], 1.0).then_inc(v_const, 1)

            def power(n):
                after(pool, ve_done, n + 1)
                nc.gpsimd.tensor_tensor(rstd[:], var_eps[:], minus_half[:], ALU.pow).then_inc(rs_done, 1)

            def lower(n, u, m):
                c = m % HC
                after(pool, qk_kept, CH * n + m + 1)
                after(pool, parts_done, (CH + 1) * (n - 1) + m + 1 if not isinstance(n, int) or n else 0)
                left, full, part = ((rest_q[:, c], full_q[:, c], part_q[:, u, 0, c]) if m < HC else
                                    (rest_k[:, c], full_k[:, c], part_k[:, u, 0, c]))
                nc.gpsimd.tensor_tensor(left, full, part, ALU.subtract).then_inc(low_done, 1)

            def batch(n, u, more):
                for m in range(CH):
                    lower(n, u, m)
                if more:
                    power(n + 1)
                after(pool, t_kept, n + 1)
                nc.gpsimd.tensor_tensor(full_t[:], full_t[:], part_t[:, 0], ALU.subtract).then_inc(low_done, 1)

            power(0)

            def body(i, last):
                batch(2 * i, 0, True)
                batch(2 * i + 1, 1, not last)

            peeled(pool, pairs, body)

        @block.vector
        def _(dve):
            def moments_of(n, u, half):
                for t in (2 * half, 2 * half + 1):
                    after(dve, h_kept, 2 * n + half + 1)
                    nc.vector.bn_stats(stats[:, t], h_sb[:, u, t]).then_inc(st_done, 1)

            def spread_of(n):
                settled(dve, st_done, QT * (n + 1), passed)
                for t in range(QT):
                    nc.vector.bn_aggr(moments[:, t], stats[:, t]).then_inc(mo_done, 1)
                after(dve, mo_done, QT * (n + 1))
                nc.vector.tensor_scalar_add(var_eps[:], moments[:, :, 1], EPS).then_inc(ve_done, 1)

            def norm(n, u):
                after(dve, rs_done, n + 1)
                after(dve, turn_done, HC * n)
                for t in range(QT):
                    ins = nc.vector.tensor_scalar(xn[:, t], h_sb[:, u, t], moments[:, t, 0:1], rstd[:, t:t + 1],
                                                  ALU.subtract, ALU.mult)
                ins.then_inc(xn_done, 1)

            def keep_turned(n):
                after(dve, turn_done, HC * n + 2)
                nc.vector.tensor_copy(xnT[:, 1], m_turn[:, 1]).then_inc(turnD, 1)

            def keep_v(n, half):
                after(dve, v_done, 2 * n + half + 1)
                if half == 0:
                    after(dve, v_out, 16 * n)
                nc.vector.tensor_tensor(
                    v_sb[:, 2 * half:2 * half + 2, :, 0:HD],
                    m_v[:].rearrange("p t (h d) -> p t h d", d=HD),
                    bv_row[:].rearrange("p (h d) -> p h d", d=HD).unsqueeze(1).to_broadcast([P, 2, NH, HD]),
                    ALU.add).then_inc(v_kept, 1)

            def split(n, u, m):
                c = m % HC
                after(dve, low_done, (CH + 1) * n + m + 1)
                if m < HC:
                    a, mid, low = rest_q[:, c], part_q[:, u, 1, c], part_q[:, u, 2, c]
                elif m < CH:
                    a, mid, low = rest_k[:, c], part_k[:, u, 1, c], part_k[:, u, 2, c]
                else:
                    a, mid, low = full_t[:], part_t[:, 1], part_t[:, 2]
                nc.vector.tensor_copy(mid, a).then_inc(mid_done, 1)
                after(dve, mid_done, (CH + 1) * n + m + 1)
                nc.vector.tensor_tensor(low, a, mid, ALU.subtract).then_inc(parts_done, 1)

            def batch(n, u, more):
                keep_turned(n)
                split(n, u, 0)
                split(n, u, 1)
                if more:
                    moments_of(n + 1, 1 - u, 0)
                split(n, u, 2)
                if more:
                    moments_of(n + 1, 1 - u, 1)
                    spread_of(n + 1)
                keep_v(n, 0)
                if more:
                    norm(n + 1, 1 - u)
                keep_v(n, 1)
                split(n, u, 3)
                split(n, u, CH)

            dve.wait_ge(v_const, 1)
            moments_of(0, 0, 0)
            moments_of(0, 0, 1)
            spread_of(0)
            norm(0, 0)

            def body(i, last):
                batch(2 * i, 0, True)
                batch(2 * i + 1, 1, not last)

            peeled(dve, pairs, body)


def attend(nc, io, B, ctx, sem, passed, d_tab, d_plain, d_stack, d_kterm, d_v, d_skew, d_ctx):
    def sb(name, shape, dt=F32):
        return ctx.enter_context(nc.sbuf_tensor("a_" + name, shape, dt))

    def ps(name, shape):
        return ctx.enter_context(nc.psum_tensor("a_ps_" + name, shape, F32))

    ident = sb("ident", [P, P])
    past = sb("past", [P, 2, P])
    tabs = sb("tabs", [ST + 3 + PLAIN, 2, NH, TW], BF16)
    stack = sb("stack", [ST + 3 + PLAIN, SR, SH, SW], BF16)
    skew_in = sb("skew_in", [P, 2, 2, QT, TW])
    bias = sb("bias", [P, AHEAD, 2, QT, S])
    beyond = sb("beyond", [P, 2, 2, QT - 1, P])
    scored = sb("scored", [P, 2, QT, S])
    top_of = sb("top_of", [P, 2, QT])
    shift = sb("shift", [P, 2, QT])
    probs = sb("probs", [P, 2, QT, S])
    probsT = sb("probsT", [P, QT, S])
    values = sb("values", [P, 2, QT, NH // 2, VROW])
    ctx_sb = sb("ctx_sb", [P, 2, S])
    m_tab = ps("m_tab", [P, 2, 2, TW])
    m_s = ps("m_s", [P, 2, S])
    m_t = ps("m_t", [P, 2, S])
    m_ctx = ps("m_ctx", [P, S])

    const_in, zeroed, zeroed_p, zero_out = (sem("a_" + n) for n in ("const_in", "zeroed", "zeroed_p", "zero_out"))
    stack_in = [sem(f"a_stack_in{u}") for u in range(SR)]
    values_in = [sem(f"a_values_in{u}") for u in range(2)]
    skew_out = [sem(f"a_skew_out{u}") for u in range(2)]
    bias_in = [sem(f"a_bias_in{u}") for u in range(AHEAD)]
    (tab_done, tab_c, tab_p, beyond_done, filled, s_done, s_kept, shifted, exp_done, turn_done, turnA, turnD,
     pv_done, ctx_kept, ctx_out) = (sem("a_" + n) for n in (
         "tab_done", "tab_c", "tab_p", "beyond_done", "filled", "s_done", "s_kept", "shifted", "exp_done",
         "turn_done", "turnA", "turnD", "pv_done", "ctx_kept", "ctx_out"))
    STACKS = SLOTS + 1
    HEADS = B * NH
    READS = 6
    TURN = 2
    scratch = d_skew.tensor
    plane = P * PITCH
    FIRST = P

    def early(b, hh, lag):
        return isinstance(b, int) and b == 0 and hh < lag

    with nc.Block() as block:
        @block.sync
        def _(sp):
            sp.dma_start(ident[:], io["ident"]).then_inc(const_in, 16)
            sp.dma_start(past[:], io["past"]).then_inc(const_in, 16)
            for w in range(2):
                for j in range(SLOTS):
                    part = (SIDE_B if w == 0 else SIDE_A)[j]
                    sp.dma_start(tabs[j * HD:(j + 1) * HD, w],
                                 d_tab[w, part].rearrange("(h d) x -> d h x", d=HD)).then_inc(const_in, 16)
            sp.wait_ge(zeroed_p, 2)
            sp.dma_start(tabs[ST + 3:, 1], d_plain).then_inc(const_in, 16)

            def load_stack(b, g):
                u = g % SR
                for j in range(SLOTS):
                    sp.dma_start(stack[j * HD:(j + 1) * HD, u],
                                 d_stack[b, j, g * SH * HD:(g + 1) * SH * HD].rearrange("(h d) x -> d h x", d=HD)
                                 ).then_inc(stack_in[u], 16)
                sp.dma_start(stack[ST:ST + 3, u, :, S:], d_kterm[b, :, g * SH:(g + 1) * SH]
                             ).then_inc(stack_in[u], 16)

            def load_values(b, half):
                sp.dma_start(values[:, half],
                             d_v[b].rearrange("(t p) x -> p t x", p=P)[
                                 :, :, half * NH // 2 * VROW:(half + 1) * NH // 2 * VROW]
                             .rearrange("p t (h r) -> p t h r", r=VROW)).then_inc(values_in[half], 16)

            def write_tables(n, hh):
                u, slot = hh % 2, hh % RING
                for kept in (tab_c, tab_p):
                    settled(sp, kept, 2 * (n + 1), passed)
                sp.dma_start(d_skew[slot].rearrange("w t p x -> p (w t) x")[:, :, FIRST:FIRST + TW],
                             skew_in[:, u].rearrange("p w t x -> p (w t) x")).then_inc(skew_out[u], 16)

            def read_tables(n, b, hh):
                u, v, slot = hh % 2, hh % AHEAD, hh % RING
                settled(sp, skew_out[u], 16 * (NH // 2 * b + hh // 2 + 1), passed)
                settled(sp, s_kept, QT * (n - AHEAD + 1), passed)
                for w in range(2):
                    base = (slot * 2 + w) * QT * plane + P - 1 + w
                    tile = bias[:, v, w, 0]
                    row = tile.ap[0][0]
                    short = ((0, P // 2, 0, NEAR - P // 2), (P // 2, P, 0, NEAR)) if w == 0 else (
                        (0, P // 2, 0, NEAR), (P // 2, P, P // 2, NEAR))
                    for at, to, skip, step, (p0, p1, x0, x1) in (
                            (0, (QT - 1) * S + (QT - 2) * P, P, (QT - 1) * plane - P, (0, P, 0, 2 * P)),
                            *((S, S + P, plane, plane, part) for part in short)):
                        sp.dma_start(bass.AP(tile.tensor, tile.offset + p0 * row + at + x0,
                                             [[row, p1 - p0], [to, 2], [1, x1 - x0]]),
                                     bass.AP(scratch, base + skip + p0 * (PITCH - 1) + x0,
                                             [[PITCH - 1, p1 - p0], [step, 2], [1, x1 - x0]])
                                     ).then_inc(bias_in[v], 16)

            def store_ctx(b, g):
                settled(sp, ctx_kept, NG * b + g + 1, passed)
                to = d_ctx[b, g] if g >= 0 else d_ctx[b - 1, NG - 1]
                sp.dma_start(to, ctx_sb[:, g % 2]).then_inc(ctx_out, 16)

            sp.wait_ge(zeroed_p, 4)
            load_stack(0, 0)
            sp.wait_ge(zeroed, 1)
            for slot in range(RING):
                rows = d_skew[slot].rearrange("w t p x -> p (w t) x")
                for a in (0, FIRST + TW):
                    sp.dma_start(rows[:, :, a:a + P], scored[:, 0, 0:2].rearrange("p a (t x) -> p (a t) x", x=P)
                                 ).then_inc(zero_out, 16)
            for g in range(1, SR - 1):
                load_stack(0, g)
            load_values(0, 0)
            load_values(0, 1)
            sp.wait_ge(zeroed, 6)
            sp.wait_ge(zeroed_p, 5)
            sp.wait_ge(zero_out, 16 * 2 * RING)
            for m in range(LEAD):
                write_tables(m, m)
                if m >= LEAD - NEXT:
                    read_tables(m - LEAD + NEXT, 0, m - LEAD + NEXT)

            def body(b, last):
                for hh in range(NH):
                    n = NH * b + hh
                    if not (last and hh + NEXT >= NH):
                        m = hh + NEXT
                        read_tables(n + NEXT, b + m // NH, m % NH)
                    if hh % SH == 0:
                        g = hh // SH + SR - 1
                        if not (last and g >= NS):
                            settled(sp, s_done, QT * n, passed)
                            load_stack(b + g // NS, g % NS)
                    if not (last and hh + LEAD >= NH):
                        write_tables(n + LEAD, (hh + LEAD) % NH)
                    if hh == TURN and not early(b, hh, NH):
                        settled(sp, pv_done, n - TURN, passed)
                        load_values(b, 1)
                    if hh == NH // 2 + TURN and not last:
                        settled(sp, pv_done, n - TURN, passed)
                        load_values(b + 1, 0)
                    if hh % GH == TURN and not early(b, hh, GH):
                        store_ctx(b, hh // GH - 1)

            peeled(sp, B, body)
            store_ctx(B - 1, NG - 1)
            sp.wait_ge(ctx_out, 16 * NG * B)

        @block.gpsimd
        def _(pool):
            nc.gpsimd.memset(scored[:, 0, 0:2], 0.0).then_inc(zeroed, 1)
            for t, x0, x1 in ((0, 2 * P, S), (1, 2 * P + P // 2, S), (2, 0, P), (2, S - P // 2, S), (3, 0, 2 * P)):
                nc.gpsimd.memset(bias[:, :, 0, t, x0:x1], 0.0).then_inc(zeroed, 1)
            pool.wait_ge(const_in, 16 * (3 + 2 * SLOTS))

            def constants(n, hh):
                u = hh % 2
                after(pool, filled, 2 * (n - 1))
                for w, kept in ((0, tab_c), (1, tab_p)):
                    after(pool, kept, 2 * (n + 1))
                    high = skew_in[:, u, w, 1:QT, 0:1] if w == 0 else skew_in[:, u, w, 0:QT - 1, TW - 1:TW]
                    nc.gpsimd.tensor_tensor(beyond[:, u, w], past[:, w].unsqueeze(1).to_broadcast([P, QT - 1, P]),
                                            high.to_broadcast([P, QT - 1, P]), ALU.mult).then_inc(beyond_done, 1)

            def fill(n, b, hh):
                u, v = hh % 2, hh % AHEAD
                after(pool, bias_in[v], 16 * READS * (NH // AHEAD * b + hh // AHEAD + 1))
                after(pool, beyond_done, 2 * (n + 1))
                for w in range(2):
                    tile = bias[:, v, w, 0]
                    block_of = bass.AP(tile.tensor, tile.offset + (S if w == 0 else P),
                                       [list(tile.ap[0]), [S + P, QT - 1], [1, P]])
                    nc.gpsimd.tensor_tensor(block_of, block_of, beyond[:, u, w], ALU.add).then_inc(filled, 1)

            for m in range(LEAD):
                if m >= LEAD - NEXT:
                    fill(m - LEAD + NEXT, 0, m - LEAD + NEXT)
                constants(m, m)

            def body(b, last):
                for hh in range(NH):
                    n = NH * b + hh
                    if not (last and hh + NEXT >= NH):
                        fill(n + NEXT, b + (hh + NEXT) // NH, (hh + NEXT) % NH)
                    if not (last and hh + LEAD >= NH):
                        constants(n + LEAD, (hh + LEAD) % NH)

            peeled(pool, B, body)

        @block.tensor
        def _(pe):
            def tables(n, b, hh, part):
                g, w, half = hh // SH, part % 2, part // 2
                if hh % SH == 0 and part == 0:
                    after(pe, stack_in[g % SR], 16 * STACKS * (NS // SR * b + g // SR + 1))
                after(pe, (tab_c, tab_p)[w], 2 * n + half)
                for k in range(2):
                    at = (S if w else 0) + (2 * half + k) * P
                    rows = ST + 3 + PLAIN if w else ST
                    mm = pe.matmul(m_tab[:, w, k], stack[0:rows, g % SR, hh % SH, at:at + P], tabs[0:rows, w, hh],
                                   start=True, stop=True)
                mm.then_inc(tab_done, 1)

            def scores(n, hh, t):
                if t == 0:
                    after(pe, filled, 2 * (n + 1))
                after(pe, s_kept, QT * n + t - 1)
                bank = m_s[:, t % 2]
                row = stack[0:ST + 3, hh // SH % SR, hh % SH]
                q = row[:, t * P:(t + 1) * P]
                far = max(0, t - 1) * P
                if far:
                    pe.matmul(bank[:, 0:far], q, row[:, 2 * S:2 * S + far], start=True, stop=False,
                              skip_group_check=True)
                pe.matmul(bank[:, far:], q, row[:, S + far:2 * S], start=not far, stop=False,
                          skip_group_check=True)
                near = [k for k in range(QT) if abs(k - t) <= 1]
                for k in near:
                    mm = pe.matmul(bank[:, k * P:(k + 1) * P], bias[:, hh % AHEAD, 1, k, t * P:(t + 1) * P],
                                   ident[:], start=False, stop=(k == near[-1]), is_transpose=True,
                                   skip_group_check=True)
                mm.then_inc(s_done, 1)

            def turn(n, hh, k):
                if k == 0:
                    after(pe, exp_done, QT * (n + 1))
                after(pe, (turnA, turnD)[k % 2], 2 * n + k // 2)
                for t in range(QT):
                    mm = pe.transpose(m_t[:, k % 2, t * P:(t + 1) * P], probs[:, hh % 2, t, k * P:(k + 1) * P],
                                      ident[:])
                mm.then_inc(turn_done, 1)

            def context(n, b, hh, k):
                half, j = hh // (NH // 2), hh % GH
                if k == 0 and hh % (NH // 2) == 0:
                    after(pe, values_in[half], 16 * (b + 1))
                if k == 0 and j == 0:
                    after(pe, ctx_kept, NG * b + hh // GH)
                after(pe, (turnA, turnD)[k % 2], 2 * n + k // 2 + 1)
                mm = pe.matmul(m_ctx[j * CROW:j * CROW + VROW], values[:, half, k, hh % (NH // 2)],
                               probsT[:, k], start=(k == 0), stop=(k == QT - 1))
                if k == QT - 1:
                    mm.then_inc(pv_done, 1)

            def turned(n, b, hh):
                for k in range(QT):
                    turn(n, hh, k)
                    if k:
                        context(n, b, hh, k - 1)
                context(n, b, hh, QT - 1)

            pe.wait_ge(const_in, 16 * (3 + 2 * SLOTS))
            pe.wait_ge(zeroed_p, 4)
            for m in range(LEAD):
                for part in range(4):
                    tables(m, 0, m, part)

            def body(b, last):
                for hh in range(NH):
                    n, m = NH * b + hh, hh + LEAD
                    old = not early(b, hh, TURN)
                    behind = (n - TURN, b - 1 if hh < TURN else b, (hh - TURN) % NH)
                    for t in range(QT):
                        scores(n, hh, t)
                        if t == 0 and not early(b, hh, TURN + 1):
                            at = hh - TURN - 1
                            context(n - TURN - 1, b - 1 if at < 0 else b, at % NH, QT - 1)
                        if old:
                            turn(behind[0], behind[2], t)
                        if t < 2 and not (last and m >= NH):
                            for part in (2 * t, 2 * t + 1):
                                tables(n + LEAD, b + m // NH, m % NH, part)
                        if old and t:
                            context(*behind, t - 1)

            peeled(pe, B, body)
            context(HEADS - TURN - 1, B - 1, NH - TURN - 1, QT - 1)
            for lag in range(TURN, 0, -1):
                turned(HEADS - lag, B - 1, NH - lag)

        @block.scalar
        def _(act):
            def keep_tables(n, hh, half):
                u = hh % 2
                after(act, tab_done, 4 * n + 2 * half + 1)
                if half == 0:
                    wait_tables(act, skew_out, n, hh)
                    after(act, beyond_done, 2 * (n - 1))
                nc.scalar.activation(skew_in[:, u, 0, 2 * half:2 * half + 2], m_tab[:, 0], ACT.Identity
                                     ).then_inc(tab_c, 1)

            def exponent(n, hh, t):
                u = hh % 2
                if t == 0:
                    after(act, shifted, n + 1)
                    after(act, turn_done, QT * (n - 1))
                nc.scalar.activation(probs[:, u, t], scored[:, u, t], ACT.Exp, bias=shift[:, u, t:t + 1],
                                     scale=SCALE).then_inc(exp_done, 1)

            def keep_turned(n, k):
                after(act, turn_done, QT * n + k + 1)
                after(act, pv_done, n)
                nc.scalar.activation(probsT[:, k], m_t[:, 0], ACT.Identity).then_inc(turnA, 1)

            def keep_context(n, b, hh):
                g = hh // GH
                after(act, pv_done, n + 1)
                after(act, ctx_out, 16 * (NG * b + g))
                nc.scalar.activation(ctx_sb[:, g % 2], m_ctx[:], ACT.Identity).then_inc(ctx_kept, 1)

            for m in range(LEAD):
                for half in range(2):
                    keep_tables(m, m, half)

            def body(b, last):
                for hh in range(NH):
                    n, m = NH * b + hh, hh + LEAD
                    old = not early(b, hh, TURN)
                    for t in range(QT):
                        if not early(b, hh, 1):
                            exponent(n - 1, (hh - 1) % NH, t)
                        if t == 0 and hh % GH == TURN and not early(b, hh, GH):
                            at = hh - TURN - 1
                            keep_context(n - TURN - 1, b - 1 if at < 0 else b, at % NH)
                        if old and t % 2 == 0:
                            keep_turned(n - TURN, t)
                        if t < 2 and not (last and m >= NH):
                            keep_tables(n + LEAD, m % NH, t)

            peeled(act, B, body)
            for t in range(QT):
                exponent(HEADS - 1, NH - 1, t)
            for lag in range(TURN, 0, -1):
                keep_turned(HEADS - lag, 0)
                keep_turned(HEADS - lag, 2)
            keep_context(HEADS - 1, B - 1, NH - 1)

        @block.vector
        def _(dve):
            nc.vector.memset(tabs[ST:, 1], 0.0).then_inc(zeroed_p, 1)
            nc.vector.memset(m_ctx[:], 0.0).then_inc(zeroed_p, 1)
            nc.vector.memset(stack[ST:, 0, :, 0:2 * S], 1.0).then_inc(zeroed_p, 1)
            nc.vector.memset(stack[ST:, 1:, :, 0:2 * S], 1.0).then_inc(zeroed_p, 1)
            nc.vector.memset(bias[:, :, 1, 1:3, 0:P + P // 2], 0.0).then_inc(zeroed_p, 1)

            def keep_tables(n, hh, half):
                u = hh % 2
                after(dve, tab_done, 4 * n + 2 * half + 2)
                if half == 0:
                    wait_tables(dve, skew_out, n, hh)
                    after(dve, beyond_done, 2 * (n - 1))
                nc.vector.tensor_copy(skew_in[:, u, 1, 2 * half:2 * half + 2], m_tab[:, 1]).then_inc(tab_p, 1)

            def add_bias(n, hh, t):
                u = hh % 2
                if t == 0:
                    after(dve, filled, 2 * (n + 1))
                    after(dve, exp_done, QT * (n - 1))
                settled(dve, s_done, QT * n + t + 1, passed)
                nc.vector.tensor_tensor_reduce(scored[:, u, t], m_s[:, t % 2], bias[:, hh % AHEAD, 0, t], 1.0,
                                               -3.0e38, ALU.add, ALU.max, top_of[:, u, t:t + 1]
                                               ).then_inc(s_kept, 1)

            def shift_of(n, hh):
                u = hh % 2
                after(dve, s_kept, QT * (n + 1))
                nc.vector.tensor_scalar(shift[:, u], top_of[:, u], -SCALE, None, ALU.mult).then_inc(shifted, 1)

            def keep_turned(n, k):
                after(dve, turn_done, QT * n + k + 1)
                after(dve, pv_done, n)
                nc.vector.tensor_copy(probsT[:, k], m_t[:, 1]).then_inc(turnD, 1)

            for m in range(LEAD):
                for half in range(2):
                    keep_tables(m, m, half)

            def body(b, last):
                for hh in range(NH):
                    n, m = NH * b + hh, hh + LEAD
                    for t in range(QT):
                        add_bias(n, hh, t)
                        if t == QT - 1:
                            shift_of(n, hh)
                        if t % 2 and not early(b, hh, TURN):
                            keep_turned(n - TURN, t)
                        if t < 2 and not (last and m >= NH):
                            keep_tables(n + LEAD, m % NH, t)

            peeled(dve, B, body)
            for lag in range(TURN, 0, -1):
                keep_turned(HEADS - lag, 1)
                keep_turned(HEADS - lag, 3)


def wait_tables(eng, skew_out, n, hh):
    if not (isinstance(n, int) and n < 2):
        eng.wait_ge(skew_out[hh % 2], 8 * (n - hh % 2))


def output(nc, io, B, ctx, sem, passed, scores, d_h, d_ctx, d_share, d_xg):
    def sb(name, shape, dt=F32):
        return ctx.enter_context(nc.sbuf_tensor("o_" + name, shape, dt))

    def ps(name, shape):
        return ctx.enter_context(nc.psum_tensor("o_ps_" + name, shape, F32))

    ident, wo = sb("ident", [P, P]), sb("wo", [P, HC, H])
    bo_row, wr, br_row = sb("bo_row", [P, H]), sb("wr", [P, HC, NE]), sb("br_row", [P, NE])
    minus_half = sb("minus_half", [P, QT])
    h_in, h_new = sb("h_in", [P, 2, QT, H]), sb("h_new", [P, 2, QT, H])
    c_in, shares = sb("c_in", [P, 2, HC, S]), sb("shares", [P, 2, HC, S])
    ctxn = sb("ctxn", [P, 2, HC, S])
    stats, moments = sb("stats", [P, QT, 6]), sb("moments", [P, QT, 2])
    var_eps, rstd = sb("var_eps", [P, QT]), sb("rstd", [P, QT])
    xg, xT = sb("xg", [P, 2, QT, XG]), sb("xT", [P, HC, S])
    logits, expd = sb("logits", [P, QT, NE]), sb("expd", [P, QT, NE])
    top_of, total, share = sb("top_of", [P, QT]), sb("total", [P, QT]), sb("share", [P, QT])
    m_o, m_turn, m_r = ps("m_o", [P, 2, QT, H]), ps("m_turn", [P, HC, S]), ps("m_r", [P, QT, NE])
    rows = min(P, B * NH)
    each = B * NH // rows
    assert rows >= 2 * NH
    sums = sb("sums", [rows, each, S])
    const_in, half_set = sem("o_const_in"), sem("o_half_set")
    sums_in, inverted = sem("o_sums_in"), sem("o_inverted")
    sums_out = [sem(f"o_sums_out{u}") for u in range(2)]
    batch_in = [sem(f"o_batch_in{u}") for u in range(2)]
    h_stored = [sem(f"o_h_stored{u}") for u in range(2)]
    xg_stored = [sem(f"o_xg_stored{u}") for u in range(2)]
    (scaled, o_done, h_added, h_done, st_done, mo_done, ve_done, rs_done, xn_done, turn_done,
     turned, r_done, soft, exp_done, xg_done) = (sem("o_" + n) for n in (
         "scaled", "o_done", "h_added", "h_done", "st_done", "mo_done", "ve_done", "rs_done",
         "xn_done", "turn_done", "turned", "r_done", "soft", "exp_done", "xg_done"))
    consts = [(ident[:], io["ident"]), (wo[:], io["Wo"].rearrange("(c p) o -> p c o", p=P)),
              (bo_row[:], io["bo"].partition_broadcast(P)),
              (wr[:], io["router_w"].rearrange("(c p) o -> p c o", p=P)),
              (br_row[:], io["router_b"].partition_broadcast(P))]
    LOADS = 1 + 2 * HC
    SOFT = 6
    pairs = B // 2

    with nc.Block() as block:
        @block.sync
        def _(sp):
            first = d_ctx[0, 0, HD]
            for e in range(each):
                sp.dma_start(sums[:, e], bass.AP(first.tensor, first.offset + e * rows * CROW * S,
                                                 [[CROW * S, rows], [1, S]])).then_inc(sums_in, 16)
            for dst, src in consts:
                sp.dma_start(dst, src).then_inc(const_in, 16)

            def load_inputs(n, u):
                sp.dma_start(h_in[:, u], d_h[n].rearrange("(t p) o -> p t o", p=P)).then_inc(batch_in[u], 16)
                for c in range(HC):
                    at = d_ctx[n, c * (NG // HC)]
                    sp.dma_start(c_in[:, u, c], bass.AP(at.tensor, at.offset,
                                                        [[CROW * S, NH // HC], [S, HD], [1, S]])
                                 ).then_inc(batch_in[u], 16)

            def load_shares(n, u):
                for c in range(HC):
                    of = d_share[n, c * (NH // HC)]
                    sp.dma_start(shares[:, u, c], bass.AP(of.tensor, of.offset, [[S, NH // HC], [0, HD], [1, S]])
                                 ).then_inc(batch_in[u], 16)

            for u in range(2):
                load_inputs(u, u)
            for e in range(each):
                sp.wait_ge(inverted, e + 1)
                sp.dma_start(d_share.rearrange("b h s -> (b h) s")[e * rows:(e + 1) * rows], sums[:, e]
                             ).then_inc(sums_out[min(e, 1)], 16)
                if e == 0:
                    sp.wait_ge(sums_out[0], 16)
                    for u in range(2):
                        load_shares(u, u)
            if each > 1:
                sp.wait_ge(sums_out[1], 16 * (each - 1))

            def store_xg(n, u):
                settled(sp, xg_done, n + 1, passed)
                sp.dma_start(d_xg.rearrange("(b t p) o -> b p t o", t=QT, p=P)[n], xg[:, u]
                             ).then_inc(xg_stored[u], 16)

            def body(i, last):
                for u in range(2):
                    n = 2 * i + u
                    settled(sp, h_done, n + 1, passed)
                    if not last:
                        load_inputs(n + 2, u)
                        load_shares(n + 2, u)
                    sp.dma_start(io["out"][n].rearrange("(t p) o -> p t o", p=P), h_new[:, u]
                                 ).then_inc(h_stored[u], 16)
                    if not (isinstance(n, int) and n == 0):
                        store_xg(n - 1, 1 - u)

            peeled(sp, pairs, body)
            store_xg(B - 1, 1)
            for u in range(2):
                sp.wait_ge(h_stored[u], 16 * pairs)
                sp.wait_ge(xg_stored[u], 16 * pairs)

        @block.gpsimd
        def _(pool):
            nc.gpsimd.memset(minus_half[:], -0.5).then_inc(half_set, 1)
            pool.wait_ge(half_set, 1)
            pool.wait_ge(const_in, 16 * len(consts))

            def scale_context(n, i, u):
                after(pool, batch_in[u], 16 * LOADS * (i + 1))
                after(pool, o_done, n - 1)
                nc.gpsimd.tensor_tensor(ctxn[:, u], c_in[:, u], shares[:, u], ALU.mult).then_inc(scaled, 1)

            def add_bias(n, u):
                nc.gpsimd.tensor_tensor(h_in[:, u], h_in[:, u], bo_row[:].unsqueeze(1).to_broadcast([P, QT, H]),
                                        ALU.add).then_inc(h_added, 1)

            def power(n):
                after(pool, ve_done, n + 1)
                nc.gpsimd.tensor_tensor(rstd[:], var_eps[:], minus_half[:], ALU.pow).then_inc(rs_done, 1)

            for u in range(2):
                scale_context(u, 0, u)
                add_bias(u, u)
            power(0)

            def body(i, last):
                for u in range(2):
                    n = 2 * i + u
                    if not last:
                        scale_context(n + 2, i + 1, u)
                    if not (last and u == 1):
                        power(n + 1)
                    if not last:
                        add_bias(n + 2, u)

            peeled(pool, pairs, body)

        @block.tensor
        def _(pe):
            def project_out(n, u):
                after(pe, scaled, n + 1)
                after(pe, h_done, n - 1)
                for t in range(QT):
                    for c in range(HC):
                        mm = pe.matmul(m_o[:, u, t], ctxn[:, u, c, t * P:(t + 1) * P], wo[:, c], start=(c == 0),
                                       stop=(c == HC - 1))
                mm.then_inc(o_done, 1)

            def turn(n, u):
                after(pe, xn_done, n + 1)
                after(pe, turned, HC * n)
                for c in range(HC):
                    for t in range(QT):
                        mm = pe.transpose(m_turn[:, c, t * P:(t + 1) * P], xg[:, u, t, c * P:(c + 1) * P],
                                          ident[:])
                    mm.then_inc(turn_done, 1)

            def route(n):
                after(pe, turned, HC * (n + 1))
                after(pe, soft, SOFT * n)
                for t in range(QT):
                    for c in range(HC):
                        mm = pe.matmul(m_r[:, t], xT[:, c, t * P:(t + 1) * P], wr[:, c], start=(c == 0),
                                       stop=(c == HC - 1))
                mm.then_inc(r_done, 1)

            pe.wait_ge(const_in, 16 * len(consts))
            for u in range(2):
                project_out(u, u)

            def body(i, last):
                for u in range(2):
                    n = 2 * i + u
                    turn(n, u)
                    route(n)
                    if not last:
                        project_out(n + 2, u)

            peeled(pe, pairs, body)

        @block.scalar
        def _(act):
            def body(i, last):
                for u in range(2):
                    n = 2 * i + u
                    for c in range(HC):
                        after(act, turn_done, HC * n + c + 1)
                        after(act, r_done, n)
                        nc.scalar.activation(xT[:, c], m_turn[:, c], ACT.Identity).then_inc(turned, 1)
                    after(act, soft, SOFT * n + 3)
                    nc.scalar.activation(expd[:], logits[:], ACT.Exp).then_inc(exp_done, 1)

            peeled(act, pairs, body)

        @block.vector
        def _(dve):
            dve.wait_ge(sums_in, 16 * each)
            for e in range(each):
                nc.vector.reciprocal(sums[:, e], sums[:, e]).then_inc(inverted, 1)
            dve.wait_ge(const_in, 16 * len(consts))

            def moments_of(n, i, u):
                after(dve, o_done, n + 1)
                after(dve, h_added, n + 1)
                after(dve, h_stored[u], 16 * i)
                nc.vector.tensor_tensor(h_new[:, u], m_o[:, u], h_in[:, u], ALU.add).then_inc(h_done, 1)
                after(dve, h_done, n + 1)
                for t in range(QT):
                    nc.vector.bn_stats(stats[:, t], h_new[:, u, t]).then_inc(st_done, 1)
                settled(dve, st_done, QT * (n + 1), passed)
                for t in range(QT):
                    nc.vector.bn_aggr(moments[:, t], stats[:, t]).then_inc(mo_done, 1)
                after(dve, mo_done, QT * (n + 1))
                nc.vector.tensor_scalar_add(var_eps[:], moments[:, :, 1], EPS).then_inc(ve_done, 1)

            def norm(n, i, u):
                after(dve, rs_done, n + 1)
                after(dve, xg_stored[u], 16 * i)
                for t in range(QT):
                    ins = nc.vector.tensor_scalar(xg[:, u, t, 0:H], h_new[:, u, t], moments[:, t, 0:1],
                                                  rstd[:, t:t + 1], ALU.subtract, ALU.mult)
                ins.then_inc(xn_done, 1)

            def soft_scores(n, u):
                def step(ins, k):
                    ins.then_inc(soft, 1)
                    after(dve, soft, SOFT * n + k)

                after(dve, r_done, n + 1)
                step(nc.vector.tensor_tensor(logits[:], m_r[:], br_row[:].unsqueeze(1).to_broadcast([P, QT, NE]),
                                             ALU.add), 1)
                step(nc.vector.tensor_reduce(top_of[:], logits[:], AX.X, ALU.max), 2)
                step(nc.vector.tensor_tensor(logits[:], logits[:], top_of[:].unsqueeze(2).to_broadcast([P, QT, NE]),
                                             ALU.subtract), 3)
                after(dve, exp_done, n + 1)
                step(nc.vector.tensor_reduce(total[:], expd[:], AX.X, ALU.add), 4)
                step(nc.vector.reciprocal(share[:], total[:]), 5)
                nc.vector.tensor_tensor(xg[:, u, :, H:], expd[:], share[:].unsqueeze(2).to_broadcast([P, QT, NE]),
                                        ALU.mult).then_inc(xg_done, 1)
                step(nc.vector.tensor_tensor(scores[:, :, bass.ts(n, QT)].rearrange("p e t -> p t e"), expd[:],
                                             share[:].unsqueeze(2).to_broadcast([P, QT, NE]), ALU.mult), 6)

            moments_of(0, 0, 0)
            norm(0, 0, 0)

            def body(i, last):
                for u in range(2):
                    n = 2 * i + u
                    if not (last and u == 1):
                        moments_of(n + 1, i + u, 1 - u)
                        norm(n + 1, i + u, 1 - u)
                    soft_scores(n, u)

            peeled(dve, pairs, body)


def choose(nc, io, NT, ctx, sem, passed, scores, chosen, d_scores, d_floor, load_expert):
    def sb(name, shape, dt=F32):
        return ctx.enter_context(nc.sbuf_tensor("c_" + name, shape, dt))

    def ps(name, shape):
        return ctx.enter_context(nc.psum_tensor("c_ps_" + name, shape, F32))

    ET = NE * NT
    before = sb("before", [P, P], BF16)
    ones = sb("ones", [P, P], BF16)
    before_f, place = sb("before_f", [P, P]), sb("place", [P, 2, NT])
    group = sb("group", [P, P])
    CH = P // NE
    spread = sb("spread", [P, P // CH, NT])
    marks = sb("marks", [P, P // CH, NT])
    pair = sb("pair", [P, 2])
    least = pair[:, 0:1].bitcast(I32)
    trial, bit, enough = sb("trial", [P, 1], I32), sb("bit", [P, 1], I32), sb("enough", [P, 1], I32)
    held = sb("held", [P, 1])
    floors = sb("floors", [P, P, 2])
    restart = sb("restart", [P, NE, NT])
    mask = sb("mask", [P, NE, NT], BF16)
    above, equal = sb("above", [P, NE, NT]), sb("equal", [P, NE, NT])
    run, rank, sel = sb("run", [P, NE, NT]), sb("rank", [P, NE, NT]), sb("sel", [P, NE, NT])
    LOW = 32
    HIGH = TOPK // LOW
    iota, iotas = sb("iota", [P, P]), sb("iotas", [P, LOW, NT], BF16)
    rank_i, digit = sb("rank_i", [P, NE, NT], I32), sb("digit", [P, 2, NE, NT], I32)
    low, high = sb("low", [P, NE, NT], BF16), sb("high", [P, NE, NT], BF16)
    tile_of = sb("tile_of", [P, NT], BF16)
    hot_low = sb("hot_low", [P, 2, LOW, NT], BF16)
    hot_high = sb("hot_high", [P, 2, HIGH, NT], BF16)
    what = sb("what", [P, 2, 2, HIGH, NT], BF16)
    index = sb("index", [LOW, NE, HIGH])
    m_count = ps("m_count", [P, 1])
    GB = min(ET, S)
    m_below, m_all = ps("m_below", [P, ET // GB, GB]), ps("m_all", [P, ET // GB, GB])
    m_list = ps("m_list", [LOW, NE, 2, HIGH])
    (c_in, c_dve, c_pe, c_hot, c_listed, scores_out, spread_in, floor_out, floors_in) = (
        sem("c_" + n) for n in ("in", "dve", "pe", "hot", "listed", "scores_out", "spread_in", "floor_out",
                                "floors_in"))
    ROUND = 5
    START = 4

    with nc.Block() as block:
        @block.sync
        def _(sp):
            sp.dma_start(d_scores, scores[:]).then_inc(scores_out, 16)
            for dst, src in ((before_f, io["before"]), (iota, io["iota"]), (place, io["place"]),
                             (group, io["group"])):
                sp.dma_start(dst[:], src).then_inc(c_in, 16)
            sp.wait_ge(scores_out, 16)
            for e in range(NE):
                sp.dma_start(spread[e * CH:(e + 1) * CH],
                             d_scores.rearrange("(c r) e t -> e c r t", c=CH)[e]).then_inc(spread_in, 16)
            for e in range(2):
                load_expert(sp, e, e)
            sp.wait_ge(c_dve, START + ROUND * BITS + 2)
            sp.dma_start(d_floor, pair[:]).then_inc(floor_out, 16)
            sp.wait_ge(floor_out, 16)
            sp.dma_start(floors[:], d_floor.partition_broadcast(P)).then_inc(floors_in, 16)

        @block.tensor
        def _(pe):
            pe.wait_ge(c_dve, START)

            with pe.Fori(0, BITS, 1) as r:
                after(pe, c_dve, START + ROUND * r + 2)
                pe.matmul(m_count[:], group[:], held[:], start=True, stop=True).then_inc(c_pe, 1)
            base = START + ROUND * BITS
            pe.wait_ge(c_dve, base + 1)
            pe.matmul(m_count[:], group[:], held[:], start=True, stop=True).then_inc(c_pe, 1)
            for stage, ready in ((0, base + 4), (1, base + 11)):
                pe.wait_ge(c_dve, ready)
                flat = mask[:].rearrange("p e t -> p (e t)")
                for g in range(ET // GB):
                    pe.matmul(m_below[:, g], before[:], flat[:, g * GB:(g + 1) * GB], start=True, stop=True)
                    mm = pe.matmul(m_all[:, g], ones[:], flat[:, g * GB:(g + 1) * GB], start=True, stop=True)
                mm.then_inc(c_pe, 1)
            for e in range(NE):
                pe.wait_ge(c_hot, 4 * (e + 1))
                for t in range(NT):
                    mm = pe.matmul(m_list[:, e], hot_low[:, e % 2, :, t], what[:, e % 2, :, :, t],
                                   start=(t == 0), stop=(t == NT - 1), skip_group_check=True)
                mm.then_inc(c_listed, 1)

        @block.vector
        def _(dve):
            count = [0]

            def step(ins):
                count[0] += 1
                ins.then_inc(c_dve, 1)
                dve.wait_ge(c_dve, count[0])

            nc.vector.memset(least, 0)
            nc.vector.memset(bit[:], 1 << (BITS - 1))
            nc.vector.memset(restart[:], 1.0)
            step(nc.vector.memset(rank[:], 0.0))
            step(nc.vector.memset(restart[:, :, 0:1], 0.0))
            dve.wait_ge(c_in, 64)
            nc.vector.tensor_copy(iotas[:], iota[:, 0:LOW].unsqueeze(2).to_broadcast([P, LOW, NT]))
            nc.vector.tensor_copy(tile_of[:], place[:, 0])
            step(nc.vector.memset(ones[:], 1.0))
            step(nc.vector.tensor_copy(before[:], before_f[:]))
            dve.wait_ge(spread_in, 16 * NE)

            with dve.Fori(0, BITS, 1) as r:
                def chain(ins, k):
                    ins.then_inc(c_dve, 1)
                    settled(dve, c_dve, START + ROUND * r + k, passed)

                chain(nc.vector.tensor_tensor(trial[:], least, bit[:], ALU.bitwise_or), 1)
                chain(nc.vector.tensor_scalar(marks[:], spread[:], trial[:].bitcast(F32), 0.0, ALU.is_ge, ALU.add,
                                              accum_out=held[:]), 2)
                chain(nc.vector.tensor_scalar(bit[:], bit[:], 1, None, ALU.logical_shift_right), 3)
                after(dve, c_pe, r + 1)
                chain(nc.vector.tensor_scalar(enough[:], m_count[:], float(TOPK), None, ALU.is_ge), 4)
                chain(nc.vector.copy_predicated(least, enough[:], trial[:]), 5)
            count[0] = START + ROUND * BITS
            step(nc.vector.tensor_scalar(marks[:], spread[:], pair[:, 0:1], 0.0, ALU.is_gt, ALU.add,
                                         accum_out=held[:]))
            dve.wait_ge(c_pe, BITS + 1)
            step(nc.vector.tensor_scalar(pair[:, 1:2], m_count[:], -1.0, float(TOPK), ALU.mult, ALU.add))
            dve.wait_ge(floors_in, 16)
            by_expert = floors[:].rearrange("p (e c) k -> p e c k", c=CH)[:, :, 0]
            floor, room = (by_expert[:, :, k:k + 1].to_broadcast([P, NE, NT]) for k in range(2))
            step(nc.vector.tensor_tensor(above[:], scores[:], floor, ALU.is_gt))
            nc.vector.tensor_tensor(equal[:], scores[:], floor, ALU.is_equal)
            step(nc.vector.tensor_tensor(mask[:], scores[:], floor, ALU.is_equal))

            def ranks():
                below = m_below[:].rearrange("p g x -> p (g x)")
                every = m_all[:].rearrange("p g x -> p (g x)")
                flat = lambda x: x[:].rearrange("p e t -> p (e t)")
                step(nc.vector.tensor_copy(flat(run), every))
                step(nc.vector.tensor_tensor_scan(flat(rank), flat(restart), flat(run), 0.0, ALU.mult, ALU.add))
                step(nc.vector.tensor_tensor(flat(rank), flat(rank), flat(run), ALU.subtract))
                step(nc.vector.tensor_tensor(flat(rank), flat(rank), below, ALU.add))

            dve.wait_ge(c_pe, BITS + 2)
            ranks()
            step(nc.vector.tensor_tensor(sel[:], rank[:], room, ALU.is_lt))
            step(nc.vector.tensor_tensor(sel[:], sel[:], equal[:], ALU.mult))
            step(nc.vector.tensor_tensor(mask[:], sel[:], above[:], ALU.add))
            dve.wait_ge(c_pe, BITS + 3)
            ranks()
            step(nc.vector.tensor_tensor(sel[:], sel[:], above[:], ALU.add))
            step(nc.vector.scalar_tensor_tensor(rank[:], rank[:], 1.0, sel[:], ALU.add, ALU.mult))
            step(nc.vector.tensor_scalar_add(rank_i[:], rank[:], -1.0))
            nc.vector.tensor_scalar(digit[:, 0], rank_i[:], LOW - 1, None, ALU.bitwise_and)
            step(nc.vector.tensor_scalar(digit[:, 1], rank_i[:], LOW.bit_length() - 1, None,
                                         ALU.arith_shift_right))
            nc.vector.tensor_copy(low[:], digit[:, 0])
            step(nc.vector.tensor_copy(high[:], digit[:, 1]))
            for e in range(NE):
                u = e % 2
                if e >= 2:
                    dve.wait_ge(c_listed, e - 1)
                of = lambda digits, n: digits[:, e].unsqueeze(1).to_broadcast([P, n, NT])
                nc.vector.tensor_tensor(hot_high[:, u], iotas[:, 0:HIGH], of(high, HIGH), ALU.is_equal
                                        ).then_inc(c_hot, 1)
                nc.vector.tensor_tensor(hot_low[:, u], iotas[:], of(low, LOW), ALU.is_equal).then_inc(c_hot, 1)
                dve.wait_ge(c_hot, 4 * e + 1)
                nc.vector.tensor_tensor(what[:, u, 0], hot_high[:, u],
                                        tile_of[:].unsqueeze(1).to_broadcast([P, HIGH, NT]), ALU.mult
                                        ).then_inc(c_hot, 1)
                nc.vector.tensor_scalar(what[:, u, 1], hot_high[:, u], place[:, 1, 0:1], None, ALU.mult
                                        ).then_inc(c_hot, 1)
            dve.wait_ge(c_listed, NE)
            step(nc.vector.tensor_copy(index[:], m_list[:, :, 1]))
            step(nc.vector.scalar_tensor_tensor(index[:], m_list[:, :, 0], float(P), index[:], ALU.mult, ALU.add))
            for g in range(P // LOW):
                ins = nc.vector.tensor_copy(chosen[g * LOW:(g + 1) * LOW], index[:, :, g * CT:(g + 1) * CT])
            step(ins)


def experts(nc, io, T, ctx, sem, passed, chosen, d_xg, w1, w2, b2, w_in, load_expert):
    def sb(name, shape, dt=F32):
        return ctx.enter_context(nc.sbuf_tensor("e_" + name, shape, dt))

    def ps(name, shape):
        return ctx.enter_context(nc.psum_tensor("e_ps_" + name, shape, F32))

    ident = sb("ident", [P, P])
    b1 = sb("b1", [P, NE, FC])
    index, gate = sb("index", [P, 2, CT], U32), sb("gate", [P, 2, CT])
    rows, rowsT = sb("rows", [P, 2, CT, XG]), sb("rowsT", [P, HC, TOPK])
    hidden = sb("hidden", [P, FC, TOPK])
    result = sb("result", [P, 2, CT, H])
    m_turn, m_1, m_2 = ps("m_turn", [P, HC, TOPK]), ps("m_1", [P, 2, TOPK]), ps("m_2", [P, 2, H * 2])
    const_in = sem("e_const_in")
    rows_in = [sem(f"e_rows_in{u}") for u in range(2)]
    (picked, gated, turn_done, turnA, turnD, one_done, one_kept, two_done, two_kept, ready, added) = (
        sem("e_" + n) for n in ("picked", "gated", "turn_done", "turnA", "turnD", "one_done", "one_kept",
                                "two_done", "two_kept", "ready", "added"))
    out_rows = io["out"].rearrange("b s o -> (b s) o")
    W = 3

    with nc.Block() as block:
        @block.sync
        def _(sp):
            sp.dma_start(ident[:], io["ident"]).then_inc(const_in, 16)
            sp.dma_start(b1[:], io["b1T"]).then_inc(const_in, 16)

            def body(i, last):
                for u in range(2):
                    if not last:
                        settled(sp, ready, CT * (2 * i + u + 1), passed)
                        load_expert(sp, 2 * i + u + 2, u)

            peeled(sp, NE // 2, body)

        @block.gpsimd
        def _(pool):
            def gather(e, i, u):
                settled(pool, picked, e + 1, passed)
                for c in range(CT):
                    nc.gpsimd.indirect_dma_start(
                        out=rows[:, u, c], out_offset=None, in_=d_xg,
                        in_offset=bass.IndirectOffsetOnAxis(ap=index[:, u, c:c + 1], axis=0)
                    ).then_inc(rows_in[u], 16)

            def add_to_out(e, u):
                for c in range(CT):
                    settled(pool, ready, CT * e + c + 1, passed)
                    nc.gpsimd.indirect_dma_start(
                        out=out_rows, out_offset=bass.IndirectOffsetOnAxis(ap=index[:, u, c:c + 1], axis=0),
                        in_=result[:, u, c], in_offset=None, compute_op=ALU.add).then_inc(added, 16)
                settled(pool, added, 16 * CT * (e + 1), passed)

            gather(0, 0, 0)

            def body(i, last):
                gather(2 * i + 1, i, 1)
                add_to_out(2 * i, 0)
                if not last:
                    gather(2 * i + 2, i + 1, 0)
                add_to_out(2 * i + 1, 1)

            peeled(pool, NE // 2, body)

        @block.tensor
        def _(pe):
            pe.wait_ge(const_in, 32)

            def turn(e, i, u):
                after(pe, rows_in[u], 16 * CT * (i + 1))
                after(pe, turnA, e)
                after(pe, turnD, e)
                for c in range(HC):
                    for t in range(CT):
                        mm = pe.transpose(m_turn[:, c, t * P:(t + 1) * P], rows[:, u, t, c * P:(c + 1) * P],
                                          ident[:])
                    mm.then_inc(turn_done, 1)

            turn(0, 0, 0)

            def body(i, last):
                for u in range(2):
                    e = 2 * i + u
                    after(pe, w_in[u], 16 * W * (i + 1))
                    after(pe, turnA, e + 1)
                    after(pe, turnD, e + 1)
                    for f in range(FC):
                        after(pe, one_kept, FC * e + f - 1)
                        for c in range(HC):
                            mm = pe.matmul(m_1[:, f % 2], w1[:, u, c, f * P:(f + 1) * P], rowsT[:, c],
                                           start=(c == 0), stop=(c == HC - 1))
                        mm.then_inc(one_done, 1)
                    if not (last and u == 1):
                        turn(e + 1, i + u, 1 - u)
                    after(pe, one_kept, FC * (e + 1))
                    for t in range(CT):
                        after(pe, two_kept, CT * e + t - 1)
                        for f in range(FC):
                            mm = pe.matmul(m_2[:, t % 2, 0:H], hidden[:, f, t * P:(t + 1) * P], w2[:, u, f],
                                           start=(f == 0), stop=(f == FC - 1))
                        mm.then_inc(two_done, 1)

            peeled(pe, NE // 2, body)

        @block.scalar
        def _(act):
            act.wait_ge(const_in, 32)

            def keep_turned(e):
                after(act, turn_done, HC * e + 1)
                nc.scalar.activation(rowsT[:, 0], m_turn[:, 0], ACT.Identity).then_inc(turnA, 1)

            keep_turned(0)

            def body(i, last):
                for u in range(2):
                    e = 2 * i + u
                    after(act, two_done, CT * e)
                    for f in range(FC):
                        after(act, one_done, FC * e + f + 1)
                        nc.scalar.activation(hidden[:, f], m_1[:, f % 2], ACT.Relu,
                                             bias=b1[:, e, f:f + 1]).then_inc(one_kept, 1)
                    if not (last and u == 1):
                        keep_turned(e + 1)

            body(0, False)
            for i in range(1, NE // 2):
                body(i, i == NE // 2 - 1)

        @block.vector
        def _(dve):
            def pick(e, u):
                if not (isinstance(e, int) and e < 2):
                    after(dve, added, 16 * CT * (e - 1))
                nc.vector.tensor_copy(index[:, u], chosen[:, e]).then_inc(picked, 1)

            def keep_turned(e, u):
                after(dve, turn_done, HC * e + 2)
                nc.vector.tensor_copy(rowsT[:, 1], m_turn[:, 1]).then_inc(turnD, 1)
                nc.vector.tensor_copy(gate[:, u], rows[:, u, :, H + e]).then_inc(gated, 1)

            def body(i, last):
                for u in range(2):
                    e = 2 * i + u
                    if not (last and u == 1):
                        pick(e + 1, 1 - u)
                        keep_turned(e + 1, 1 - u)
                    after(dve, gated, e + 1)
                    for t in range(CT):
                        after(dve, two_done, CT * e + t + 1)
                        nc.vector.tensor_tensor(result[:, u, t], m_2[:, t % 2, 0:H], b2[:, u], ALU.add
                                                ).then_inc(two_kept, 1)
                        after(dve, two_kept, CT * e + t + 1)
                        nc.vector.tensor_scalar(result[:, u, t], result[:, u, t], gate[:, u, t:t + 1], None,
                                                ALU.mult).then_inc(ready, 1)

            pick(0, 0)
            keep_turned(0, 0)
            body(0, False)
            for i in range(1, NE // 2):
                body(i, i == NE // 2 - 1)
            dve.wait_ge(added, 16 * CT * NE)


def distances():
    d = np.arange(1 - S, S)
    mid, reach = SPAN // 2, NP
    a = np.abs(d).astype(np.float64)
    far = np.ceil(np.log(np.maximum(a, 1) / mid) / np.log((reach - 1) / mid) * (mid - 1) - 1e-6) + mid
    bucket = np.where(a <= mid, d, far * np.sign(d)).astype(np.int64)
    return np.clip(bucket + SPAN, 0, NP - 1)


def shape_constants(B):
    row = distances()
    low, high = row[0], row[-1]
    assert (row[:S - TLOW] == low).all() and (row[S - 2 + TLOW:] == high).all()
    pick = np.zeros((P, 2, TW), np.float32)
    for x in range(TW):
        d = x - TLOW
        for w, at in ((0, TW - 1 - x), (1, x)):
            pick[row[d + S - 1], w, at] += 1
            pick[low, w, at] -= 1
    ends = np.zeros((P, 2), np.float32)
    ends[low, 0] = ends[high, 1] = 1
    p = np.arange(P)
    own = np.zeros((P, HC, NH), np.float32)
    for c in range(HC):
        own[p, c, (c * P + p) // HD] = 1
    place = np.stack([np.broadcast_to(np.arange(B * QT, dtype=np.float32), (P, B * QT)),
                      np.broadcast_to(p[:, None].astype(np.float32), (P, B * QT))], 1)
    return {"pick": pick, "ends": ends, "own": own, "ident": np.eye(P, dtype=np.float32),
            "past": np.stack([p[None, :] <= p[:, None], p[None, :] >= p[:, None]], 1).astype(np.float32),
            "group": (p[:, None] * NE // P == p[None, :] * NE // P).astype(np.float32),
            "before": (p[:, None] < p[None, :]).astype(np.float32),
            "iota": np.ascontiguousarray(np.broadcast_to(p.astype(np.float32), (P, P))),
            "place": np.ascontiguousarray(place)}


def kernel(**inputs):
    import concourse.bacc as bacc
    from concourse.bass_utils import run_bass_kernel_spmd

    g = {k.replace("L0_", "").replace("attn_", "").replace("ffn_", ""): np.asarray(v) for k, v in inputs.items()}
    B = g["x"].shape[0]
    turn = np.ascontiguousarray
    arrays = {
        "xT": turn(g["x"].transpose(0, 3, 2, 1)),
        "tok_weight": turn(g["tok_weight"].T), "wsT": turn(g["tok_weighted_sum"].T),
        "bq_col": turn(g["bq"].reshape(HC, P).T), "bk_col": turn(g["bk"].reshape(HC, P).T),
        "b1T": turn(g["b1"].reshape(NE, FC, P).transpose(2, 0, 1)),
        **{k: turn(g[k]) for k in ("Wq", "Wk", "Wv", "Wo", "Wpk", "Wpq", "bv", "bo", "bpk", "bpq", "rel_emb",
                                   "ln_g", "ln_b", "router_w", "router_b", "w1", "w2", "b2")},
        **shape_constants(B),
    }
    nc = bacc.Bacc("TRN2", target_bir_lowering=False, num_devices=1)
    io = {k: nc.dram_tensor("in_" + k, a.shape, mybir.dt.from_np(a.dtype), kind="ExternalInput").ap()
          for k, a in arrays.items()}
    io["out"] = nc.dram_tensor("out", (B, S, H), F32, kind="ExternalOutput").ap()
    build(nc, io, B)
    result = run_bass_kernel_spmd(nc, [{"in_" + k: a for k, a in arrays.items()}], core_ids=[0])
    return result.results[0]["out"]
```
